# Optimizing a Trainium2 kernel written in Bass

```python
import numpy as np
import jax
import jax.numpy as jnp

def _softmax(x, axis=-1):
    return jax.nn.softmax(x, axis=axis)

def _gelu(x):
    return jax.nn.gelu(x, approximate=True)

def _silu(x):
    return jax.nn.silu(x)

def _sigmoid(x):
    return jax.nn.sigmoid(x)

def _layernorm(x, axis=-1, eps=1e-05):
    m = jnp.mean(x, axis=axis, keepdims=True)
    v = jnp.var(x, axis=axis, keepdims=True)
    return (x - m) / jnp.sqrt(v + eps)

def _scatter_add(tgt, idx, src, axis=0):
    return tgt.at[idx].add(src)

def _segment_sum(src, seg, n):
    return jax.ops.segment_sum(src, seg, n)
kernel_name = 'mk_flamingo_gated_d4_seqx_r8_23ee38'

def setup_inputs(seed: int=0):
    np.random.seed(seed)
    _w = jnp.asarray

    def _rec_inputs():
        import jax
        import jax.numpy as jnp
        _rk = jax.random.key(seed)
        x = 0.0003765 + 1 * jax.random.normal(jax.random.fold_in(_rk, 1), (128, 64, 128), jnp.float32)
        _lenS = 64 - jax.random.randint(jax.random.fold_in(_rk, 7), (128,), 0, max(1, 64 // 4) + 1, jnp.int32)
        _lenS2 = 64 - jax.random.randint(jax.random.fold_in(_rk, 8), (128,), 0, max(1, 64 // 4) + 1, jnp.int32)
        _ctx_1024P = jax.random.normal(jax.random.fold_in(_rk, 11), (128, 16, 128), jnp.float32)
        _ctx_1024c = jax.random.dirichlet(jax.random.fold_in(_rk, 511), 0.3 * jnp.ones((16,), jnp.float32), (128, 64))
        _ctx_1024t = jnp.einsum('bsk,bkd->bsd', _ctx_1024c, _ctx_1024P)
        _ctx_1024t = _ctx_1024t * jax.lax.rsqrt(jnp.mean(jnp.square(_ctx_1024t)) + 1e-12) * 0.953939
        ctx_1024 = -0.000292821 + 1.00034 * (_ctx_1024t + 0.3 * jax.random.normal(jax.random.fold_in(_rk, 611), (128, 64, 128), jnp.float32))
        _validS = jnp.arange(64)[None, :] < _lenS[:, None]
        _validS2 = jnp.arange(64)[None, :] < _lenS2[:, None]
        _causal = jnp.tril(jnp.ones((64, 64), dtype=bool))
        mask_Bx1x1xS2_if1 = jnp.where(jnp.ones((128, 1, 1, 64), dtype=bool), 1, 0).astype(jnp.int32)
        mask_Bx1x1xS2_fk0 = jnp.where(jnp.broadcast_to(_validS2[:, None, None, :], (128, 1, 1, 64)), 0.0, 1.0).astype(jnp.float32)
        _g = jax.random.normal(jax.random.fold_in(_rk, 9001), (2, 4), jnp.float32)
        _g = jnp.sign(_g) * jnp.maximum(jnp.abs(_g), 1.0) + (_g == 0) * 1.0
        g_xattn = _g[0]
        g_ffn = _g[1]
        return (x, ctx_1024, mask_Bx1x1xS2_if1, mask_Bx1x1xS2_fk0, g_xattn, g_ffn)
    x, ctx_1024, mask_Bx1x1xS2_if1, mask_Bx1x1xS2_fk0, g_xattn, g_ffn = _rec_inputs()

    def _L0_xattn_setup():
        import jax, jax.numpy as jnp
        import numpy as np
        EMBED_SIZE = 128
        HEADS = 16
        HEAD_DIM = EMBED_SIZE // HEADS
        key = jax.random.key(seed)
        ks = jax.random.split(key, 8)
        N, S = (2, 256)
        inv = 1.0 / np.sqrt(HEAD_DIM)
        return {'values': jax.random.normal(ks[0], (N, S, EMBED_SIZE), dtype=jnp.float32), 'keys': jax.random.normal(ks[1], (N, S, EMBED_SIZE), dtype=jnp.float32), 'query': jax.random.normal(ks[2], (N, S, EMBED_SIZE), dtype=jnp.float32), 'mask': jnp.ones((N, 1, 1, S), dtype=jnp.int32), 'Wv': jax.random.normal(ks[3], (HEAD_DIM, HEAD_DIM), dtype=jnp.float32) * inv, 'Wk': jax.random.normal(ks[4], (HEAD_DIM, HEAD_DIM), dtype=jnp.float32) * inv, 'Wq': jax.random.normal(ks[5], (HEAD_DIM, HEAD_DIM), dtype=jnp.float32) * inv, 'Wo': jax.random.normal(ks[6], (EMBED_SIZE, EMBED_SIZE), dtype=jnp.float32) / np.sqrt(EMBED_SIZE), 'bo': jnp.zeros((EMBED_SIZE,), dtype=jnp.float32)}
    _L0_xattn_all = _L0_xattn_setup()
    _L0_xattn_in = {k: v for k, v in _L0_xattn_all.items() if k in ('Wv', 'Wk', 'Wq', 'Wo', 'bo')}
    del _L0_xattn_all

    def _L0_ffn_setup():
        import math
        import jax, jax.numpy as jnp
        import numpy as np
        D_MODEL = 128
        D_FF = 512
        E = 8
        K = 2
        CAP_FACTOR = 1.25
        CLAMP = 10000.0
        LN_EPS = 1e-05
        B, S = (2, 256)
        key = jax.random.key(seed)
        ks = jax.random.split(key, 6)
        b12 = math.sqrt(6.0 / (D_MODEL + 2 * D_FF))
        b3 = math.sqrt(6.0 / (D_FF + D_MODEL))
        br = 0.02 * math.sqrt(3.0)
        return {'x': jax.random.normal(ks[0], (B, S, D_MODEL), dtype=jnp.float32), 'ln_gamma': jnp.ones((D_MODEL,), jnp.float32), 'ln_beta': jnp.zeros((D_MODEL,), jnp.float32), 'router_w': jax.random.uniform(ks[1], (E, D_MODEL), jnp.float32, -br, br), 'w12': jax.random.uniform(ks[2], (E, 2 * D_FF, D_MODEL), jnp.float32, -b12, b12), 'w3': jax.random.uniform(ks[3], (E, D_MODEL, D_FF), jnp.float32, -b3, b3)}
    _L0_ffn_all = _L0_ffn_setup()
    _L0_ffn_in = {k: v for k, v in _L0_ffn_all.items() if k in ('ln_gamma', 'ln_beta', 'router_w', 'w12', 'w3')}
    del _L0_ffn_all

    def _L1_xattn_setup():
        import jax, jax.numpy as jnp
        import numpy as np
        key = jax.random.key(seed)
        k1, k2, k3 = jax.random.split(key, 3)
        B, N, D = (4, 512, 128)
        return {'q': jax.random.normal(k1, (B, N, D), dtype=jnp.float32), 'k': jax.random.normal(k2, (B, N, D), dtype=jnp.float32), 'v': jax.random.normal(k3, (B, N, D), dtype=jnp.float32), 'ctx': 128}
    _L1_xattn_all = _L1_xattn_setup()
    _L1_xattn_in = {k: v for k, v in _L1_xattn_all.items() if k in ()}
    del _L1_xattn_all

    def _L1_ffn_setup():
        import jax, jax.numpy as jnp
        import numpy as np
        DIM = 128
        NUM_EXPERTS = 8
        HIDDEN = 512
        CAP_FACTOR = 2.0
        B, S = (4, 256)
        key = jax.random.key(seed)
        ks = jax.random.split(key, 6)
        scale_r = 1.0 / np.sqrt(DIM)
        scale_1 = 1.0 / np.sqrt(DIM)
        scale_2 = 1.0 / np.sqrt(HIDDEN)
        return {'x': jax.random.normal(ks[0], (B, S, DIM), dtype=jnp.float32), 'router_w': jax.random.uniform(ks[1], (NUM_EXPERTS, DIM), jnp.float32, -scale_r, scale_r), 'w1': jax.random.uniform(ks[2], (NUM_EXPERTS, DIM, HIDDEN), jnp.float32, -scale_1, scale_1), 'b1': jax.random.uniform(ks[3], (NUM_EXPERTS, HIDDEN), jnp.float32, -scale_1, scale_1), 'w2': jax.random.uniform(ks[4], (NUM_EXPERTS, HIDDEN, DIM), jnp.float32, -scale_2, scale_2), 'b2': jax.random.uniform(ks[5], (NUM_EXPERTS, DIM), jnp.float32, -scale_2, scale_2)}
    _L1_ffn_all = _L1_ffn_setup()
    _L1_ffn_in = {k: v for k, v in _L1_ffn_all.items() if k in ('router_w', 'w1', 'b1', 'w2', 'b2')}
    del _L1_ffn_all

    def _L2_xattn_setup():
        import jax, jax.numpy as jnp
        import numpy as np
        B, C_LEN, Q_LEN, D = (8, 256, 64, 128)
        key = jax.random.key(seed)
        ks = jax.random.split(key, 10)
        scale = 1.0 / np.sqrt(D)
        return {'c': jax.random.normal(ks[0], (B, C_LEN, D), dtype=jnp.float32), 'q': jax.random.normal(ks[1], (B, Q_LEN, D), dtype=jnp.float32), 'w_cq': jax.random.normal(ks[2], (D,), dtype=jnp.float32) * scale, 'b_cq': jax.random.normal(ks[3], (), dtype=jnp.float32) * scale, 'w_c': jax.random.normal(ks[4], (D,), dtype=jnp.float32) * scale, 'b_c': jax.random.normal(ks[5], (), dtype=jnp.float32) * scale, 'w_q': jax.random.normal(ks[6], (D,), dtype=jnp.float32) * scale, 'b_q': jax.random.normal(ks[7], (), dtype=jnp.float32) * scale, 'W_l': jax.random.normal(ks[8], (D, 4 * D), dtype=jnp.float32) * (1.0 / np.sqrt(4 * D)), 'b_l': jax.random.normal(ks[9], (D,), dtype=jnp.float32) * (1.0 / np.sqrt(4 * D))}
    _L2_xattn_all = _L2_xattn_setup()
    _L2_xattn_in = {k: v for k, v in _L2_xattn_all.items() if k in ('w_cq', 'b_cq', 'w_c', 'b_c', 'w_q', 'b_q', 'W_l', 'b_l')}
    del _L2_xattn_all

    def _L2_ffn_setup():
        import jax, jax.numpy as jnp
        import numpy as np
        B, T, C, H, E = (1, 32, 128, 256, 8)
        STD = 0.02
        key = jax.random.key(seed)
        ks = jax.random.split(key, 8)
        f32 = jnp.float32
        return {'x': jax.random.normal(ks[0], (B, T, C), f32), 'up': jax.random.normal(ks[1], (E, H, C), f32) * STD, 'gate': jax.random.normal(ks[2], (E, H, C), f32) * STD, 'down': jax.random.normal(ks[3], (E, C, H), f32) * STD, 'router': jax.random.normal(ks[4], (E, C), f32) * STD, 'w_up_s': jax.random.normal(ks[5], (H, C), f32) * STD, 'w_gate_s': jax.random.normal(ks[6], (H, C), f32) * STD, 'w_down_s': jax.random.normal(ks[7], (C, H), f32) * STD}
    _L2_ffn_all = _L2_ffn_setup()
    _L2_ffn_in = {k: v for k, v in _L2_ffn_all.items() if k in ('up', 'gate', 'down', 'router', 'w_up_s', 'w_gate_s', 'w_down_s')}
    del _L2_ffn_all

    def _L3_xattn_setup():
        import jax, jax.numpy as jnp
        import numpy as np
        EMBED = 128
        HEADS = 16
        HEAD_DIM = EMBED // HEADS

        def _split_heads(x, B):
            return x.reshape(B, -1, HEADS, HEAD_DIM).transpose(0, 2, 1, 3)
        key = jax.random.key(seed)
        ks = jax.random.split(key, 13)
        B, S = (2, 256)
        inp = {'v': jax.random.normal(ks[0], (B, S, EMBED), jnp.float32), 'k': jax.random.normal(ks[1], (B, S, EMBED), jnp.float32), 'q': jax.random.normal(ks[2], (B, S, EMBED), jnp.float32), 'mask': jax.random.randint(ks[3], (B, 1, 1, S), 0, 2).astype(jnp.float32)}
        scale = 1.0 / np.sqrt(EMBED)
        inp['wq'] = jax.random.normal(ks[4], (EMBED, EMBED), jnp.float32) * scale
        inp['bq'] = jnp.zeros((EMBED,), jnp.float32)
        inp['wk'] = jax.random.normal(ks[5], (EMBED, EMBED), jnp.float32) * scale
        inp['bk'] = jnp.zeros((EMBED,), jnp.float32)
        inp['wv'] = jax.random.normal(ks[6], (EMBED, EMBED), jnp.float32) * scale
        inp['bv'] = jnp.zeros((EMBED,), jnp.float32)
        inp['wo'] = jax.random.normal(ks[7], (EMBED, EMBED), jnp.float32) * scale
        inp['bo'] = jnp.zeros((EMBED,), jnp.float32)
        return inp
    _L3_xattn_all = _L3_xattn_setup()
    _L3_xattn_in = {k: v for k, v in _L3_xattn_all.items() if k in ('wq', 'bq', 'wk', 'bk', 'wv', 'bv', 'wo', 'bo')}
    del _L3_xattn_all

    def _L3_ffn_setup():
        import jax, jax.numpy as jnp
        import numpy as np
        TOPK = 2
        CAPACITY_FACTOR = 1.0
        EPS = 1e-06
        B, S, D = (4, 512, 128)
        E = 8
        SUB_H = 256 // E
        key = jax.random.key(seed)
        ks = jax.random.split(key, 7)
        x = jax.random.normal(ks[0], (B, S, D), dtype=jnp.float32)
        w_gate_w = jax.random.normal(ks[1], (D, E), dtype=jnp.float32) * 0.02
        w_gate_b = jnp.zeros((E,), jnp.float32)
        W1 = jax.random.normal(ks[2], (E, D, SUB_H), dtype=jnp.float32) * 0.02
        b1 = jnp.zeros((E, SUB_H), jnp.float32)
        W2 = jax.random.normal(ks[3], (E, SUB_H, D), dtype=jnp.float32) * 0.02
        b2 = jnp.zeros((E, D), jnp.float32)
        return {'x': x, 'w_gate_w': w_gate_w, 'w_gate_b': w_gate_b, 'W1': W1, 'b1': b1, 'W2': W2, 'b2': b2}
    _L3_ffn_all = _L3_ffn_setup()
    _L3_ffn_in = {k: v for k, v in _L3_ffn_all.items() if k in ('w_gate_w', 'w_gate_b', 'W1', 'b1', 'W2', 'b2')}
    del _L3_ffn_all
    return {'x': x, 'ctx_1024': ctx_1024, 'mask_Bx1x1xS2_if1': mask_Bx1x1xS2_if1, 'mask_Bx1x1xS2_fk0': mask_Bx1x1xS2_fk0, 'g_xattn': g_xattn, 'g_ffn': g_ffn, 'L0_xattn_Wv': _L0_xattn_in['Wv'], 'L0_xattn_Wk': _L0_xattn_in['Wk'], 'L0_xattn_Wq': _L0_xattn_in['Wq'], 'L0_xattn_Wo': _L0_xattn_in['Wo'], 'L0_xattn_bo': _L0_xattn_in['bo'], 'L0_ffn_ln_gamma': _L0_ffn_in['ln_gamma'], 'L0_ffn_ln_beta': _L0_ffn_in['ln_beta'], 'L0_ffn_router_w': _L0_ffn_in['router_w'], 'L0_ffn_w12': _L0_ffn_in['w12'], 'L0_ffn_w3': _L0_ffn_in['w3'], 'L1_ffn_router_w': _L1_ffn_in['router_w'], 'L1_ffn_w1': _L1_ffn_in['w1'], 'L1_ffn_b1': _L1_ffn_in['b1'], 'L1_ffn_w2': _L1_ffn_in['w2'], 'L1_ffn_b2': _L1_ffn_in['b2'], 'L2_xattn_w_cq': _L2_xattn_in['w_cq'], 'L2_xattn_b_cq': _L2_xattn_in['b_cq'], 'L2_xattn_w_c': _L2_xattn_in['w_c'], 'L2_xattn_b_c': _L2_xattn_in['b_c'], 'L2_xattn_w_q': _L2_xattn_in['w_q'], 'L2_xattn_b_q': _L2_xattn_in['b_q'], 'L2_xattn_W_l': _L2_xattn_in['W_l'], 'L2_xattn_b_l': _L2_xattn_in['b_l'], 'L2_ffn_up': _L2_ffn_in['up'], 'L2_ffn_gate': _L2_ffn_in['gate'], 'L2_ffn_down': _L2_ffn_in['down'], 'L2_ffn_router': _L2_ffn_in['router'], 'L2_ffn_w_up_s': _L2_ffn_in['w_up_s'], 'L2_ffn_w_gate_s': _L2_ffn_in['w_gate_s'], 'L2_ffn_w_down_s': _L2_ffn_in['w_down_s'], 'L3_xattn_wq': _L3_xattn_in['wq'], 'L3_xattn_bq': _L3_xattn_in['bq'], 'L3_xattn_wk': _L3_xattn_in['wk'], 'L3_xattn_bk': _L3_xattn_in['bk'], 'L3_xattn_wv': _L3_xattn_in['wv'], 'L3_xattn_bv': _L3_xattn_in['bv'], 'L3_xattn_wo': _L3_xattn_in['wo'], 'L3_xattn_bo': _L3_xattn_in['bo'], 'L3_ffn_w_gate_w': _L3_ffn_in['w_gate_w'], 'L3_ffn_w_gate_b': _L3_ffn_in['w_gate_b'], 'L3_ffn_W1': _L3_ffn_in['W1'], 'L3_ffn_b1': _L3_ffn_in['b1'], 'L3_ffn_W2': _L3_ffn_in['W2'], 'L3_ffn_b2': _L3_ffn_in['b2']}

def reference(x, ctx_1024, mask_Bx1x1xS2_if1, mask_Bx1x1xS2_fk0, g_xattn, g_ffn, L0_xattn_Wv, L0_xattn_Wk, L0_xattn_Wq, L0_xattn_Wo, L0_xattn_bo, L0_ffn_ln_gamma, L0_ffn_ln_beta, L0_ffn_router_w, L0_ffn_w12, L0_ffn_w3, L1_ffn_router_w, L1_ffn_w1, L1_ffn_b1, L1_ffn_w2, L1_ffn_b2, L2_xattn_w_cq, L2_xattn_b_cq, L2_xattn_w_c, L2_xattn_b_c, L2_xattn_w_q, L2_xattn_b_q, L2_xattn_W_l, L2_xattn_b_l, L2_ffn_up, L2_ffn_gate, L2_ffn_down, L2_ffn_router, L2_ffn_w_up_s, L2_ffn_w_gate_s, L2_ffn_w_down_s, L3_xattn_wq, L3_xattn_bq, L3_xattn_wk, L3_xattn_bk, L3_xattn_wv, L3_xattn_bv, L3_xattn_wo, L3_xattn_bo, L3_ffn_w_gate_w, L3_ffn_w_gate_b, L3_ffn_W1, L3_ffn_b1, L3_ffn_W2, L3_ffn_b2):
    import jax
    import jax.numpy as jnp

    def _L0_xattn_ref(values, keys, query, mask, Wv, Wk, Wq, Wo, bo):
        import jax, jax.numpy as jnp
        import numpy as np
        EMBED_SIZE = 128
        HEADS = 16
        HEAD_DIM = EMBED_SIZE // HEADS
        N, S, E = query.shape
        H, D = (HEADS, HEAD_DIM)
        v = values.reshape(N, S, H, D)
        k = keys.reshape(N, S, H, D)
        q = query.reshape(N, S, H, D)
        v = jnp.einsum('nshd,ed->nshe', v, Wv)
        k = jnp.einsum('nshd,ed->nshe', k, Wk)
        q = jnp.einsum('nshd,ed->nshe', q, Wq)
        energy = jnp.einsum('nqhd,nkhd->nhqk', q, k)
        energy = jnp.where(mask == 0, jnp.asarray(-1e+20, energy.dtype), energy)
        attn = jax.nn.softmax(energy / jnp.sqrt(jnp.asarray(E, energy.dtype)), axis=-1)
        out = jnp.einsum('nhql,nlhd->nqhd', attn, v).reshape(N, S, H * D)
        return out @ Wo.T + bo

    def _L0_ffn_ref(x, ln_gamma, ln_beta, router_w, w12, w3):
        import math
        import jax, jax.numpy as jnp
        import numpy as np
        D_MODEL = 128
        D_FF = 512
        E = 8
        K = 2
        CAP_FACTOR = 1.25
        CLAMP = 10000.0
        LN_EPS = 1e-05
        B, S = (2, 256)
        Bq, Sq, D = x.shape
        T = Bq * Sq
        mu = jnp.mean(x, axis=-1, keepdims=True)
        var = jnp.mean(jnp.square(x - mu), axis=-1, keepdims=True)
        xn = (x - mu) * jax.lax.rsqrt(var + LN_EPS) * ln_gamma + ln_beta
        xf = xn.reshape(T, D)
        logits = jnp.clip(xf @ router_w.T, -CLAMP, CLAMP)
        top_v, top_i = jax.lax.top_k(logits, K)
        m = jnp.max(top_v, axis=-1, keepdims=True)
        ev = jnp.exp(top_v - m)
        top_p = ev / (jnp.sum(ev, axis=-1, keepdims=True) + 1e-12)
        Stot = T * K
        experts = top_i.reshape(-1)
        weights = top_p.reshape(-1)
        tokens = jnp.repeat(jnp.arange(T), K)
        oh = (experts[:, None] == jnp.arange(E)[None, :]).astype(jnp.int32)
        pos = jnp.take_along_axis(jnp.cumsum(oh, axis=0) - 1, experts[:, None], axis=1)[:, 0]
        C = max(1, math.ceil(T * K * CAP_FACTOR / E))
        kept = pos < C
        slot = jnp.where(kept, experts * C + pos, E * C)
        buf = jnp.zeros((E * C + 1, D), x.dtype).at[slot].set(xf[tokens])
        xb = buf[:E * C].reshape(E, C, D)
        gu = jnp.einsum('ecd,efd->ecf', xb, w12)
        g, u = jnp.split(gu, 2, axis=-1)
        h = jax.nn.silu(g) * u
        yb = jnp.einsum('ecf,edf->ecd', h, w3).reshape(E * C, D)
        ys = yb[jnp.minimum(slot, E * C - 1)] * (weights * kept.astype(weights.dtype))[:, None]
        out = jnp.zeros((T, D), x.dtype).at[tokens].add(ys)
        return out.reshape(Bq, Sq, D)

    def _L1_xattn_ref(q, k, v, ctx):
        import jax, jax.numpy as jnp
        import numpy as np
        N = q.shape[1]
        g = jax.nn.relu(k) * v
        c = jnp.cumsum(g, axis=1)
        i = jnp.arange(N)
        hi = jnp.minimum(i + ctx, N - 1)
        lo = i - ctx - 1
        upper = c[:, hi, :]
        lower = jnp.where((lo >= 0)[None, :, None], c[:, jnp.clip(lo, 0, N - 1), :], jnp.zeros((), dtype=c.dtype))
        attn = upper - lower
        return jax.nn.relu(q) * attn

    def _L1_ffn_ref(x, router_w, w1, b1, w2, b2):
        import jax, jax.numpy as jnp
        import numpy as np
        DIM = 128
        NUM_EXPERTS = 8
        HIDDEN = 512
        CAP_FACTOR = 2.0
        B, S = (4, 256)
        Bz, Sz, Dz = x.shape
        E = router_w.shape[0]
        capacity = max(1, int(Sz * CAP_FACTOR / E) + 1)
        scores = jax.nn.softmax(jnp.einsum('bsd,ed->bse', x, router_w), axis=-1)
        scores_t = jnp.swapaxes(scores, 1, 2)
        gate_vals, sel_idx = jax.lax.top_k(scores_t, capacity)
        b_idx = jnp.arange(Bz)[:, None, None]
        tokens = x[b_idx, sel_idx]
        h = jnp.einsum('becd,edh->bech', tokens, w1) + b1[None, :, None, :]
        h = jax.nn.gelu(h, approximate=False)
        y = jnp.einsum('bech,ehd->becd', h, w2) + b2[None, :, None, :]
        gated = y * gate_vals[..., None]
        out = jnp.zeros_like(x).at[b_idx, sel_idx].add(gated)
        return out

    def _L2_xattn_ref(c, q, w_cq, b_cq, w_c, b_c, w_q, b_q, W_l, b_l):
        import jax, jax.numpy as jnp
        import numpy as np
        B, C_LEN, Q_LEN, D = (8, 256, 64, 128)
        cq = jnp.einsum('bcd,bqd,d->bcq', c, q, w_cq) + b_cq
        s = (c @ w_c + b_c)[:, :, None] + (q @ w_q + b_q)[:, None, :] + cq
        a = jax.nn.softmax(s, axis=2)
        c2q_att = jnp.einsum('bcq,bqd->bcd', a, q)
        b_att = jax.nn.softmax(jnp.max(s, axis=2), axis=1)
        q2c_att = jnp.einsum('bc,bcd->bd', b_att, c)[:, None, :]
        x = jnp.concatenate([c, c2q_att, c * c2q_att, c * q2c_att], axis=-1)
        z = x @ W_l.T + b_l
        return z

    def _L2_ffn_ref(x, up, gate, down, router, w_up_s, w_gate_s, w_down_s):
        import jax, jax.numpy as jnp
        import numpy as np
        B, T, C, H, E = (1, 32, 128, 256, 8)
        STD = 0.02
        b, t, c = x.shape
        x_ = x.reshape(b * t, c)
        logits = x_ @ router.T
        idx = jnp.argmax(logits, axis=-1)
        onehot = jax.nn.one_hot(idx, router.shape[0], dtype=x.dtype)
        u = jnp.einsum('bc,ehc->ebh', x_, up)
        g = jnp.einsum('bc,ehc->ebh', x_, gate)
        h = jax.nn.silu(g) * u
        ye = jnp.einsum('ebh,ech->ebc', h, down)
        y = jnp.einsum('ebc,be->bc', ye, onehot)
        ys = jax.nn.silu(x_ @ w_gate_s.T) * (x_ @ w_up_s.T) @ w_down_s.T
        return (y + ys).reshape(b, t, c)

    def _L3_xattn_ref(v, k, q, mask, wq, bq, wk, bk, wv, bv, wo, bo):
        import jax, jax.numpy as jnp
        import numpy as np
        EMBED = 128
        HEADS = 16
        HEAD_DIM = EMBED // HEADS

        def _split_heads(x, B):
            return x.reshape(B, -1, HEADS, HEAD_DIM).transpose(0, 2, 1, 3)
        B = q.shape[0]
        qh = _split_heads(q @ wq + bq, B)
        kh = _split_heads(k @ wk + bk, B)
        vh = _split_heads(v @ wv + bv, B)
        logits = jnp.einsum('bhqd,bhkd->bhqk', qh, kh) / jnp.sqrt(jnp.float32(HEAD_DIM))
        logits = logits + mask * -1000000000.0
        attn = jax.nn.softmax(logits, axis=-1)
        out = jnp.einsum('bhqk,bhkd->bhqd', attn, vh)
        out = out.transpose(0, 2, 1, 3).reshape(B, -1, EMBED)
        return out @ wo + bo

    def _L3_ffn_ref(x, w_gate_w, w_gate_b, W1, b1, W2, b2):
        import jax, jax.numpy as jnp
        import numpy as np
        TOPK = 2
        CAPACITY_FACTOR = 1.0
        EPS = 1e-06
        B, S, D = (4, 512, 128)
        E = 8
        SUB_H = 256 // E
        Bx, Sx, Dx = x.shape
        Ex = w_gate_b.shape[0]
        K = Sx // 2
        capacity = int(CAPACITY_FACTOR * Bx)
        gate_scores = jax.nn.softmax(x @ w_gate_w + w_gate_b, axis=-1)
        _, top_idx = jax.lax.top_k(gate_scores, TOPK)
        mask = jax.nn.one_hot(top_idx, Ex, dtype=gate_scores.dtype).sum(axis=-2)
        masked = gate_scores * mask
        denom = masked.sum(axis=0, keepdims=True) + EPS
        route = masked / denom * capacity
        route_eb = jnp.transpose(route, (2, 0, 1))
        _, seq_ids = jax.lax.top_k(route_eb, K)
        seq_ids = jnp.sort(seq_ids, axis=-1)
        xg = jax.vmap(lambda idx: jnp.take_along_axis(x, idx[..., None], axis=1))(seq_ids)
        h = jnp.einsum('ebkd,edh->ebkh', xg, W1) + b1[:, None, None, :]
        h = jax.nn.gelu(h, approximate=False)
        o = jnp.einsum('ebkh,ehd->ebkd', h, W2) + b2[:, None, None, :]
        flat_ids = (jnp.arange(Bx)[None, :, None] * Sx + seq_ids).reshape(-1)
        outs = jnp.zeros((Bx * Sx, Dx), x.dtype).at[flat_ids].add(o.reshape(-1, Dx))
        return outs.reshape(Bx, Sx, Dx)
    x = x + jnp.tanh(g_xattn[0]) * _L0_xattn_ref(ctx_1024, ctx_1024, _layernorm(x, axis=-1), mask_Bx1x1xS2_if1, L0_xattn_Wv, L0_xattn_Wk, L0_xattn_Wq, L0_xattn_Wo, L0_xattn_bo)
    x = x + jnp.tanh(g_ffn[0]) * _L0_ffn_ref(_layernorm(x, axis=-1), L0_ffn_ln_gamma, L0_ffn_ln_beta, L0_ffn_router_w, L0_ffn_w12, L0_ffn_w3)
    x = x + jnp.tanh(g_xattn[1]) * _L1_xattn_ref(_layernorm(x, axis=-1), ctx_1024, ctx_1024, 128)
    x = x + jnp.tanh(g_ffn[1]) * _L1_ffn_ref(_layernorm(x, axis=-1), L1_ffn_router_w, L1_ffn_w1, L1_ffn_b1, L1_ffn_w2, L1_ffn_b2)
    x = x + jnp.tanh(g_xattn[2]) * _L2_xattn_ref(_layernorm(x, axis=-1), ctx_1024, L2_xattn_w_cq, L2_xattn_b_cq, L2_xattn_w_c, L2_xattn_b_c, L2_xattn_w_q, L2_xattn_b_q, L2_xattn_W_l, L2_xattn_b_l)
    x = x + jnp.tanh(g_ffn[2]) * _L2_ffn_ref(_layernorm(x, axis=-1), L2_ffn_up, L2_ffn_gate, L2_ffn_down, L2_ffn_router, L2_ffn_w_up_s, L2_ffn_w_gate_s, L2_ffn_w_down_s)
    x = x + jnp.tanh(g_xattn[3]) * _L3_xattn_ref(ctx_1024, ctx_1024, _layernorm(x, axis=-1), mask_Bx1x1xS2_fk0, L3_xattn_wq, L3_xattn_bq, L3_xattn_wk, L3_xattn_bk, L3_xattn_wv, L3_xattn_bv, L3_xattn_wo, L3_xattn_bo)
    x = x + jnp.tanh(g_ffn[3]) * _L3_ffn_ref(_layernorm(x, axis=-1), L3_ffn_w_gate_w, L3_ffn_w_gate_b, L3_ffn_W1, L3_ffn_b1, L3_ffn_W2, L3_ffn_b2)
    return x

_drawn_inputs = setup_inputs


def setup_inputs(seed=0):
    import zlib

    import numpy as np

    out = dict(_drawn_inputs(seed))
    spreads = {'L0_xattn_bo': (0.0, 0.1),
     'L0_ffn_ln_gamma': (1.0, 0.2),
     'L0_ffn_ln_beta': (0.0, 0.278),
     'L3_xattn_bq': (0.0, 0.8),
     'L3_xattn_bk': (0.0, 2.0),
     'L3_xattn_bv': (0.0, 0.8),
     'L3_xattn_bo': (0.0, 2.0),
     'L3_ffn_w_gate_b': (0.0, 0.8),
     'L3_ffn_b1': (0.0, 2.0),
     'L3_ffn_b2': (0.0, 0.8)}
    factors = {'g_ffn': 8.0,
     'L1_ffn_router_w': 8.0,
     'L1_ffn_w1': 8.0,
     'L1_ffn_b1': 8.0,
     'L1_ffn_w2': 8.0,
     'L1_ffn_b2': 8.0,
     'L2_xattn_w_cq': 5.031,
     'L2_xattn_w_c': 8.0,
     'L2_xattn_w_q': 7.871,
     'L2_xattn_b_l': 8.0,
     'L2_ffn_up': 8.0,
     'L2_ffn_gate': 8.0,
     'L2_ffn_down': 8.0,
     'L2_ffn_router': 8.0,
     'L2_ffn_w_up_s': 8.0,
     'L2_ffn_w_gate_s': 8.0,
     'L2_ffn_w_down_s': 8.0,
     'L3_xattn_wq': 8.0,
     'L3_xattn_wk': 8.0,
     'L3_xattn_wv': 3.851,
     'L3_xattn_wo': 3.802,
     'L3_ffn_w_gate_w': 8.0,
     'L3_ffn_W1': 8.0,
     'L3_ffn_W2': 8.0}
    for name, (base, spread) in spreads.items():
        noise = np.random.default_rng([zlib.crc32(name.encode()), seed]).standard_normal(out[name].shape)
        drawn = base * np.exp(spread * noise) if base else spread * noise
        out[name] = jnp.asarray(drawn.astype(out[name].dtype))
    for name, factor in factors.items():
        out[name] = (out[name] * factor).astype(out[name].dtype)
    return out
```

```python
from contextlib import ExitStack

import concourse.bass as bass
from concourse import mybir

F32 = mybir.dt.float32
BF16 = mybir.dt.bfloat16
I32 = mybir.dt.int32
U32 = mybir.dt.uint32
ALU = mybir.AluOpType
ACT = mybir.ActivationFunctionType
AX = mybir.AxisListType

P = 128
B, S = 128, 64
T = B * S
NT = T // P
G = 512
NG = T // G
TG = G // P
BG = G // S
E = 8
H, HD = 16, 8
EPS = 1e-5



class Chip:

    def __init__(self, nc, ctx):
        self.nc, self.ctx = nc, ctx
        self.sems = []

    def sb(self, name, shape, dt=F32):
        return self.ctx.enter_context(self.nc.sbuf_tensor(name, shape, dt))

    def sem(self, name):
        handle = self.nc.alloc_semaphore(name=name)
        self.sems.append(handle)
        return handle

    def recycle_semaphores(self):
        self.nc.clear_and_free_semaphores(self.sems)
        self.sems = []
        self.nc.all_engine_barrier()


def cols(t, at, n=G):
    return t[:, bass.ds(at, n)]


def over(ap, shape):
    return ap.broadcast_to(shape)


def setup(c, A):
    nc = c.nc
    c.x = c.sb("x", [P, T])
    c.xn = c.sb("xn", [P, T])
    c.wa = c.sb("weights_a", [P, 12288])
    c.wb = c.sb("weights_b", [P, 8192])
    c.work = c.sb("work", [P, 10240])
    c.avg = c.sb("avg", [P, P])
    c.ident = c.sb("ident", [P, P])
    c.same_pos = c.sb("same_pos", [P, P])
    c.before = c.sb("before", [P, P], BF16)
    c.ones = c.sb("ones", [P, P], BF16)
    c.lower = c.sb("lower", [P, E, E])
    c.half = c.sb("half", [P, 2])
    c.half16 = c.sb("half16", [P, 2, HD])
    c.quad = c.sb("quad", [P, 4])
    c.eps = c.sb("eps", [P, 1])
    c.gate_in = c.sb("gate_in", [P, 8])
    c.tanh_g = c.sb("tanh_g", [P, 8])
    c.gates = c.sb("gates", [P, NT, E])
    c.cols16 = c.sb("cols16", [P, 64])
    c.banks = c.ctx.enter_context(nc.psum_tensor("banks", [P, 8, G], F32))
    x_in = c.sem("x_in")
    small_in = c.sem("small_in")
    filled = c.sem("filled")
    tanhed = c.sem("tanhed")
    with nc.Block() as block:
        @block.sync
        def _(sp):
            for k in range(4):
                sp.dma_start(c.x[:, k * 2048:(k + 1) * 2048], A["xT"][:, k * 2048:(k + 1) * 2048]).then_inc(x_in, 16)
            sp.wait_ge(x_in, 64)

        @block.scalar
        def _(act):
            act.dma_start(c.gate_in[:, 0:4], A["g_xattn"].partition_broadcast(P)).then_inc(small_in, 16)
            act.dma_start(c.gate_in[:, 4:8], A["g_ffn"].partition_broadcast(P)).then_inc(small_in, 16)
            act.wait_ge(small_in, 32)
            nc.scalar.activation(c.tanh_g[:, :], c.gate_in[:, :], ACT.Tanh).then_inc(tanhed, 1)

        @block.gpsimd
        def _(pool):
            done = [0]

            def put(ins):
                done[0] += 1
                ins.then_inc(filled, 1)
                pool.wait_ge(filled, done[0])

            def keep(t, pattern, base, mult, cmp, fill=0.0):
                put(nc.gpsimd.affine_select(out=t, in_=t, compare_op=cmp, fill=fill, base=base,
                                            pattern=pattern, channel_multiplier=mult))

            put(nc.gpsimd.memset(c.avg[:, :], 1.0 / P))
            put(nc.gpsimd.memset(c.eps[:, :], EPS))
            put(nc.gpsimd.memset(c.ones[:, :], 1.0))
            put(nc.gpsimd.memset(c.ident[:, :], 0.0))
            keep(c.ident[:, :], [[-1, P]], 0, 1, ALU.not_equal, 1.0)
            put(nc.gpsimd.memset(c.same_pos[:, :], 0.0))
            for off in (-S, 0, S):
                keep(c.same_pos[:, :], [[-1, P]], off, 1, ALU.not_equal, 1.0)
            put(nc.gpsimd.memset(c.before[:, :], 1.0))
            keep(c.before[:, :], [[1, P]], -1, -1, ALU.is_ge)
            put(nc.gpsimd.memset(c.lower[:, :, :], 1.0))
            keep(c.lower[:, :, :], [[1, E], [-1, E]], -1, 0, ALU.is_ge)
            put(nc.gpsimd.memset(c.half[:, :], 1.0))
            keep(c.half[:, :], [[-S, 2]], 0, 1, ALU.is_ge)
            keep(c.half[:, :], [[S, 2]], S - 1, -1, ALU.is_ge)
            put(nc.gpsimd.memset(c.half16[:, :, :], 1.0))
            keep(c.half16[:, :, :], [[-S, 2], [0, HD]], 0, 1, ALU.is_ge)
            keep(c.half16[:, :, :], [[S, 2], [0, HD]], S - 1, -1, ALU.is_ge)
            put(nc.gpsimd.memset(c.quad[:, :], 0.0))
            for q in range(4):
                rows = c.quad[32 * q:32 * q + 32, :]
                put(nc.gpsimd.memset(rows, 1.0))
                keep(rows, [[-HD, 4]], 0, 1, ALU.is_ge)
                keep(rows, [[HD, 4]], HD - 1, -1, ALU.is_ge)


def layer_norm(c, tag, src, dst, affine=None):
    nc = c.nc
    U = 4
    xc = c.work[:, 0:U * G].rearrange("p (u n) -> p u n", u=U)
    sq = c.work[:, U * G:2 * U * G].rearrange("p (u n) -> p u n", u=U)
    rs = c.work[:, 2 * U * G:3 * U * G].rearrange("p (u n) -> p u n", u=U)
    mean, var = c.banks[:, 0:U, :], c.banks[:, U:2 * U, :]
    mean_done = c.sem(tag + "_mean_done")
    xc_done = c.sem(tag + "_xc_done")
    sq_done = c.sem(tag + "_sq_done")
    var_done = c.sem(tag + "_var_done")
    ln_done = c.sem(tag + "_ln_done")
    rs_done = c.sem(tag + "_rs_done")
    scaled_done = c.sem(tag + "_scaled_done")
    out_done = c.sem(tag + "_out_done")
    with nc.Block() as block:
        @block.tensor
        def _(pe):
            with pe.Fori(0, NG // U) as i:
                for u in range(U):
                    pe.wait_ge(xc_done, i * U + (u + 1))
                    nc.tensor.matmul(mean[:, u, :], c.avg[:, :], cols(src, i * (U * G) + u * G),
                                     start=True, stop=True).then_inc(mean_done, 1)
                for u in range(U):
                    pe.wait_ge(sq_done, i * U + (u + 1))
                    pe.wait_ge(ln_done, i * U + (u + 1))
                    nc.tensor.matmul(var[:, u, :], c.avg[:, :], sq[:, u, :],
                                     start=True, stop=True).then_inc(var_done, 1)

        @block.vector
        def _(dve):
            dve.sem_inc(xc_done, U)
            dve.sem_inc(out_done, U)
            with dve.Fori(0, NG // U) as i:
                for u in range(U):
                    dve.wait_ge(mean_done, i * U + (u + 1))
                    dve.wait_ge(out_done, i * U + (u + 1))
                    nc.vector.tensor_tensor(xc[:, u, :], cols(src, i * (U * G) + u * G), mean[:, u, :],
                                            ALU.subtract).then_inc(xc_done, 1)
                for u in range(U):
                    dve.wait_ge(rs_done, i * U + (u + 1))
                    at = cols(dst, i * (U * G) + u * G)
                    if affine is None:
                        nc.vector.tensor_tensor(at, xc[:, u, :], rs[:, u, :], ALU.mult).then_inc(out_done, 1)
                    else:
                        nc.vector.scalar_tensor_tensor(out=xc[:, u, :], in0=xc[:, u, :], scalar=affine[0],
                                                       in1=rs[:, u, :], op0=ALU.mult,
                                                       op1=ALU.mult).then_inc(scaled_done, 1)
                if affine is not None:
                    for u in range(U):
                        dve.wait_ge(scaled_done, i * U + (u + 1))
                        nc.vector.tensor_scalar(cols(dst, i * (U * G) + u * G), xc[:, u, :], affine[1], None,
                                                ALU.add).then_inc(out_done, 1)

        @block.scalar
        def _(act):
            act.sem_inc(ln_done, U)
            with act.Fori(0, NG // U) as i:
                for u in range(U):
                    act.wait_ge(xc_done, i * U + (u + 1 + U))
                    act.wait_ge(var_done, i * U)
                    nc.scalar.activation(sq[:, u, :], xc[:, u, :], ACT.Square).then_inc(sq_done, 1)
                for u in range(U):
                    act.wait_ge(var_done, i * U + (u + 1))
                    nc.scalar.activation(rs[:, u, :], var[:, u, :], ACT.Ln, bias=c.eps[:, :]).then_inc(ln_done, 1)
                for u in range(U):
                    act.wait_ge(ln_done, i * U + (u + 1 + U))
                    nc.scalar.activation(rs[:, u, :], rs[:, u, :], ACT.Exp, scale=-0.5).then_inc(rs_done, 1)


def router(c, tag, w_in, bias=None):
    nc = c.nc
    w = c.router_w
    w_loaded = c.sem(tag + "_router_loaded")
    logits_done = c.sem(tag + "_logits_done")
    with nc.Block() as block:
        @block.sync
        def _(sp):
            sp.dma_start(w[:, :], w_in).then_inc(w_loaded, 16)
            if bias is not None:
                sp.dma_start(c.bias8[:, :], bias.partition_broadcast(P)).then_inc(w_loaded, 16)
            sp.wait_ge(w_loaded, 16 if bias is None else 32)

        @block.tensor
        def _(pe):
            pe.wait_ge(w_loaded, 16 if bias is None else 32)
            for t in range(NT):
                last = nc.tensor.matmul(c.banks[:, 0, t * E:(t + 1) * E], c.xn[:, t * P:(t + 1) * P], w[:, :],
                                        start=True, stop=True)
            last.then_inc(logits_done, 1)


def chain_on(engine, sem):
    n = [0]

    def link(ins):
        n[0] += 1
        ins.then_inc(sem, 1)
        engine.wait_ge(sem, n[0])
    return link


def rank_experts(c, link, v):
    nc = c.nc
    gt = c.wb[:, 0:4096].rearrange("p (t e f) -> p t e f", t=NT, e=E)
    eq = c.wb[:, 4096:8192].rearrange("p (t e f) -> p t e f", t=NT, e=E)
    other = v.unsqueeze(2).broadcast_to([P, NT, E, E])
    own = v.unsqueeze(3).broadcast_to([P, NT, E, E])
    link(nc.vector.tensor_tensor(gt, other, own, ALU.is_gt))
    link(nc.vector.tensor_tensor(eq, other, own, ALU.is_equal))
    link(nc.vector.tensor_tensor(eq, eq, c.lower[:, :, :].unsqueeze(1).broadcast_to([P, NT, E, E]), ALU.mult))
    link(nc.vector.tensor_tensor(gt, gt, eq, ALU.add))
    link(nc.vector.tensor_reduce(c.rank[:, :, :], gt, axis=AX.X, op=ALU.add))


def softmax_steps(c, link, logits, out):
    nc = c.nc
    link(nc.vector.tensor_reduce(c.s1[:, :], logits, axis=AX.X, op=ALU.max))
    link(nc.vector.tensor_tensor(out, logits, c.s1[:, :].unsqueeze(2).broadcast_to([P, NT, E]), ALU.subtract))


def route_top2_capacity(c, tag):
    nc = c.nc
    cap = -(-T * 2 * 5 // (4 * E))
    logits = c.banks[:, 0, :].rearrange("p (t e) -> p t e", e=E)
    step = c.sem(tag + "_step")
    d_ready, e_ready, m_ready, cnt_ready = (c.sem(tag + n) for n in ("_d", "_e", "_m", "_cnt"))
    flat = "p t e -> p (t e)"
    with nc.Block() as block:
        @block.vector
        def _(dve):
            link = chain_on(dve, step)
            v, oh1, oh2 = c.t1, c.t2, c.t3
            link(nc.vector.tensor_scalar(v[:, :, :], logits, 1e4, -1e4, ALU.min, ALU.max))
            rank_experts(c, link, v[:, :, :])
            link(nc.vector.tensor_scalar(oh1[:, :, :], c.rank[:, :, :], 0.0, None, ALU.is_equal))
            link(nc.vector.tensor_scalar(oh2[:, :, :], c.rank[:, :, :], 1.0, None, ALU.is_equal))
            nc.vector.tensor_scalar(c.m_b[:, :, :], c.rank[:, :, :], 2.0, None, ALU.is_lt).then_inc(m_ready, 1)
            link(nc.vector.tensor_tensor(c.t4[:, :, :], v[:, :, :], oh1[:, :, :], ALU.mult))
            link(nc.vector.tensor_reduce(c.s1[:, :], c.t4[:, :, :], axis=AX.X, op=ALU.add))
            link(nc.vector.tensor_tensor(c.t4[:, :, :], v[:, :, :], oh2[:, :, :], ALU.mult))
            link(nc.vector.tensor_reduce(c.s2[:, :], c.t4[:, :, :], axis=AX.X, op=ALU.add))
            nc.vector.tensor_tensor(c.s2[:, :], c.s2[:, :], c.s1[:, :], ALU.subtract).then_inc(d_ready, 1)
            dve.wait_ge(e_ready, 1)
            link(nc.vector.tensor_scalar(c.s1[:, :], c.s3[:, :], 1.0, 1e-12, ALU.add, ALU.add))
            link(nc.vector.reciprocal(c.s1[:, :], c.s1[:, :]))
            link(nc.vector.tensor_scalar(c.s1[:, :], c.s1[:, :], c.tanh_g[:, 4:5], None, ALU.mult))
            link(nc.vector.tensor_tensor(c.s3[:, :], c.s3[:, :], c.s1[:, :], ALU.mult))
            link(nc.vector.tensor_tensor(oh1[:, :, :], oh1[:, :, :],
                                         c.s1[:, :].unsqueeze(2).broadcast_to([P, NT, E]), ALU.mult))
            link(nc.vector.tensor_tensor(oh2[:, :, :], oh2[:, :, :],
                                         c.s3[:, :].unsqueeze(2).broadcast_to([P, NT, E]), ALU.mult))
            link(nc.vector.tensor_tensor(oh1[:, :, :], oh1[:, :, :], oh2[:, :, :], ALU.add))
            dve.wait_ge(cnt_ready, 1)
            tot, run = c.t2x, c.t4
            link(nc.vector.tensor_copy(tot[:, :, :].rearrange(flat), c.banks[:, 2, :]))
            link(nc.vector.memset(oh2[:, :, :], 1.0))
            for e in range(E):
                link(nc.vector.tensor_tensor_scan(run[:, :, e], oh2[:, :, e], tot[:, :, e], 0.0,
                                                  ALU.mult, ALU.add))
            link(nc.vector.tensor_tensor(run[:, :, :], run[:, :, :], tot[:, :, :], ALU.subtract))
            link(nc.vector.tensor_tensor(run[:, :, :].rearrange(flat), run[:, :, :].rearrange(flat),
                                         c.banks[:, 1, :], ALU.add))
            link(nc.vector.tensor_scalar(run[:, :, :], run[:, :, :], float(cap), None, ALU.is_lt))
            link(nc.vector.tensor_tensor(c.gates[:, :, :], oh1[:, :, :], run[:, :, :], ALU.mult))

        @block.scalar
        def _(act):
            act.wait_ge(d_ready, 1)
            nc.scalar.activation(c.s3[:, :], c.s2[:, :], ACT.Exp).then_inc(e_ready, 1)

        @block.tensor
        def _(pe):
            pe.wait_ge(m_ready, 1)
            nc.tensor.matmul(c.banks[:, 1, :], c.before[:, :], c.m_b[:, :, :].rearrange(flat), start=True, stop=True)
            nc.tensor.matmul(c.banks[:, 2, :], c.ones[:, :], c.m_b[:, :, :].rearrange(flat),
                             start=True, stop=True).then_inc(cnt_ready, 1)


def route_argmax(c, tag):
    nc = c.nc
    logits = c.banks[:, 0, :].rearrange("p (t e) -> p t e", e=E)
    step = c.sem(tag + "_step")
    with nc.Block() as block:
        @block.vector
        def _(dve):
            link = chain_on(dve, step)
            link(nc.vector.tensor_copy(c.t1[:, :, :], logits))
            rank_experts(c, link, c.t1[:, :, :])
            link(nc.vector.tensor_scalar(c.gates[:, :, :], c.rank[:, :, :], 0.0, c.tanh_g[:, 6:7],
                                         ALU.is_equal, ALU.mult))


def route_expert_choice(c, tag, layer, top2, keep, bias):
    nc = c.nc
    logits = c.banks[:, 0, :].rearrange("p (t e) -> p t e", e=E)
    flat = "p t e -> p (t e)"
    NQ = NT * E // P
    step, max_ready, exp_ready, score_ready, rows_ready, kept_ready, back_ready = (
        c.sem(tag + n) for n in ("_step", "_max", "_exp", "_score", "_rows", "_kept", "_back"))
    sum_in, sum_out = c.sem(tag + "_sum_in"), c.sem(tag + "_sum_out")
    rows = c.wb[:, 0:512].rearrange("p (q b s) -> p q b s", q=NQ, b=2)
    best = c.wb[:, 1024:1088]
    iota = c.wb[:, 1152:1216]
    first = c.wb[:, 1280:1344].bitcast(U32)
    hit = c.wb[:, 1408:1408 + 512].rearrange("p (q b s) -> p q b s", q=NQ, b=2)
    orig = c.wb[:, 2048:2048 + 512].rearrange("p (q b s) -> p q b s", q=NQ, b=2)
    iota_done = c.sem(tag + "_iota")
    with nc.Block() as block:
        @block.gpsimd
        def _(pool):
            nc.gpsimd.iota(c.iota_i[:, :], pattern=[[1, S]], base=0, channel_multiplier=0).then_inc(iota_done, 1)

        @block.vector
        def _(dve):
            link = chain_on(dve, step)
            v = c.t1
            if bias:
                link(nc.vector.tensor_tensor(v[:, :, :], logits, c.bias8[:, :].unsqueeze(1).broadcast_to([P, NT, E]),
                                             ALU.add))
            else:
                link(nc.vector.tensor_copy(v[:, :, :], logits))
            link(nc.vector.tensor_reduce(c.s1[:, :], v[:, :, :], axis=AX.X, op=ALU.max))
            nc.vector.tensor_tensor(v[:, :, :], v[:, :, :], c.s1[:, :].unsqueeze(2).broadcast_to([P, NT, E]),
                                    ALU.subtract).then_inc(max_ready, 1)
            dve.wait_ge(exp_ready, 1)
            link(nc.vector.tensor_reduce(c.s1[:, :], c.t2[:, :, :], axis=AX.X, op=ALU.add))
            link(nc.vector.reciprocal(c.s1[:, :], c.s1[:, :]))
            link(nc.vector.tensor_tensor(c.t3[:, :, :], c.t2[:, :, :],
                                         c.s1[:, :].unsqueeze(2).broadcast_to([P, NT, E]), ALU.mult))
            if top2:
                rank_experts(c, link, c.t3[:, :, :])
                link(nc.vector.tensor_scalar(c.t4[:, :, :], c.rank[:, :, :], 2.0, None, ALU.is_lt))
                link(nc.vector.tensor_tensor(c.t3[:, :, :], c.t3[:, :, :], c.t4[:, :, :], ALU.mult))
                nc.vector.tensor_reduce(c.s1[:, 0:E], c.t3[:, :, :].rearrange("p t e -> p e t"),
                                        axis=AX.X, op=ALU.add).then_inc(sum_in, 1)
                dve.wait_ge(sum_out, 1)
                link(nc.vector.tensor_scalar(c.s1[:, 8:16], c.banks[:, 1, 0:E], 1e-6, None, ALU.add))
                link(nc.vector.reciprocal(c.s1[:, 8:16], c.s1[:, 8:16]))
                link(nc.vector.tensor_tensor(c.t3[:, :, :], c.t3[:, :, :],
                                             c.s1[:, 8:16].unsqueeze(1).broadcast_to([P, NT, E]), ALU.mult))
                link(nc.vector.tensor_scalar(c.t3[:, :, :], c.t3[:, :, :], float(B), None, ALU.mult))
            dve.sem_inc(score_ready, 1)
            dve.wait_ge(rows_ready, 1)
            dve.wait_ge(iota_done, 1)
            link(nc.vector.tensor_copy(iota, c.iota_i[:, :]))
            link(nc.vector.tensor_copy(rows.rearrange("p q b s -> p (q b s)"), c.banks[:, 2, :]))
            link(nc.vector.tensor_copy(orig.rearrange("p q b s -> p (q b s)"), rows.rearrange("p q b s -> p (q b s)")))
            for r in range(keep // 8):
                for q in range(NQ):
                    for b in range(2):
                        k = (q * 2 + b) * 8
                        link(nc.vector.max(best[:, k:k + 8], rows[:, q, b, :]))
                        link(nc.vector.match_replace(rows[:, q, b, :], best[:, k:k + 8], rows[:, q, b, :], -1.0))
            link(nc.vector.tensor_scalar(hit, rows, 0.0, None, ALU.is_lt))
            if keep % 8:
                assert keep % 8 == 1
                for q in range(NQ):
                    for b in range(2):
                        k = (q * 2 + b) * 8
                        link(nc.vector.max(best[:, k:k + 8], rows[:, q, b, :]))
                        link(nc.vector.max_index(first[:, k:k + 8], best[:, k:k + 8], rows[:, q, b, :]))
                        link(nc.vector.tensor_copy(best[:, k:k + 8], first[:, k:k + 8]))
                        link(nc.vector.scalar_tensor_tensor(out=hit[:, q, b, :], in0=iota, scalar=best[:, k:k + 1],
                                                            in1=hit[:, q, b, :], op0=ALU.is_equal, op1=ALU.add))
            if not top2:
                link(nc.vector.tensor_tensor(hit, hit, orig, ALU.mult))
            dve.sem_inc(kept_ready, 1)
            dve.wait_ge(back_ready, 1)
            if top2:
                link(nc.vector.tensor_copy(c.gates[:, :, :].rearrange(flat), c.banks[:, 3, :]))
            else:
                link(nc.vector.tensor_scalar(c.gates[:, :, :].rearrange(flat), c.banks[:, 3, :],
                                             c.tanh_g[:, 4 + layer:5 + layer], None, ALU.mult))

        @block.scalar
        def _(act):
            act.wait_ge(max_ready, 1)
            nc.scalar.activation(c.t2[:, :, :], c.t1[:, :, :], ACT.Exp).then_inc(exp_ready, 1)

        @block.tensor
        def _(pe):
            if top2:
                pe.wait_ge(sum_in, 1)
                nc.tensor.matmul(c.banks[:, 1, 0:E], c.same_pos[:, :], c.s1[:, 0:E],
                                 start=True, stop=True).then_inc(sum_out, 1)
            pe.wait_ge(score_ready, 1)
            t3 = c.t3[:, :, :].rearrange(flat)
            for q in range(NQ):
                last = nc.tensor.transpose(c.banks[:, 2, q * P:(q + 1) * P], t3[:, q * P:(q + 1) * P], c.ident[:, :])
            last.then_inc(rows_ready, 1)
            pe.wait_ge(kept_ready, 1)
            hits = c.wb[:, 1408:1408 + 512]
            for q in range(NQ):
                last = nc.tensor.transpose(c.banks[:, 3, q * P:(q + 1) * P], hits[:, q * P:(q + 1) * P], c.ident[:, :])
            last.then_inc(back_ready, 1)


def expert_ffn(c, tag, NE, NF, gated, up, down, b1=None, b2=None, shared_gate=None, weight_loads=(), next_loads=()):
    nc = c.nc
    GB, UB, YB, BB = 0, 2, 4, 6
    hid = c.work[:, 0:8 * G].rearrange("p (k j n) -> p k j n", k=2, j=4)
    sil = c.work[:, 8 * G:10 * G].rearrange("p (k n) -> p k n", k=2)
    gbs = c.work[:, 10 * G:12 * G].rearrange("p (k n) -> p k n", k=2)
    tmp = c.work[:, 12 * G:14 * G].rearrange("p (k n) -> p k n", k=2)
    total = c.work[:, 14 * G:15 * G]
    gfix = c.gfix
    sum_used = c.sem(tag + "_sum_used")
    loaded = c.sem(tag + "_loaded")
    fetched = c.sem(tag + "_fetched")
    gfix_done = c.sem(tag + "_gfix_done")
    gb_done = c.sem(tag + "_gb_done")
    gbs_done = c.sem(tag + "_gbs_done")
    up_done = c.sem(tag + "_up_done")
    sil_done = c.sem(tag + "_sil_done")
    h_done = c.sem(tag + "_h_done")
    down_done = c.sem(tag + "_down_done")
    tmp_done = c.sem(tag + "_tmp_done")
    x_done = c.sem(tag + "_x_done")
    with nc.Block() as block:
        @block.sync
        def _(sp):
            for dst, src in weight_loads:
                sp.dma_start(dst, src).then_inc(loaded, 16)
            for dst, src in next_loads:
                sp.dma_start(dst, src).then_inc(fetched, 16)
            if weight_loads:
                sp.wait_ge(loaded, 16 * len(weight_loads))
            if next_loads:
                sp.wait_ge(fetched, 16 * len(next_loads))

        @block.tensor
        def _(pe):
            pe.sem_inc(down_done, 2)
            if weight_loads:
                pe.wait_ge(loaded, 16 * len(weight_loads))

            def down_of(g, e):
                n = g * NE + e
                pe.wait_ge(h_done, n * NF + (NF + 2))
                pe.wait_ge(tmp_done, n + 1)
                for j in range(NF):
                    last = nc.tensor.matmul(c.banks[:, YB + e % 2, :], down(e, j), hid[:, e % 2, j, :],
                                            start=(j == 0), stop=(j == NF - 1))
                last.then_inc(down_done, 1)

            with pe.Fori(0, NG) as g:
                pe.wait_ge(gfix_done, g + 1)
                for e in range(NE):
                    if e < E:
                        pe.wait_ge(gbs_done, g * E + (e + 1))
                        for k in range(TG):
                            last = nc.tensor.matmul(c.banks[:, BB + e % 2, k * P:(k + 1) * P],
                                                    gfix[:, k, e:e + 1].broadcast_to([P, P]), c.ident[:, :],
                                                    start=True, stop=True)
                        last.then_inc(gb_done, 1)
                    for j in range(NF):
                        n = (g * NE + e) * NF + j
                        pe.wait_ge(h_done, n + 1)
                        last = nc.tensor.matmul(c.banks[:, GB + j % 2, :], up(e, j, 0), cols(c.xn, g * G),
                                                start=True, stop=True)
                        if gated:
                            last = nc.tensor.matmul(c.banks[:, UB + j % 2, :], up(e, j, 1), cols(c.xn, g * G),
                                                    start=True, stop=True)
                        last.then_inc(up_done, 1)
                        if j == 0 and e > 0:
                            down_of(g, e - 1)
                down_of(g, NE - 1)

        @block.scalar
        def _(act):
            act.sem_inc(gbs_done, 2)
            if not gated:
                act.sem_inc(h_done, 2)
                if weight_loads:
                    act.wait_ge(loaded, 16 * len(weight_loads))
            with act.Fori(0, NG) as g:
                for e in range(NE):
                    if e < E:
                        act.wait_ge(gb_done, g * E + (e + 1))
                        act.wait_ge(tmp_done, g * NE + (e + 1))
                        nc.scalar.activation(gbs[:, e % 2, :], c.banks[:, BB + e % 2, :], ACT.Copy).then_inc(gbs_done, 1)
                    for j in range(NF):
                        n = (g * NE + e) * NF + j
                        act.wait_ge(up_done, n + 1)
                        if gated:
                            act.wait_ge(h_done, n + 1)
                            nc.scalar.activation(sil[:, j % 2, :], c.banks[:, GB + j % 2, :], ACT.Silu).then_inc(sil_done, 1)
                        else:
                            act.wait_ge(down_done, g * NE + (e + 1))
                            nc.scalar.activation(hid[:, e % 2, j, :], c.banks[:, GB + j % 2, :], ACT.Gelu,
                                                 bias=b1(e, j)).then_inc(h_done, 1)

        @block.vector
        def _(dve):
            dve.sem_inc(tmp_done, 2)
            if gated:
                dve.sem_inc(h_done, 2)
            if weight_loads:
                dve.wait_ge(loaded, 16 * len(weight_loads))

            def tmp_of(g, e):
                n = g * NE + e
                dve.wait_ge(down_done, n + 3)
                dve.wait_ge(x_done, n + 1)
                y = c.banks[:, YB + e % 2, :]
                if e == E:
                    nc.vector.tensor_scalar(tmp[:, e % 2, :], y, shared_gate, None, ALU.mult).then_inc(tmp_done, 1)
                    return
                dve.wait_ge(gbs_done, g * E + (e + 3))
                if b2 is None:
                    nc.vector.tensor_tensor(tmp[:, e % 2, :], y, gbs[:, e % 2, :], ALU.mult).then_inc(tmp_done, 1)
                else:
                    nc.vector.scalar_tensor_tensor(out=tmp[:, e % 2, :], in0=y, scalar=b2(e), in1=gbs[:, e % 2, :],
                                                   op0=ALU.add, op1=ALU.mult).then_inc(tmp_done, 1)

            with dve.Fori(0, NG) as g:
                for e in range(NE):
                    if gated:
                        for j in range(NF):
                            n = (g * NE + e) * NF + j
                            dve.wait_ge(sil_done, n + 1)
                            dve.wait_ge(down_done, g * NE + (e + 1))
                            nc.vector.tensor_tensor(hid[:, e % 2, j, :], sil[:, j % 2, :], c.banks[:, UB + j % 2, :],
                                                    ALU.mult).then_inc(h_done, 1)
                            if j == 1 and e > 0:
                                tmp_of(g, e - 1)
                    elif e > 0:
                        tmp_of(g, e - 1)
                tmp_of(g, NE - 1)
                dve.wait_ge(x_done, g * NE + (NE + 2))
                nc.vector.tensor_tensor(cols(c.x, g * G), cols(c.x, g * G), total, ALU.add).then_inc(sum_used, 1)

        @block.gpsimd
        def _(pool):
            pool.sem_inc(x_done, 2)
            with pool.Fori(0, NG) as g:
                pool.wait_ge(gb_done, g * E)
                nc.gpsimd.tensor_copy(gfix[:, :, :].rearrange("p k e -> p (k e)"),
                                      c.gates[:, :, :].rearrange("p t e -> p (t e)")[:, bass.ds(g * (TG * E), TG * E)]
                                      ).then_inc(gfix_done, 1)
                for e in range(1, NE):
                    pool.wait_ge(tmp_done, g * NE + (e + 3))
                    if e == 1:
                        pool.wait_ge(sum_used, g)
                        nc.gpsimd.tensor_tensor(total, tmp[:, 0, :], tmp[:, 1, :], ALU.add).then_inc(x_done, 2)
                    else:
                        pool.wait_ge(x_done, g * NE + (e + 2))
                        nc.gpsimd.tensor_tensor(total, total, tmp[:, e % 2, :], ALU.add).then_inc(x_done, 1)


def windowed_product(c, tag, ctxT):
    nc = c.nc
    cb = c.work[:, 0:2 * G].rearrange("p (k n) -> p k n", k=2)
    sq = c.work[:, 2 * G:3 * G]
    y = c.work[:, 3 * G:4 * G]
    total = c.work[:, 4 * G:4 * G + 16]
    ctx_in = [c.sem(tag + f"_ctx_in{k}") for k in range(2)]
    sq_done = c.sem(tag + "_sq_done")
    sum_done = c.sem(tag + "_sum_done")
    y_done = c.sem(tag + "_y_done")
    x_done = c.sem(tag + "_x_done")
    with nc.Block() as block:
        @block.sync
        def _(sp):
            with sp.Fori(0, NG // 2) as i:
                for k in range(2):
                    sp.wait_ge(sq_done, i * 2)
                    sp.dma_start(cb[:, k, :], cols(ctxT, i * (2 * G) + k * G)).then_inc(ctx_in[k], 16)

        @block.vector
        def _(dve):
            with dve.Fori(0, NG // 2) as i:
                for k in range(2):
                    dve.wait_ge(ctx_in[k], i * 16 + 16)
                    nc.vector.scalar_tensor_tensor(out=sq, in0=cb[:, k, :], scalar=0.0, in1=cb[:, k, :],
                                                   op0=ALU.max, op1=ALU.mult).then_inc(sq_done, 1)
                    dve.wait_ge(sq_done, i * 2 + (k + 1))
                    nc.vector.tensor_reduce(total[:, 0:BG], sq.rearrange("p (b s) -> p b s", s=S), axis=AX.X,
                                            op=ALU.add).then_inc(sum_done, 1)
                    dve.wait_ge(sum_done, i * 2 + (k + 1))
                    at = cols(c.xn, i * (2 * G) + k * G)
                    nc.vector.scalar_tensor_tensor(out=y.rearrange("p (b s) -> p b s", s=S),
                                                   in0=at.rearrange("p (b s) -> p b s", s=S), scalar=0.0,
                                                   in1=total[:, 0:BG].unsqueeze(2).broadcast_to([P, BG, S]),
                                                   op0=ALU.max, op1=ALU.mult).then_inc(y_done, 1)
                    dve.wait_ge(y_done, i * 2 + (k + 1))
                    xg = cols(c.x, i * (2 * G) + k * G)
                    nc.vector.scalar_tensor_tensor(out=xg, in0=y, scalar=c.tanh_g[:, 1:2], in1=xg,
                                                   op0=ALU.mult, op1=ALU.add).then_inc(x_done, 1)


def mask_rows(c, tag, mask, kind, scale):
    nc = c.nc
    raw = c.wb[:, 0:64].bitcast(I32) if kind == "zero_is_off" else c.wb[:, 0:64]
    val, rest = c.wb[:, 64:128], c.wb[:, 128:192]
    part = [c.wb[:, 192 + 32 * k:224 + 32 * k].bitcast(BF16) for k in range(3)]
    got, step, moved = c.sem(tag + "_mask_in"), c.sem(tag + "_mask_step"), c.sem(tag + "_mask_moved")
    made = c.sem(tag + "_mask_made")
    with nc.Block() as block:
        @block.sync
        def _(sp):
            sp.dma_start(raw, mask).then_inc(got, 16)
            sp.wait_ge(made, 1)
            for k in range(3):
                sp.dma_start(c.mrow[k:k + 1, :], part[k]).then_inc(moved, 16)
            sp.wait_ge(moved, 48)

        @block.vector
        def _(dve):
            link = chain_on(dve, step)
            dve.wait_ge(got, 16)
            if kind == "zero_is_off":
                link(nc.vector.tensor_scalar(val, raw, 0.0, -1e20 * scale, ALU.is_equal, ALU.mult))
            else:
                link(nc.vector.tensor_scalar(val, raw, -1e9, None, ALU.mult))
            link(nc.vector.tensor_copy(part[0], val))
            link(nc.vector.tensor_tensor(rest, val, part[0], ALU.subtract))
            link(nc.vector.tensor_copy(part[1], rest))
            link(nc.vector.tensor_tensor(val, rest, part[1], ALU.subtract))
            link(nc.vector.tensor_copy(part[2], val))
            dve.sem_inc(made, 1)


def attention(c, tag, ctxT, scale, gate, bq=None, bk=None, bv=None, bo=None):
    nc = c.nc
    at, wt = 0, {}
    wq, wk, wv, wo = (c.attn_w[:, k, :] for k in range(4))
    cb = c.wb[:, 4096:5120].rearrange("p (b two s) -> p b two s", b=BG, two=2)
    cbf = c.wb[:, 4096:5120]
    qs = c.wb[:, 512:1024]
    kb = c.wb[:, 1024:3072].rearrange("p (j n) -> p j n", j=4)
    ot = c.wb[:, 3072:3584]
    add = c.wb[:, 3584:4096]
    pr = c.work[:, 0:2048].rearrange("p (u n) -> p u n", u=2)
    pt = c.work[:, 2048:4096].rearrange("p (u n) -> p u n", u=2)
    vb = c.work[:, 4096:4096 + 2 * 288].rearrange("p (u a n) -> p u a n", u=2, a=16)
    on = c.work[:, 4800:4928]
    rd = c.work[:, 4928:4944]
    nm = c.work[:, 4944:4976].rearrange("p (u h) -> p u h", u=2)
    VBANK, OBANK = c.banks[:, 6, :], c.banks[:, 7, :]

    def scores(u):
        return c.banks[:, 2 * u:2 * u + 2, :]

    names = ("ctx_in", "prep", "q_mm", "k_mm", "q_done", "k_done", "s_order", "s_mm", "mask_fix", "nm_done", "sub_done", "v_mm",
             "v_used", "p_done", "t_mm", "t_used", "av_mm", "rd_done", "on_done", "ot_mm", "ot_done", "wo_mm", "add_done",
             "x_done", "ctx_free")
    m = {n: c.sem(f"{tag}_{n}") for n in names}
    with nc.Block() as block:
        @block.sync
        def _(sp):
            with sp.Fori(0, NG) as g:
                sp.wait_ge(m["v_mm"], g * TG)
                for two in range(2):
                    sp.dma_start(cb[:, :, two, :], cols(ctxT, g * G).rearrange("p (b s) -> p b s", s=S)).then_inc(
                        m["ctx_in"], 16)

        @block.tensor
        def _(pe):
            pe.wait_ge(m["prep"], 1)

            def make_scores(g, k):
                u, n = k % 2, g * TG + k
                pe.wait_ge(m["sub_done"], n + 1)
                tok = k * P
                for w in range(2):
                    for b in range(2):
                        last = nc.tensor.matmul(
                            scores(u)[S * b:S * b + S, w, :].rearrange("p (h k) -> p h k", h=8), c.ones[0:3, 0:S],
                            c.mrow_fix[0:3, tok + S * b:tok + S * b + S].unsqueeze(1).broadcast_to([3, 8, S]),
                            start=True, stop=False)
                last.then_inc(m["s_order"], 1)
                pe.wait_ge(m["s_order"], n * 2 + 1)
                for w in range(2):
                    for r in (w, 2 + w):
                        for b in range(2):
                            rows = slice(32 * r, 32 * r + 32)
                            last = nc.tensor.matmul(
                                scores(u)[S * b:S * b + S, r // 2, w * 256:w * 256 + 256].rearrange(
                                    "p (j k) -> p j k", j=4),
                                qs[rows, tok + S * b:tok + S * b + S], kb[rows, :, tok + S * b:tok + S * b + S],
                                start=False, stop=(w == 1))
                    if w == 0:
                        last.then_inc(m["s_order"], 1)
                        pe.wait_ge(m["s_order"], n * 2 + 2)
                last.then_inc(m["s_mm"], 1)
                pe.wait_ge(m["v_used"], n)
                for b in range(2):
                    last = nc.tensor.matmul(VBANK[:, b * P:(b + 1) * P],
                                            cbf[:, (2 * k + b) * P:(2 * k + b + 1) * P], wv,
                                            start=True, stop=True)
                last.then_inc(m["v_mm"], 1)

            def transpose_out(g, k):
                n = g * TG + k
                pe.wait_ge(m["on_done"], n + 1)
                nc.tensor.transpose(OBANK[:, 384:512], on, c.ident[:, :]).then_inc(m["ot_mm"], 1)

            def apply(g, k):
                u, n = k % 2, g * TG + k
                pe.wait_ge(m["p_done"], n + 1)
                for w in range(2):
                    pe.wait_ge(m["t_used"], n * 2 + (w + 1))
                    for i in range(4):
                        last = nc.tensor.transpose(c.banks[:, 4 + w, i * P:(i + 1) * P],
                                                   pr[:, u, (4 * w + i) * P:(4 * w + i + 1) * P], c.ident[:, :])
                    last.then_inc(m["t_mm"], 1)
                pe.wait_ge(m["ot_done"], n)
                pe.wait_ge(m["v_used"], n + 1)
                for w in range(2):
                    pe.wait_ge(m["t_used"], n * 2 + (w + 3))
                    for i in range(4 * w, 4 * w + 4):
                        for b in range(2):
                            last = nc.tensor.matmul(OBANK[S * b:S * b + S, i * 18:i * 18 + 18],
                                                    pt[:, u, i * P + S * b:i * P + S * b + S], vb[:, u, b * 8 + i, :],
                                                    start=True, stop=True)
                last.then_inc(m["av_mm"], 1)

            with pe.Fori(0, NG) as g:
                pe.wait_ge(m["ctx_in"], g * 32 + 32)
                pe.wait_ge(m["add_done"], g)
                nc.tensor.matmul(OBANK, wq, cols(c.xn, g * G), start=True, stop=True).then_inc(m["q_mm"], 1)
                pe.wait_ge(m["v_used"], g * TG)
                nc.tensor.matmul(VBANK.rearrange("p (b s) -> p b s", s=S), wk, cb[:, :, 0, :], start=True, stop=True).then_inc(m["k_mm"], 1)
                pe.wait_ge(m["q_done"], g + 1)
                pe.wait_ge(m["mask_fix"], g + 1)
                pe.wait_ge(m["k_done"], g * 4 + 4)
                make_scores(g, 0)
                for k in range(TG):
                    if k + 1 < TG:
                        make_scores(g, k + 1)
                    if k > 0:
                        transpose_out(g, k - 1)
                    apply(g, k)
                transpose_out(g, TG - 1)
                pe.wait_ge(m["ot_done"], g * TG + TG)
                nc.tensor.matmul(OBANK, wo, ot, start=True, stop=True).then_inc(m["wo_mm"], 1)

        @block.vector
        def _(dve):
            nc.vector.tensor_copy(vb[:, 0, :, 16:18], c.half[:, :].unsqueeze(1).broadcast_to([P, 16, 2]))
            nc.vector.tensor_copy(vb[:, 1, :, 16:18], c.half[:, :].unsqueeze(1).broadcast_to([P, 16, 2])).then_inc(
                m["prep"], 1)
            dve.sem_inc(m["sub_done"], 2)

            def soften(g, k):
                u, n = k % 2, g * TG + k
                dve.wait_ge(m["s_mm"], n + 1)
                s3 = scores(u).rearrange("p w (h k) -> p (w h) k", k=S)
                nc.vector.tensor_reduce(nm[:, u, :], s3, axis=AX.X, op=ALU.max).then_inc(m["nm_done"], 1)
                dve.wait_ge(m["nm_done"], n + 1)
                dve.wait_ge(m["t_mm"], n * 2)
                nc.vector.tensor_tensor(pr[:, u, :].rearrange("p (h k) -> p h k", k=S), s3,
                                        nm[:, u, :].unsqueeze(2).broadcast_to([P, H, S]),
                                        ALU.subtract).then_inc(m["sub_done"], 1)

            def keep_values(g, k):
                u, n = k % 2, g * TG + k
                dve.wait_ge(m["v_mm"], n + 1)
                dve.wait_ge(m["av_mm"], n)
                nc.vector.tensor_tensor(vb[:, u, :, 0:16].rearrange("p a n -> p a n"),
                                        VBANK[:, 0:256].rearrange("p (a n) -> p a n", n=16),
                                        c.half16[:, :, :].rearrange("p j d -> p (j d)").unsqueeze(1).broadcast_to(
                                            [P, 16, 16]), ALU.mult).then_inc(m["v_used"], 1)

            def normalise(g, k):
                n = g * TG + k
                dve.wait_ge(m["av_mm"], n + 1)
                o = OBANK[:, 0:144].rearrange("p (i n) -> p i n", n=18)
                nc.vector.reciprocal(rd.rearrange("p (i j) -> p i j", j=2), o[:, :, 16:18]).then_inc(m["rd_done"], 1)
                dve.wait_ge(m["rd_done"], n + 1)
                dve.wait_ge(m["ot_mm"], n)
                nc.vector.tensor_tensor(on.rearrange("p (i j d) -> p i j d", i=8, j=2),
                                        o[:, :, 0:16].rearrange("p i (j d) -> p i j d", j=2),
                                        rd.rearrange("p (i j) -> p i j", j=2).unsqueeze(3).broadcast_to([P, 8, 2, HD]),
                                        ALU.mult).then_inc(m["on_done"], 1)

            with dve.Fori(0, NG) as g:
                dve.wait_ge(m["k_mm"], g + 1)
                dve.wait_ge(m["s_mm"], g * TG)
                for j in range(4):
                    nc.vector.tensor_scalar(kb[:, j, :], VBANK, bk, c.quad[:, j:j + 1], ALU.add,
                                            ALU.mult).then_inc(m["k_done"], 1)
                soften(g, 0)
                keep_values(g, 0)
                for k in range(TG):
                    if k + 1 < TG:
                        soften(g, k + 1)
                        keep_values(g, k + 1)
                    normalise(g, k)
                dve.wait_ge(m["add_done"], g + 1)
                nc.vector.tensor_tensor(cols(c.x, g * G), cols(c.x, g * G), add, ALU.add).then_inc(m["x_done"], 1)

        @block.gpsimd
        def _(pool):
            with pool.Fori(0, NG) as g:
                pool.wait_ge(m["s_mm"], g * TG)
                nc.gpsimd.tensor_copy(c.mrow_fix[0:3, :], c.mrow[0:3, bass.ds(g * G, G)]).then_inc(m["mask_fix"], 1)

        @block.scalar
        def _(act):
            act.sem_inc(m["t_used"], 2)

            def exps(g, k):
                u, n = k % 2, g * TG + k
                act.wait_ge(m["sub_done"], n + 3)
                nc.scalar.activation(pr[:, u, :], pr[:, u, :], ACT.Exp).then_inc(m["p_done"], 1)

            def copies(g, k):
                u, n = k % 2, g * TG + k
                act.wait_ge(m["av_mm"], n)
                for w in range(2):
                    act.wait_ge(m["t_mm"], n * 2 + (w + 1))
                    nc.scalar.activation(pt[:, u, w * G:(w + 1) * G], c.banks[:, 4 + w, :], ACT.Copy).then_inc(
                        m["t_used"], 1)

            def copy_out(g, k):
                n = g * TG + k
                act.wait_ge(m["ot_mm"], n + 1)
                nc.scalar.activation(ot[:, k * P:(k + 1) * P], OBANK[:, 384:512], ACT.Identity, bias=bv).then_inc(
                    m["ot_done"], 1)

            with act.Fori(0, NG) as g:
                act.wait_ge(m["q_mm"], g + 1)
                nc.scalar.activation(qs, OBANK, ACT.Identity, bias=bq, scale=scale).then_inc(m["q_done"], 1)
                exps(g, 0)
                for k in range(TG):
                    if k + 1 < TG:
                        exps(g, k + 1)
                    if k > 0:
                        copy_out(g, k - 1)
                    copies(g, k)
                copy_out(g, TG - 1)
                act.wait_ge(m["wo_mm"], g + 1)
                act.wait_ge(m["x_done"], g)
                nc.scalar.activation(add, OBANK, ACT.Identity, bias=bo, scale=gate).then_inc(m["add_done"], 1)


def attention_weights(c, tag, A, layer, block_diagonal, biases):
    nc = c.nc
    got, cleared, step = c.sem(tag + "_w_in"), c.sem(tag + "_w_cleared"), c.sem(tag + "_w_step")
    scale = HD ** -0.5 if not block_diagonal else P ** -0.5
    col = c.attn_b
    with nc.Block() as block:
        @block.gpsimd
        def _(pool):
            nc.gpsimd.memset(c.attn_w[:, :, :], 0.0).then_inc(cleared, 1)
            nc.gpsimd.memset(col[:, :], 0.0).then_inc(cleared, 1)

        @block.sync
        def _(sp):
            n = 0
            sp.wait_ge(cleared, 2)
            for k, w in enumerate(("Wq", "Wk", "Wv", "Wo")):
                src = A[f"L{layer}_xattn_{w}T"]
                if block_diagonal and w != "Wo":
                    for h in range(H):
                        sp.dma_start(c.attn_w[h * HD:(h + 1) * HD, k, h * HD:(h + 1) * HD], src).then_inc(got, 16)
                        n += 1
                else:
                    sp.dma_start(c.attn_w[:, k, :], src).then_inc(got, 16)
                    n += 1
            for k, b in enumerate(biases):
                if b is not None:
                    sp.dma_start(col[:, k:k + 1], A[b].unsqueeze(1)).then_inc(got, 16)
                    n += 1
            sp.wait_ge(got, 16 * n)
            sp.sem_inc(step, 1)

        @block.vector
        def _(dve):
            dve.wait_ge(step, 1)
            nc.vector.tensor_scalar(col[:, 0:1], col[:, 0:1], scale, None, ALU.mult)
            nc.vector.tensor_tensor(col[:, 3:4], col[:, 3:4], c.tanh_g[:, layer:layer + 1], ALU.mult).then_inc(step, 1)
            dve.wait_ge(step, 2)


def two_way_attention(c, tag, A, ctxT, ctx_q):
    nc = c.nc
    wl = c.attn_w
    col = c.cols16
    cb = c.work[:, 0:512]
    ctq = c.work[0:S, 512:1536].rearrange("q (b d) -> q b d", b=BG)
    cc = c.work[:, 1536:2048]
    xg = c.work[:, 2048:2560]
    a = c.work[:, 2560:2816].rearrange("p (k q) -> p k q", q=S)
    at = c.work[0:S, 3072:3584]
    ml = c.work[:, 3584:3588]
    cw = c.work[:, 3588:3592]
    sm = c.work[:, 3592:3596]
    lg = c.work[:, 3600:3664]
    lt = c.work[0:NT, 3712:3840].rearrange("t (b s) -> t b s", b=2)
    lm = c.work[0:NT, 3840:3842]
    wtok = c.work[:, 3904:3968]
    c2q = c.wb
    names = ("w_in", "b_done", "ctx_in", "ctq_in", "cc_done", "xg_done", "s_mm", "m_done", "l_done", "a_sub", "a_exp", "r_done",
             "a_done", "at_mm", "at_done", "c2q_mm", "c2q_done", "rr_done", "s1_done")
    m = {n: c.sem(f"{tag}_{n}") for n in names}
    SB, TB, CB = c.banks[:, 0, :], c.banks[0:S, 1, :], c.banks[:, 2, :]
    with nc.Block() as block:
        @block.sync
        def _(sp):
            sp.dma_start(wl[:, :, :].rearrange("p k n -> p (k n)"), A["L2_xattn_W_lT"]).then_inc(m["w_in"], 16)
            for k, n in enumerate(("L2_xattn_w_cq", "L2_xattn_w_q", "L2_xattn_w_c", "L2_xattn_b_l")):
                sp.dma_start(col[:, k:k + 1], A[n].unsqueeze(1)).then_inc(m["w_in"], 16)
            for k, n in enumerate(("L2_xattn_b_cq", "L2_xattn_b_c", "L2_xattn_b_q")):
                sp.dma_start(col[:, 4 + k:5 + k], A[n].partition_broadcast(P)).then_inc(m["w_in"], 16)
            with sp.Fori(0, NG) as g:
                sp.wait_ge(m["c2q_mm"], g)
                sp.dma_start(cb, cols(ctxT, g * G)).then_inc(m["ctx_in"], 16)
                sp.dma_start(ctq.rearrange("q b d -> q (b d)"), cols(ctx_q, g * (BG * P), BG * P)).then_inc(
                    m["ctq_in"], 16)

        @block.tensor
        def _(pe):
            pe.wait_ge(m["w_in"], 128)
            with pe.Fori(0, NG) as g:
                pe.wait_ge(m["ctx_in"], g * 16 + 16)
                pe.wait_ge(m["cc_done"], g + 1)
                pe.wait_ge(m["xg_done"], g + 1)
                pe.wait_ge(m["a_sub"], g)
                pe.wait_ge(m["l_done"], g)
                for k in range(TG):
                    for b in range(2):
                        t0 = k * P + b * S
                        nc.tensor.matmul(SB[b * S:(b + 1) * S, k * S:(k + 1) * S], cc[:, t0:t0 + S], cb[:, t0:t0 + S],
                                         start=True, stop=True)
                    last = nc.tensor.matmul(SB[:, 256 + k:257 + k], xg[:, k * P:(k + 1) * P], col[:, 2:3],
                                            start=True, stop=True)
                last.then_inc(m["s_mm"], 1)
                pe.wait_ge(m["a_done"], g + 1)
                for k in range(TG):
                    last = nc.tensor.matmul(TB[:, k * P:(k + 1) * P], a[:, k, :], c.ident[:, :], start=True, stop=True)
                last.then_inc(m["at_mm"], 1)
                pe.wait_ge(m["at_done"], g + 1)
                pe.wait_ge(m["ctq_in"], g * 16 + 16)
                pe.wait_ge(m["c2q_done"], g)
                for b in range(BG):
                    last = nc.tensor.matmul(CB[:, b * S:(b + 1) * S], ctq[:, b, :], at[:, b * S:(b + 1) * S],
                                            start=True, stop=True)
                last.then_inc(m["c2q_mm"], 1)

        @block.vector
        def _(dve):
            dve.wait_ge(m["w_in"], 128)
            nc.vector.tensor_scalar(col[:, 4:5], col[:, 4:5], col[:, 5:6], col[:, 6:7], ALU.add, ALU.add)
            nc.vector.tensor_tensor(col[:, 7:8], col[:, 3:4], c.tanh_g[:, 2:3], ALU.mult).then_inc(m["b_done"], 1)
            dve.wait_ge(m["b_done"], 1)
            s3 = SB[:, 0:256].rearrange("p (k q) -> p k q", q=S)
            with dve.Fori(0, NG) as g:
                dve.wait_ge(m["s_mm"], g)
                nc.vector.tensor_scalar(cc, cols(c.xn, g * G), col[:, 0:1], col[:, 1:2], ALU.mult,
                                        ALU.add).then_inc(m["cc_done"], 1)
                dve.wait_ge(m["s_mm"], g + 1)
                nc.vector.tensor_reduce(ml, s3, axis=AX.X, op=ALU.max).then_inc(m["m_done"], 1)
                dve.wait_ge(m["m_done"], g + 1)
                nc.vector.scalar_tensor_tensor(out=lg[:, bass.ds(g * TG, TG)], in0=SB[:, 256:260], scalar=col[:, 4:5],
                                               in1=ml, op0=ALU.add, op1=ALU.add).then_inc(m["l_done"], 1)
                dve.wait_ge(m["at_mm"], g)
                nc.vector.tensor_tensor(a, s3, ml.unsqueeze(2).broadcast_to([P, TG, S]),
                                        ALU.subtract).then_inc(m["a_sub"], 1)
                dve.wait_ge(m["a_exp"], g + 1)
                nc.vector.tensor_reduce(sm, a, axis=AX.X, op=ALU.add).then_inc(m["s1_done"], 1)
                dve.wait_ge(m["s1_done"], g + 1)
                nc.vector.reciprocal(sm, sm).then_inc(m["r_done"], 1)
                dve.wait_ge(m["r_done"], g + 1)
                nc.vector.tensor_tensor(a, a, sm.unsqueeze(2).broadcast_to([P, TG, S]), ALU.mult).then_inc(
                    m["a_done"], 1)

        @block.scalar
        def _(act):
            with act.Fori(0, NG) as g:
                act.wait_ge(m["s_mm"], g)
                nc.scalar.activation(xg, cols(c.xn, g * G), ACT.Copy).then_inc(m["xg_done"], 1)
                act.wait_ge(m["a_sub"], g + 1)
                nc.scalar.activation(a, a, ACT.Exp).then_inc(m["a_exp"], 1)
                act.wait_ge(m["at_mm"], g + 1)
                act.wait_ge(m["c2q_mm"], g)
                nc.scalar.activation(at, TB, ACT.Copy).then_inc(m["at_done"], 1)
                act.wait_ge(m["c2q_mm"], g + 1)
                nc.scalar.activation(cols(c2q, g * G), CB, ACT.Copy).then_inc(m["c2q_done"], 1)

    step, lt_mm, lt_sub, lt_exp, lt_done, back = (c.sem(tag + n) for n in ("_st", "_ltm", "_lts", "_lte", "_ltd", "_bk"))
    with nc.Block() as block:
        @block.tensor
        def _(pe):
            nc.tensor.transpose(c.banks[0:NT, 3, 0:P], lg, c.ident[:, :]).then_inc(lt_mm, 1)
            pe.wait_ge(lt_done, 1)
            nc.tensor.transpose(c.banks[:, 4, 0:NT], lt.rearrange("t b s -> t (b s)"),
                                c.ident[0:NT, 0:NT]).then_inc(back, 1)

        @block.scalar
        def _(act):
            act.wait_ge(lt_sub, 1)
            nc.scalar.activation(lt, lt, ACT.Exp).then_inc(lt_exp, 1)

        @block.vector
        def _(dve):
            link = chain_on(dve, step)
            dve.wait_ge(lt_mm, 1)
            raw = c.banks[0:NT, 3, 0:P].rearrange("t (b s) -> t b s", b=2)
            link(nc.vector.tensor_reduce(lm, raw, axis=AX.X, op=ALU.max))
            nc.vector.tensor_tensor(lt, raw, lm.unsqueeze(2).broadcast_to([NT, 2, S]), ALU.subtract).then_inc(lt_sub, 1)
            dve.wait_ge(lt_exp, 1)
            link(nc.vector.tensor_reduce(lm, lt, axis=AX.X, op=ALU.add))
            link(nc.vector.reciprocal(lm, lm))
            nc.vector.tensor_tensor(lt, lt, lm.unsqueeze(2).broadcast_to([NT, 2, S]), ALU.mult).then_inc(lt_done, 1)
            dve.wait_ge(back, 1)
            link(nc.vector.tensor_copy(wtok, c.banks[:, 4, 0:NT]))

    wfix = c.work[:, 4000:4004]
    prod = c.work[:, 4096:4608]
    x3 = c.work[:, 4608:5120]
    x4 = c.work[:, 5120:5632]
    add = c.work[:, 5632:6144]
    qc = c.work[:, 6144:6144 + BG]
    m = {n: c.sem(f"{tag}b_{n}") for n in ("wfix", "bc_mm", "prod", "qc", "x3", "x4", "z_mm", "add", "x")}
    with nc.Block() as block:
        @block.gpsimd
        def _(pool):
            with pool.Fori(0, NG) as g:
                pool.wait_ge(m["bc_mm"], g)
                nc.gpsimd.tensor_copy(wfix, wtok[:, bass.ds(g * TG, TG)]).then_inc(m["wfix"], 1)

        @block.tensor
        def _(pe):
            with pe.Fori(0, NG) as g:
                pe.wait_ge(m["wfix"], g + 1)
                pe.wait_ge(m["prod"], g)
                for k in range(TG):
                    last = nc.tensor.matmul(c.banks[:, 5, k * P:(k + 1) * P], wfix[:, k:k + 1].broadcast_to([P, P]),
                                            c.ident[:, :], start=True, stop=True)
                last.then_inc(m["bc_mm"], 1)
                pe.wait_ge(m["add"], g)
                nc.tensor.matmul(c.banks[:, 6, :], wl[:, 0, :], cols(c.xn, g * G), start=True, stop=False)
                nc.tensor.matmul(c.banks[:, 6, :], wl[:, 1, :], cols(c2q, g * G), start=False, stop=False)
                pe.wait_ge(m["x3"], g + 1)
                nc.tensor.matmul(c.banks[:, 6, :], wl[:, 2, :], x3, start=False, stop=False)
                pe.wait_ge(m["x4"], g + 1)
                nc.tensor.matmul(c.banks[:, 6, :], wl[:, 3, :], x4, start=False, stop=True).then_inc(m["z_mm"], 1)

        @block.vector
        def _(dve):
            with dve.Fori(0, NG) as g:
                xn = cols(c.xn, g * G)
                dve.wait_ge(m["z_mm"], g)
                nc.vector.tensor_tensor(x3, xn, cols(c2q, g * G), ALU.mult).then_inc(m["x3"], 1)
                dve.wait_ge(m["bc_mm"], g + 1)
                dve.wait_ge(m["qc"], g)
                nc.vector.tensor_tensor(prod, xn, c.banks[:, 5, :], ALU.mult).then_inc(m["prod"], 1)
                dve.wait_ge(m["prod"], g + 1)
                dve.wait_ge(m["x4"], g)
                nc.vector.tensor_reduce(qc, prod.rearrange("p (b s) -> p b s", s=S), axis=AX.X, op=ALU.add).then_inc(
                    m["qc"], 1)
                dve.wait_ge(m["qc"], g + 1)
                nc.vector.tensor_tensor(x4.rearrange("p (b s) -> p b s", s=S), xn.rearrange("p (b s) -> p b s", s=S),
                                        qc.unsqueeze(2).broadcast_to([P, BG, S]), ALU.mult).then_inc(m["x4"], 1)
                dve.wait_ge(m["add"], g + 1)
                nc.vector.tensor_tensor(cols(c.x, g * G), cols(c.x, g * G), add, ALU.add).then_inc(m["x"], 1)

        @block.scalar
        def _(act):
            with act.Fori(0, NG) as g:
                act.wait_ge(m["z_mm"], g + 1)
                act.wait_ge(m["x"], g)
                nc.scalar.activation(add, c.banks[:, 6, :], ACT.Identity, bias=col[:, 7:8],
                                     scale=c.tanh_g[:, 2:3]).then_inc(m["add"], 1)


def small_ffn(c, tag, A):
    nc = c.nc
    F = 32
    w1 = c.wa[:, 0:256]
    w2 = c.wa[:, 256:512].rearrange("p (j n) -> p j n", j=2)
    b1, b2 = c.wa[:, 512:514], c.wa[0:E, 640:768]
    wide = c.work[:, 0:1024].rearrange("p (k e f) -> p k e f", k=TG, e=E)
    narrow = c.work[:, 1024:1056].rearrange("p (k e) -> p k e", k=TG)
    hg = c.work[:, 1536:2560].rearrange("p (j n) -> p j n", j=2)
    hm = c.work[:, 2560:3584].rearrange("p (j n) -> p j n", j=2)
    mt = c.work[0:E, 3584:4096]
    m = {n: c.sem(f"{tag}_{n}") for n in ("w_in", "wide", "narrow", "h_mm", "mask_mm", "mt_mm", "hg", "hm", "mt", "y_mm", "x")}
    with nc.Block() as block:
        @block.sync
        def _(sp):
            sp.dma_start(w1, A["L3_ffn_W1T"]).then_inc(m["w_in"], 16)
            sp.dma_start(c.wa[:, 256:512], A["L3_ffn_W2T"]).then_inc(m["w_in"], 16)
            sp.dma_start(b1, A["L3_ffn_b1T"]).then_inc(m["w_in"], 16)
            sp.dma_start(b2, A["L3_ffn_b2"]).then_inc(m["w_in"], 16)

        @block.gpsimd
        def _(pool):
            with pool.Fori(0, NG) as g:
                pool.wait_ge(m["mt_mm"], g)
                pool.wait_ge(m["wide"], g)
                flat = c.gates[:, :, :].rearrange("p t e -> p (t e)")[:, bass.ds(g * (TG * E), TG * E)]
                nc.gpsimd.tensor_copy(narrow.rearrange("p k e -> p (k e)"), flat).then_inc(m["narrow"], 1)

        @block.tensor
        def _(pe):
            pe.wait_ge(m["w_in"], 64)
            with pe.Fori(0, NG) as g:
                for j in range(2):
                    pe.wait_ge(m["hg"], g * 2 + j)
                    nc.tensor.matmul(c.banks[:, j, :], w1[:, j * P:(j + 1) * P], cols(c.xn, g * G),
                                     start=True, stop=True).then_inc(m["h_mm"], 1)
                pe.wait_ge(m["wide"], g + 1)
                for j in range(2):
                    pe.wait_ge(m["hm"], g * 2 + j)
                    for k in range(TG):
                        last = nc.tensor.matmul(c.banks[:, 2 + j, k * P:(k + 1) * P],
                                                wide[:, k, 4 * j:4 * j + 4, :].rearrange("p e f -> p (e f)"),
                                                c.ident[:, :], start=True, stop=True)
                    last.then_inc(m["mask_mm"], 1)
                pe.wait_ge(m["mt"], g)
                for k in range(TG):
                    last = nc.tensor.matmul(c.banks[0:E, 4, k * P:(k + 1) * P], narrow[:, k, :], c.ident[:, :],
                                            start=True, stop=True)
                last.then_inc(m["mt_mm"], 1)
                pe.wait_ge(m["x"], g)
                for j in range(2):
                    pe.wait_ge(m["hm"], g * 2 + j + 1)
                    nc.tensor.matmul(c.banks[:, 5, :], w2[:, j, :], hm[:, j, :], start=(j == 0), stop=False)
                pe.wait_ge(m["mt"], g + 1)
                nc.tensor.matmul(c.banks[:, 5, :], b2, mt, start=False, stop=True).then_inc(m["y_mm"], 1)

        @block.scalar
        def _(act):
            act.wait_ge(m["w_in"], 64)
            with act.Fori(0, NG) as g:
                act.wait_ge(m["narrow"], g + 1)
                act.wait_ge(m["mask_mm"], g * 2)
                nc.scalar.activation(wide.rearrange("p k e f -> p (k e) f"),
                                     narrow.rearrange("p k e -> p (k e)").unsqueeze(2).broadcast_to([P, TG * E, F]),
                                     ACT.Copy).then_inc(m["wide"], 1)
                for j in range(2):
                    act.wait_ge(m["h_mm"], g * 2 + j + 1)
                    act.wait_ge(m["hm"], g * 2 + j)
                    nc.scalar.activation(hg[:, j, :], c.banks[:, j, :], ACT.Gelu, bias=b1[:, j:j + 1]).then_inc(
                        m["hg"], 1)
                act.wait_ge(m["mt_mm"], g + 1)
                act.wait_ge(m["y_mm"], g)
                nc.scalar.activation(mt, c.banks[0:E, 4, :], ACT.Copy).then_inc(m["mt"], 1)

        @block.vector
        def _(dve):
            with dve.Fori(0, NG) as g:
                for j in range(2):
                    dve.wait_ge(m["hg"], g * 2 + j + 1)
                    dve.wait_ge(m["mask_mm"], g * 2 + j + 1)
                    dve.wait_ge(m["y_mm"], g)
                    nc.vector.tensor_tensor(hm[:, j, :], hg[:, j, :], c.banks[:, 2 + j, :], ALU.mult).then_inc(m["hm"], 1)
                dve.wait_ge(m["y_mm"], g + 1)
                xg = cols(c.x, g * G)
                nc.vector.scalar_tensor_tensor(out=xg, in0=c.banks[:, 5, :], scalar=c.tanh_g[:, 7:8], in1=xg,
                                               op0=ALU.mult, op1=ALU.add).then_inc(m["x"], 1)


def store(c, out):
    nc = c.nc
    stored = c.sem("stored")
    with nc.Block() as block:
        @block.sync
        def _(sp):
            for k in range(4):
                sp.dma_start(out[:, k * 2048:(k + 1) * 2048], c.x[:, k * 2048:(k + 1) * 2048]).then_inc(stored, 16)
            sp.wait_ge(stored, 64)


def small_loads(c, tag, loads):
    nc = c.nc
    got = c.sem(tag + "_got")
    with nc.Block() as block:
        @block.sync
        def _(sp):
            for dst, src in loads:
                sp.dma_start(dst, src).then_inc(got, 16)
            sp.wait_ge(got, 16 * len(loads))


def program(nc, A, out):
    with ExitStack() as ctx:
        c = Chip(nc, ctx)
        setup(c, A)
        c.router_w = c.sb("router_w", [P, E])
        c.bias8 = c.sb("bias8", [P, E])
        c.rank = c.sb("rank", [P, NT, E])
        c.t1, c.t2, c.t3, c.t4, c.t2x = (c.sb(f"route{k}", [P, NT, E]) for k in range(5))
        c.m_b = c.sb("chosen", [P, NT, E], BF16)
        c.s1, c.s2, c.s3 = (c.sb(f"per_token{k}", [P, NT]) for k in range(3))
        c.gfix = c.sb("gfix", [P, TG, E])
        c.iota_i = c.sb("iota_i", [P, S], I32)

        c.attn_w = c.sb("attn_w", [P, 4, P])
        c.attn_b = c.sb("attn_b", [P, 4])
        c.mrow = c.wa[:, 0:4096].bitcast(BF16)
        c.mrow_fix = c.sb("mrow_fix", [P, G], BF16)

        def attend(layer, scale, mask, kind, biases, block_diagonal):
            t = f"a{layer}"
            attention_weights(c, t, A, layer, block_diagonal, biases)
            mask_rows(c, t, mask, kind, scale)
            col = [c.attn_b[:, k:k + 1] for k in range(4)]
            attention(c, t, A["ctxT"], scale, c.tanh_g[:, layer:layer + 1], *col)


        layer_norm(c, "n0", c.x, c.xn)
        attend(0, P ** -0.5, A["mask_if1"], "zero_is_off", (None, None, None, "L0_xattn_bo"), True)

        small_loads(c, "l0f_affine", [(c.cols16[:, 0:1], A["L0_ffn_ln_gamma"].unsqueeze(1)),
                                      (c.cols16[:, 1:2], A["L0_ffn_ln_beta"].unsqueeze(1))])
        layer_norm(c, "n1a", c.x, c.xn)
        layer_norm(c, "n1b", c.xn, c.xn, (c.cols16[:, 0:1], c.cols16[:, 1:2]))
        router(c, "l0", A["L0_ffn_router_wT"])
        route_top2_capacity(c, "l0")
        w12 = c.wa[:, 0:8192].rearrange("p (e f) -> p e f", e=E)
        w3 = c.wa[:, 8192:12288].rearrange("p (e j n) -> p e j n", e=E, j=4)
        expert_ffn(c, "l0f", E, 4, True,
                   lambda e, j, k: w12[:, e, (4 * k + j) * P:(4 * k + j + 1) * P],
                   lambda e, j: w3[:, e, j, :],
                   weight_loads=[(c.wa[:, 0:8192], A["L0_ffn_w12T"]), (c.wa[:, 8192:12288], A["L0_ffn_w3T"])])

        c.recycle_semaphores()
        layer_norm(c, "n2", c.x, c.xn)
        windowed_product(c, "l1x", A["ctxT"])

        c.recycle_semaphores()
        layer_norm(c, "n3", c.x, c.xn)
        router(c, "l1", A["L1_ffn_router_wT"])
        route_expert_choice(c, "l1", 1, False, S * 2 // E + 1, False)
        w1 = c.wb[:, 0:4096].rearrange("p (e f) -> p e f", e=E)
        w2 = c.wb[:, 4096:8192].rearrange("p (e j n) -> p e j n", e=E, j=4)
        b1 = c.cols16[:, 2:34].rearrange("p (e j) -> p e j", e=E)
        expert_ffn(c, "l1f", E, 4, False,
                   lambda e, j, k: w1[:, e, j * P:(j + 1) * P], lambda e, j: w2[:, e, j, :],
                   b1=lambda e, j: b1[:, e, j:j + 1], b2=lambda e: c.cols16[:, 34 + e:35 + e],
                   weight_loads=[(c.wb[:, 0:4096], A["L1_ffn_w1T"]), (c.wb[:, 4096:8192], A["L1_ffn_w2T"]),
                                 (c.cols16[:, 2:34], A["L1_ffn_b1T"]), (c.cols16[:, 34:42], A["L1_ffn_b2T"])])

        layer_norm(c, "n4", c.x, c.xn)
        two_way_attention(c, "bi", A, A["ctxT"], A["ctx_q"])

        c.recycle_semaphores()
        layer_norm(c, "n5", c.x, c.xn)
        router(c, "l2", A["L2_ffn_routerT"])
        route_argmax(c, "l2")
        NE = E + 1
        wu = c.wa[:, 0:2304].rearrange("p (e f) -> p e f", e=NE)
        wg = c.wa[:, 2304:4608].rearrange("p (e f) -> p e f", e=NE)
        wd = c.wa[:, 4608:6912].rearrange("p (e j n) -> p e j n", e=NE, j=2)
        expert_ffn(c, "l2f", NE, 2, True,
                   lambda e, j, k: (wg, wu)[k][:, e, j * P:(j + 1) * P], lambda e, j: wd[:, e, j, :],
                   shared_gate=c.tanh_g[:, 6:7],
                   weight_loads=[(c.wa[:, 0:2304], A["L2_ffn_upT"]), (c.wa[:, 2304:4608], A["L2_ffn_gateT"]),
                                 (c.wa[:, 4608:6912], A["L2_ffn_downT"])])

        c.recycle_semaphores()
        layer_norm(c, "n6", c.x, c.xn)
        attend(3, HD ** -0.5, A["mask_fk0"], "one_is_off",
               ("L3_xattn_bq", "L3_xattn_bk", "L3_xattn_bv", "L3_xattn_bo"), False)

        layer_norm(c, "n7", c.x, c.xn)
        router(c, "l3", A["L3_ffn_w_gate_w"], A["L3_ffn_w_gate_b"])
        route_expert_choice(c, "l3", 3, True, S // 2, True)
        small_ffn(c, "l3f", A)
        store(c, out)


def kernel(**inputs):
    import numpy as _np
    import concourse.bacc as _bacc
    from concourse import mybir as _mybir
    from concourse.bass_utils import run_bass_kernel_spmd as _run

    v = {k: _np.asarray(a) for k, a in inputs.items()}

    def tiles_last(w):
        e, o, f = w.shape
        return w.reshape(e, o, f // 128, 128).transpose(3, 0, 2, 1).reshape(128, -1)

    def tiles_first(w):
        e, f, o = w.shape
        return w.reshape(e, f // 128, 128, o).transpose(2, 0, 1, 3).reshape(128, -1)

    lay = {
        "xT": v["x"].reshape(8192, 128).T,
        "ctxT": v["ctx_1024"].reshape(8192, 128).T,
        "ctx_q": v["ctx_1024"].transpose(1, 0, 2).reshape(64, -1),
        "L2_xattn_W_lT": v["L2_xattn_W_l"].reshape(128, 4, 128).transpose(2, 1, 0).reshape(128, -1),
        "L2_xattn_b_cq": v["L2_xattn_b_cq"].reshape(1),
        "L2_xattn_b_c": v["L2_xattn_b_c"].reshape(1),
        "L2_xattn_b_q": v["L2_xattn_b_q"].reshape(1),
        "L3_ffn_W1T": v["L3_ffn_W1"].transpose(1, 0, 2).reshape(128, -1),
        "L3_ffn_W2T": v["L3_ffn_W2"].reshape(2, 128, 128).transpose(1, 0, 2).reshape(128, -1),
        "L3_ffn_b1T": v["L3_ffn_b1"].reshape(2, 128).T,
        "L0_ffn_router_wT": v["L0_ffn_router_w"].T,
        "L0_ffn_w12T": v["L0_ffn_w12"].transpose(2, 0, 1).reshape(128, -1),
        "L0_ffn_w3T": tiles_last(v["L0_ffn_w3"]),
        "L1_ffn_router_wT": v["L1_ffn_router_w"].T,
        "L1_ffn_w1T": v["L1_ffn_w1"].transpose(1, 0, 2).reshape(128, -1),
        "L1_ffn_w2T": tiles_first(v["L1_ffn_w2"]),
        "L1_ffn_b1T": v["L1_ffn_b1"].reshape(8, 4, 128).transpose(2, 0, 1).reshape(128, -1),
        "L1_ffn_b2T": v["L1_ffn_b2"].T,
        "L2_ffn_routerT": v["L2_ffn_router"].T,
        "L2_ffn_upT": _np.concatenate([v["L2_ffn_up"], v["L2_ffn_w_up_s"][None]]).transpose(2, 0, 1).reshape(128, -1),
        "L2_ffn_gateT": _np.concatenate([v["L2_ffn_gate"], v["L2_ffn_w_gate_s"][None]]).transpose(2, 0, 1).reshape(128, -1),
        "L2_ffn_downT": tiles_last(_np.concatenate([v["L2_ffn_down"], v["L2_ffn_w_down_s"][None]])),
    }
    for w in ("Wq", "Wk", "Wv", "Wo"):
        lay[f"L0_xattn_{w}T"] = v[f"L0_xattn_{w}"].T
        lay[f"L3_xattn_{w}T"] = v[f"L3_xattn_{w.lower()}"]
    lay["mask_if1"] = v["mask_Bx1x1xS2_if1"].reshape(128, 64)
    lay["mask_fk0"] = v["mask_Bx1x1xS2_fk0"].reshape(128, 64)
    for name in ("L0_xattn_bo", "L3_xattn_bq", "L3_xattn_bk", "L3_xattn_bv", "L3_xattn_bo",
                 "L2_xattn_w_cq", "L2_xattn_w_q", "L2_xattn_w_c", "L2_xattn_b_l", "L3_ffn_w_gate_w", "L3_ffn_w_gate_b",
                 "L3_ffn_b2", "g_xattn", "g_ffn", "L0_ffn_ln_gamma", "L0_ffn_ln_beta"):
        lay[name] = v[name]

    nc = _bacc.Bacc("TRN2", target_bir_lowering=False, num_devices=1)
    arrays, A = {}, {}
    for name, a in lay.items():
        a = _np.ascontiguousarray(a)
        arrays[f"in_{name}"] = a
        A[name] = nc.dram_tensor(f"in_{name}", a.shape, _mybir.dt.from_np(a.dtype), kind="ExternalInput").ap()
    out = nc.dram_tensor("out_0_dram", (128, 8192), _mybir.dt.float32, kind="ExternalOutput").ap()
    program(nc, A, out)
    r = _run(nc, [arrays], core_ids=[0])
    return _np.ascontiguousarray(r.results[0]["out_0_dram"].T).reshape(128, 64, 128)
```

```python
from contextlib import ExitStack

import concourse.bass as bass
from concourse import mybir

F32 = mybir.dt.float32
BF16 = mybir.dt.bfloat16
I32 = mybir.dt.int32
U32 = mybir.dt.uint32
ALU = mybir.AluOpType
ACT = mybir.ActivationFunctionType
AX = mybir.AxisListType

P = 128
B, S = 128, 64
T = B * S
NT = T // P
G = 512
NG = T // G
TG = G // P
BG = G // S
E = 8
H, HD = 16, 8
EPS = 1e-5
L0_CAP = -(-T * 2 * 5 // (4 * E))
L0_GROUPS = E * L0_CAP // G
assert L0_CAP % G == 0
L2_GROUPS = (NG + E) // 2 * 2
BEYOND = float(2 ** 20)





class Chip:

    def __init__(self, nc, ctx):
        self.nc, self.ctx = nc, ctx
        self.sems = []

    def sb(self, name, shape, dt=F32):
        return self.ctx.enter_context(self.nc.sbuf_tensor(name, shape, dt))

    def sem(self, name):
        handle = self.nc.alloc_semaphore(name=name)
        self.sems.append(handle)
        return handle

    def recycle_semaphores(self):
        self.nc.clear_and_free_semaphores(self.sems)
        self.sems = []
        self.nc.all_engine_barrier()


def cols(t, at, n=G):
    return t[:, bass.ds(at, n)]


def over(ap, shape):
    return ap.broadcast_to(shape)


def start_at_1(engine, m, *names):
    for name in names:
        engine.sem_inc(m[name], 1)


def setup(c, A):
    nc = c.nc
    c.xpad = c.sb("x", [P, G + T])
    c.x = c.xpad[:, G:G + T]
    c.xn = c.sb("xn", [P, T])
    c.wa = c.sb("weights_a", [P, 12288])
    c.wb = c.sb("weights_b", [P, 8192])
    c.work = c.sb("work", [P, 8192])
    c.avg = c.sb("avg", [P, P])
    c.ident = c.sb("ident", [P, P])
    c.same_pos = c.sb("same_pos", [P, P])
    c.before = c.sb("before", [P, P], BF16)
    c.ones = c.sb("ones", [P, P], BF16)
    c.lower = c.sb("lower", [P, E, E])
    c.half = c.sb("half", [P, 2])
    c.half16 = c.sb("half16", [P, 2, HD])
    c.quad = c.sb("quad", [P, 4])
    c.eps = c.sb("eps", [P, 1])
    c.gate_in = c.sb("gate_in", [P, 8])
    c.tanh_g = c.sb("tanh_g", [P, 8])
    c.gates = c.sb("gates", [P, NT, E])
    c.cols16 = c.sb("cols16", [P, 64])
    c.banks = c.ctx.enter_context(nc.psum_tensor("banks", [P, 8, G], F32))
    x_in = c.sem("x_in")
    small_in = c.sem("small_in")
    filled = c.sem("filled")
    tanhed = c.sem("tanhed")
    with nc.Block() as block:
        @block.sync
        def _(sp):
            for k in range(4):
                sp.dma_start(c.x[:, k * 2048:(k + 1) * 2048], A["xT"][:, k * 2048:(k + 1) * 2048]).then_inc(x_in, 16)
            sp.wait_ge(x_in, 64)

        @block.scalar
        def _(act):
            act.dma_start(c.gate_in[:, 0:4], A["g_xattn"].partition_broadcast(P)).then_inc(small_in, 16)
            act.dma_start(c.gate_in[:, 4:8], A["g_ffn"].partition_broadcast(P)).then_inc(small_in, 16)
            act.wait_ge(small_in, 32)
            nc.scalar.activation(c.tanh_g[:, :], c.gate_in[:, :], ACT.Tanh).then_inc(tanhed, 1)

        @block.gpsimd
        def _(pool):
            done = [0]

            def put(ins):
                done[0] += 1
                ins.then_inc(filled, 1)
                pool.wait_ge(filled, done[0])

            def keep(t, pattern, base, mult, cmp, fill=0.0):
                put(nc.gpsimd.affine_select(out=t, in_=t, compare_op=cmp, fill=fill, base=base,
                                            pattern=pattern, channel_multiplier=mult))

            put(nc.gpsimd.memset(c.avg[:, :], 1.0 / P))
            put(nc.gpsimd.memset(c.xpad[:, 0:G], 0.0))
            put(nc.gpsimd.memset(c.eps[:, :], EPS))
            put(nc.gpsimd.memset(c.ones[:, :], 1.0))
            put(nc.gpsimd.memset(c.ident[:, :], 0.0))
            keep(c.ident[:, :], [[-1, P]], 0, 1, ALU.not_equal, 1.0)
            put(nc.gpsimd.memset(c.same_pos[:, :], 0.0))
            for off in (-S, 0, S):
                keep(c.same_pos[:, :], [[-1, P]], off, 1, ALU.not_equal, 1.0)
            put(nc.gpsimd.memset(c.before[:, :], 1.0))
            keep(c.before[:, :], [[1, P]], -1, -1, ALU.is_ge)
            put(nc.gpsimd.memset(c.lower[:, :, :], 1.0))
            keep(c.lower[:, :, :], [[1, E], [-1, E]], -1, 0, ALU.is_ge)
            put(nc.gpsimd.memset(c.half[:, :], 1.0))
            keep(c.half[:, :], [[-S, 2]], 0, 1, ALU.is_ge)
            keep(c.half[:, :], [[S, 2]], S - 1, -1, ALU.is_ge)
            put(nc.gpsimd.memset(c.half16[:, :, :], 1.0))
            keep(c.half16[:, :, :], [[-S, 2], [0, HD]], 0, 1, ALU.is_ge)
            keep(c.half16[:, :, :], [[S, 2], [0, HD]], S - 1, -1, ALU.is_ge)
            put(nc.gpsimd.memset(c.quad[:, :], 0.0))
            for q in range(4):
                rows = c.quad[32 * q:32 * q + 32, :]
                put(nc.gpsimd.memset(rows, 1.0))
                keep(rows, [[-HD, 4]], 0, 1, ALU.is_ge)
                keep(rows, [[HD, 4]], HD - 1, -1, ALU.is_ge)


def layer_norm(c, tag, src, dst, affine=None):
    nc = c.nc
    U, AHEAD = 4, 3
    sq = c.work[:, 0:U * G].rearrange("p (u n) -> p u n", u=U)
    fix = c.work[:, U * G:U * G + U * TG].rearrange("p (u k) -> p u k", u=U)
    rs, va, nw = (c.work[:, 2176 + 64 * k:2240 + 64 * k] for k in range(3))
    mean, var, wide = c.banks[:, 0:U, :], c.banks[:, 4, 0:NT], c.banks[:, 0:U, :]
    m = {n: c.sem(f"{tag}_{n}") for n in ("mean", "xc", "sq", "var", "ln", "exp", "step", "rs", "fix", "wide", "scaled",
                                          "out")}

    def slots(engine, slot):
        with engine.Fori(0, NG // U - 1) as i:
            for u in range(U):
                slot(i * U + u, u, True)
        for u in range(U):
            slot(NG - U + u, u, u + AHEAD < U)

    with nc.Block() as block:
        @block.tensor
        def _(pe):
            pe.sem_inc(m["var"], U)
            pe.sem_inc(m["wide"], U)

            def take_mean(s, u):
                pe.wait_ge(m["xc"], s + 1)
                nc.tensor.matmul(mean[:, u, :], c.avg[:, :], cols(src, s * G), start=True,
                                 stop=True).then_inc(m["mean"], 1)

            def variance(s, u, more):
                pe.wait_ge(m["sq"], s + 1)
                for k in range(TG):
                    last = nc.tensor.matmul(var[:, bass.ds(s * TG + k, 1)], sq[:, u, k * P:(k + 1) * P],
                                            c.avg[:, 0:1], start=True, stop=True)
                last.then_inc(m["var"], 1)
                if more:
                    take_mean(s + AHEAD, (u + AHEAD) % U)

            def widen(s, u, more):
                pe.wait_ge(m["fix"], s + 1)
                pe.wait_ge(m["out"], s + 1)
                for k in range(TG):
                    last = nc.tensor.matmul(wide[:, u, k * P:(k + 1) * P], fix[:, u, k:k + 1].broadcast_to([P, P]),
                                            c.ident[:, :], start=True, stop=True)
                last.then_inc(m["wide"], 1)

            for s in range(AHEAD):
                take_mean(s, s)
            slots(pe, variance)
            slots(pe, widen)

        @block.vector
        def _(dve):
            dve.sem_inc(m["xc"], U)
            dve.sem_inc(m["out"], U)
            link = chain_on(dve, m["step"])

            def centre(s, u):
                dve.wait_ge(m["mean"], s + 1)
                nc.vector.tensor_tensor(cols(dst, s * G), cols(src, s * G), mean[:, u, :],
                                        ALU.subtract).then_inc(m["xc"], 1)

            def scale(s, u, more):
                dve.wait_ge(m["wide"], s + (U + 1))
                at = cols(dst, s * G)
                if affine is None:
                    nc.vector.tensor_tensor(at, at, wide[:, u, :], ALU.mult).then_inc(m["out"], 1)
                else:
                    nc.vector.scalar_tensor_tensor(out=at, in0=at, scalar=affine[0], in1=wide[:, u, :], op0=ALU.mult,
                                                   op1=ALU.mult).then_inc(m["out"], 1)

            for s in range(AHEAD):
                centre(s, s)
            with dve.Fori(0, NG // U - 1) as i:
                for u in range(U):
                    centre(i * U + u + AHEAD, (u + AHEAD) % U)
            for s in range(NG - U + AHEAD, NG):
                centre(s, s % U)
            dve.wait_ge(m["exp"], 1)
            link(nc.vector.tensor_tensor(nw, rs, rs, ALU.mult))
            link(nc.vector.tensor_tensor(nw, nw, va, ALU.mult))
            link(nc.vector.tensor_scalar(nw, nw, -0.5, 1.5, ALU.mult, ALU.add))
            nc.vector.tensor_tensor(rs, rs, nw, ALU.mult).then_inc(m["rs"], 1)
            slots(dve, scale)

        @block.scalar
        def _(act):
            def square(s, u):
                act.wait_ge(m["xc"], s + (U + 1))
                act.wait_ge(m["var"], s + 1)
                nc.scalar.activation(sq[:, u, :], cols(dst, s * G), ACT.Square).then_inc(m["sq"], 1)

            def fixed(s, u, more):
                act.wait_ge(m["wide"], s + 1)
                nc.scalar.activation(fix[:, u, :], rs[:, bass.ds(s * TG, TG)], ACT.Copy).then_inc(m["fix"], 1)

            def shift(s, u, more):
                act.wait_ge(m["out"], s + (U + 1))
                at = cols(dst, s * G)
                nc.scalar.activation(at, at, ACT.Identity, bias=affine[1]).then_inc(m["scaled"], 1)

            for s in range(AHEAD):
                square(s, s)
            with act.Fori(0, NG // U - 1) as i:
                for u in range(U):
                    square(i * U + u + AHEAD, (u + AHEAD) % U)
            for s in range(NG - U + AHEAD, NG):
                square(s, s % U)
            act.wait_ge(m["var"], NG + U)
            nc.scalar.activation(va, var, ACT.Identity, bias=c.eps[:, :]).then_inc(m["ln"], 1)
            act.wait_ge(m["ln"], 1)
            nc.scalar.activation(rs, va, ACT.Ln).then_inc(m["ln"], 1)
            act.wait_ge(m["ln"], 2)
            nc.scalar.activation(rs, rs, ACT.Exp, scale=-0.5).then_inc(m["exp"], 1)
            act.wait_ge(m["rs"], 1)
            slots(act, fixed)
            if affine is not None:
                slots(act, shift)


def router(c, tag, w_in, bias=None):
    nc = c.nc
    w = c.router_w
    w_loaded = c.sem(tag + "_router_loaded")
    logits_done = c.sem(tag + "_logits_done")
    with nc.Block() as block:
        @block.sync
        def _(sp):
            sp.dma_start(w[:, :], w_in).then_inc(w_loaded, 16)
            if bias is not None:
                sp.dma_start(c.bias8[:, :], bias.partition_broadcast(P)).then_inc(w_loaded, 16)
            sp.wait_ge(w_loaded, 16 if bias is None else 32)

        @block.tensor
        def _(pe):
            pe.wait_ge(w_loaded, 16 if bias is None else 32)
            for t in range(NT):
                last = nc.tensor.matmul(c.banks[:, 0, t * E:(t + 1) * E], c.xn[:, t * P:(t + 1) * P], w[:, :],
                                        start=True, stop=True)
            last.then_inc(logits_done, 1)


def chain_on(engine, sem):
    n = [0]

    def link(ins):
        n[0] += 1
        ins.then_inc(sem, 1)
        engine.wait_ge(sem, n[0])
    return link


def rank_experts(c, link, v):
    nc = c.nc
    gt = c.wb[:, 0:4096].rearrange("p (t e f) -> p t e f", t=NT, e=E)
    eq = c.wb[:, 4096:8192].rearrange("p (t e f) -> p t e f", t=NT, e=E)
    other = v.unsqueeze(2).broadcast_to([P, NT, E, E])
    own = v.unsqueeze(3).broadcast_to([P, NT, E, E])
    link(nc.vector.tensor_tensor(gt, other, own, ALU.is_gt))
    link(nc.vector.tensor_tensor(eq, other, own, ALU.is_equal))
    link(nc.vector.tensor_tensor(eq, eq, c.lower[:, :, :].unsqueeze(1).broadcast_to([P, NT, E, E]), ALU.mult))
    link(nc.vector.tensor_tensor(gt, gt, eq, ALU.add))
    link(nc.vector.tensor_reduce(c.rank[:, :, :], gt, axis=AX.X, op=ALU.add))


def softmax_steps(c, link, logits, out):
    nc = c.nc
    link(nc.vector.tensor_reduce(c.s1[:, :], logits, axis=AX.X, op=ALU.max))
    link(nc.vector.tensor_tensor(out, logits, c.s1[:, :].unsqueeze(2).broadcast_to([P, NT, E]), ALU.subtract))


def running_counts(c, link, ready):
    nc = c.nc
    flat = "p t e -> p (t e)"
    tot, run, one = c.t2x, c.t4, c.rank
    ready()
    link(nc.vector.tensor_copy(tot[:, :, :].rearrange(flat), c.banks[:, 2, :]))
    link(nc.vector.memset(one[:, :, :], 1.0))
    for e in range(E):
        link(nc.vector.tensor_tensor_scan(run[:, :, e], one[:, :, e], tot[:, :, e], 0.0, ALU.mult, ALU.add))
    link(nc.vector.tensor_copy(c.per_expert[:, 0, :], run[:, NT - 1, :]))
    link(nc.vector.tensor_tensor(run[:, :, :], run[:, :, :], tot[:, :, :], ALU.subtract))
    link(nc.vector.tensor_tensor(run[:, :, :].rearrange(flat), run[:, :, :].rearrange(flat), c.banks[:, 1, :], ALU.add))


def count_chosen(c, pe, chosen, counted):
    nc = c.nc
    chose = c.m_b[:, :, :].rearrange("p t e -> p (t e)")
    pe.wait_ge(chosen, 1)
    nc.tensor.matmul(c.banks[:, 1, :], c.before[:, :], chose, start=True, stop=True)
    nc.tensor.matmul(c.banks[:, 2, :], c.ones[:, :], chose, start=True, stop=True).then_inc(counted, 1)


def pick(c, link, out, one_hot, values):
    nc = c.nc
    link(nc.vector.tensor_tensor(c.t2x[:, :, :], one_hot, values, ALU.mult))
    link(nc.vector.tensor_reduce(out, c.t2x[:, :, :], axis=AX.X, op=ALU.add))


def route_top2_capacity(c, tag):
    nc = c.nc
    cap = L0_CAP
    logits = c.banks[:, 0, :].rearrange("p (t e) -> p t e", e=E)
    step = c.sem(tag + "_step")
    gap_ready, exp_ready, chosen, counted = (c.sem(tag + n) for n in ("_gap", "_exp", "_chosen", "_counted"))
    with nc.Block() as block:
        @block.vector
        def _(dve):
            link = chain_on(dve, step)
            v, oh = c.t1, (c.t2, c.t3)
            link(nc.vector.tensor_scalar(v[:, :, :], logits, 1e4, -1e4, ALU.min, ALU.max))
            rank_experts(c, link, v[:, :, :])
            nc.vector.tensor_scalar(c.m_b[:, :, :], c.rank[:, :, :], 2.0, None, ALU.is_lt).then_inc(chosen, 1)
            for k in range(2):
                link(nc.vector.tensor_scalar(oh[k][:, :, :], c.rank[:, :, :], float(k), None, ALU.is_equal))
            pick(c, link, c.s1[:, :], oh[0][:, :, :], v[:, :, :])
            pick(c, link, c.s2[:, :], oh[1][:, :, :], v[:, :, :])
            nc.vector.tensor_tensor(c.s2[:, :], c.s2[:, :], c.s1[:, :], ALU.subtract).then_inc(gap_ready, 1)
            running_counts(c, link, lambda: dve.wait_ge(counted, 1))
            dve.wait_ge(exp_ready, 1)
            link(nc.vector.tensor_scalar(c.s1[:, :], c.s3[:, :], 1.0, 1e-12, ALU.add, ALU.add))
            link(nc.vector.reciprocal(c.s1[:, :], c.s1[:, :]))
            link(nc.vector.tensor_scalar(c.s1[:, :], c.s1[:, :], c.tanh_g[:, 4:5], None, ALU.mult))
            link(nc.vector.tensor_tensor(c.s3[:, :], c.s3[:, :], c.s1[:, :], ALU.mult))
            link(nc.vector.tensor_reduce(c.per_expert[:, 0, :], c.lower[:, :, :], axis=AX.X, op=ALU.add))
            link(nc.vector.tensor_scalar(c.per_expert[:, 0, :], c.per_expert[:, 0, :], float(cap), None, ALU.mult))
            for k, gate in enumerate((c.s1, c.s3)):
                pick(c, link, c.s2[:, :], oh[k][:, :, :], c.t4[:, :, :])
                link(nc.vector.tensor_scalar(c.s2[:, :], c.s2[:, :], float(cap), None, ALU.is_lt))
                link(nc.vector.tensor_tensor(c.token_gates[:, :, k], gate[:, :], c.s2[:, :], ALU.mult))
                link(nc.vector.tensor_scalar(c.s2[:, :], c.s2[:, :], -BEYOND, BEYOND, ALU.mult, ALU.add))
                pick(c, link, c.slots[:, :, k], oh[k][:, :, :], c.t4[:, :, :])
                link(nc.vector.tensor_tensor(c.s2[:, :], c.s2[:, :], c.slots[:, :, k], ALU.add))
                pick(c, link, c.slots[:, :, k], oh[k][:, :, :],
                     c.per_expert[:, 0, :].unsqueeze(1).broadcast_to([P, NT, E]))
                link(nc.vector.tensor_tensor(c.slots[:, :, k], c.slots[:, :, k], c.s2[:, :], ALU.add))

        @block.scalar
        def _(act):
            act.wait_ge(gap_ready, 1)
            nc.scalar.activation(c.s3[:, :], c.s2[:, :], ACT.Exp).then_inc(exp_ready, 1)

        @block.tensor
        def _(pe):
            count_chosen(c, pe, chosen, counted)


def route_argmax(c, tag):
    nc = c.nc
    logits = c.banks[:, 0, :].rearrange("p (t e) -> p t e", e=E)
    step, chosen, counted = (c.sem(tag + n) for n in ("_step", "_chosen", "_counted"))
    numbered = c.sem(tag + "_numbered")
    at = c.wb[:, 0:L2_GROUPS]
    row = c.wb[:, 64:65]
    past = c.wb[:, 128:128 + L2_GROUPS * E]
    full = c.wb[:, 512:512 + E * NG].rearrange("p (e g) -> p e g", e=E)
    with nc.Block() as block:
        @block.gpsimd
        def _(pool):
            nc.gpsimd.iota(c.iota_i[:, 0:32], pattern=[[1, 32]], base=0, channel_multiplier=0).then_inc(numbered, 1)
            nc.gpsimd.iota(c.iota_i[:, 32:33], pattern=[[0, 1]], base=0, channel_multiplier=1).then_inc(numbered, 1)

        @block.vector
        def _(dve):
            link = chain_on(dve, step)
            link(nc.vector.tensor_copy(c.t1[:, :, :], logits))
            rank_experts(c, link, c.t1[:, :, :])
            nc.vector.tensor_scalar(c.m_b[:, :, :], c.rank[:, :, :], 1.0, None, ALU.is_lt).then_inc(chosen, 1)
            link(nc.vector.tensor_scalar(c.t3[:, :, :], c.rank[:, :, :], 0.0, None, ALU.is_equal))
            running_counts(c, link, lambda: dve.wait_ge(counted, 1))
            dve.wait_ge(numbered, 2)
            link(nc.vector.tensor_copy(at, c.iota_i[:, 0:L2_GROUPS]))
            link(nc.vector.tensor_copy(row, c.iota_i[:, 32:33]))
            tokens, ends, groups = (c.per_expert[:, k, :] for k in range(3))
            link(nc.vector.tensor_scalar(c.s1[:, 0:NG], at[:, 0:NG], float(G), None, ALU.mult))
            link(nc.vector.tensor_tensor(full, tokens.unsqueeze(2).broadcast_to([P, E, NG]),
                                         c.s1[:, 0:NG].unsqueeze(1).broadcast_to([P, E, NG]), ALU.is_gt))
            link(nc.vector.tensor_reduce(groups, full, axis=AX.X, op=ALU.add))
            link(nc.vector.memset(c.s2[:, 0:E], 1.0))
            link(nc.vector.tensor_tensor_scan(ends, c.s2[:, 0:E], groups, 0.0, ALU.mult, ALU.add))
            p3 = past.rearrange("p (g e) -> p g e", e=E)
            link(nc.vector.tensor_tensor(p3, ends.unsqueeze(1).broadcast_to([P, L2_GROUPS, E]),
                                         at.unsqueeze(2).broadcast_to([P, L2_GROUPS, E]), ALU.is_le))
            link(nc.vector.tensor_reduce(at, p3, axis=AX.X, op=ALU.add))
            link(nc.vector.tensor_scalar(at, at, float(E - 1), float(P), ALU.min, ALU.mult))
            link(nc.vector.tensor_scalar(c.weight_rows[:, :], at, row, None, ALU.add))
            link(nc.vector.tensor_tensor(ends, ends, groups, ALU.subtract))
            link(nc.vector.tensor_scalar(ends, ends, float(G), None, ALU.mult))
            link(nc.vector.tensor_tensor(c.t4[:, :, :], c.t4[:, :, :], ends.unsqueeze(1).broadcast_to([P, NT, E]),
                                         ALU.add))
            pick(c, link, c.slots[:, :, 0], c.t3[:, :, :], c.t4[:, :, :])

        @block.tensor
        def _(pe):
            count_chosen(c, pe, chosen, counted)


def row_groups(dram):
    return dram.rearrange("(g p s) d -> p g (s d)", p=P, s=TG)


def dispatch(c, tag, K, last_slot, shared=None, zeroed=False):
    nc = c.nc
    fix = c.work[:, 0:2 * G].rearrange("p (u n) -> p u n", u=2)
    rows = c.wb[:, 0:2 * G].rearrange("p (u k n) -> p u k n", u=2, k=TG)
    sil = c.work[:, 2 * G:4 * G].rearrange("p (j n) -> p j n", j=2)
    hid = c.work[:, 4 * G:6 * G].rearrange("p (j n) -> p j n", j=2)
    index = c.index[:, :, 0:TG * K]
    written = [c.sem(f"{tag}_written{u}") for u in range(2)]
    m = {n: c.sem(f"{tag}_{n}") for n in ("fix", "t_mm", "rows", "index", "up_mm", "silu", "hid", "y_mm", "x", "go")}
    per_use = 16 * TG * K
    slots = c.slots[:, :, :].rearrange("p t k -> p k t")[:, 0:K, :]
    with nc.Block() as block:
        def groups(engine, body):
            with engine.Fori(0, NG // 2) as i:
                for u in range(2):
                    body(i, i * 2 + u, u)

        @block.scalar
        def _(act):
            def body(i, g, u):
                act.wait_ge(m["t_mm"], g + 1)
                if shared:
                    act.wait_ge(m["up_mm"], g + 1)
                nc.scalar.activation(fix[:, u, :], cols(c.xn, g * G), ACT.Copy).then_inc(m["fix"], 1)
                if shared:
                    act.wait_ge(m["up_mm"], g + 3)
                    act.wait_ge(m["hid"], g * 2 + 1)
                    for j in range(2):
                        nc.scalar.activation(sil[:, j, :], c.banks[:, 2 + j, :], ACT.Silu).then_inc(m["silu"], 1)

            groups(act, body)

        @block.tensor
        def _(pe):
            pe.sem_inc(m["t_mm"], 2)
            pe.sem_inc(m["up_mm"], 2)
            pe.sem_inc(m["y_mm"], 1)

            def body(i, g, u):
                pe.wait_ge(m["fix"], g + 1)
                pe.wait_ge(m["rows"], g + 1)
                for k in range(TG):
                    last = nc.tensor.transpose(c.banks[:, u, k * P:(k + 1) * P], fix[:, u, k * P:(k + 1) * P],
                                               c.ident[:, :])
                last.then_inc(m["t_mm"], 1)
                if shared:
                    pe.wait_ge(m["hid"], g * 2 + 1)
                    for j in range(2):
                        nc.tensor.matmul(c.banks[:, 2 + j, :], shared[0][:, j * P:(j + 1) * P], fix[:, u, :],
                                         start=True, stop=True)
                        last = nc.tensor.matmul(c.banks[:, 4 + j, :], shared[1][:, j * P:(j + 1) * P], fix[:, u, :],
                                                start=True, stop=True)
                    last.then_inc(m["up_mm"], 1)
                    pe.wait_ge(m["hid"], g * 2 + 3)
                    pe.wait_ge(m["x"], g + 1)
                    for j in range(2):
                        last = nc.tensor.matmul(c.banks[:, 6, :], shared[2][:, j, :], hid[:, j, :],
                                                start=(j == 0), stop=(j == 1))
                    last.then_inc(m["y_mm"], 1)

            groups(pe, body)

        @block.vector
        def _(dve):
            dve.sem_inc(m["rows"], 2)
            dve.sem_inc(m["hid"], 1)
            dve.sem_inc(m["x"], 1)

            def body(i, g, u, first=False):
                if not first:
                    dve.wait_ge(written[u], i * per_use)
                nc.vector.tensor_copy(index[:, u, :].rearrange("p (k t) -> p k t", k=K),
                                      slots[:, :, bass.ds(g * TG, TG)]).then_inc(m["index"], 1)
                dve.wait_ge(m["t_mm"], g + 3)
                nc.vector.tensor_copy(rows[:, u, :, :].rearrange("p k n -> p (k n)"), c.banks[:, u, :]).then_inc(
                    m["rows"], 1)
                if shared:
                    for j in range(2):
                        dve.wait_ge(m["silu"], g * 2 + (j + 1))
                        dve.wait_ge(m["y_mm"], g + 1)
                        nc.vector.tensor_tensor(hid[:, j, :], sil[:, j, :], c.banks[:, 4 + j, :], ALU.mult).then_inc(
                            m["hid"], 1)
                    dve.wait_ge(m["y_mm"], g + 2)
                    at = cols(c.x, g * G)
                    nc.vector.scalar_tensor_tensor(out=at, in0=c.banks[:, 6, :], scalar=shared[3], in1=at,
                                                   op0=ALU.mult, op1=ALU.add).then_inc(m["x"], 1)

            for u in range(2):
                body(0, u, u, first=True)
            with dve.Fori(1, NG // 2) as i:
                for u in range(2):
                    body(i, i * 2 + u, u)

        @block.gpsimd
        def _(pool):
            limit = pool.to_reg(last_slot)
            if zeroed:
                pool.wait_ge(c.zeroed, 16 * ZEROING)

            def body(i, g, u):
                pool.wait_ge(m["index"], g + 1)
                pool.wait_ge(m["rows"], g + 3)
                pool.sem_inc(m["go"], 1)
                for t in range(TG):
                    for k in range(K):
                        nc.gpsimd.indirect_dma_start(
                            c.rows_in[:, :], bass.IndirectOffsetOnAxis(index[:, u, k * TG + t:k * TG + t + 1], 0),
                            rows[:, u, t, :], None, bounds_check=limit, oob_is_err=False).then_inc(written[u], 16)

            groups(pool, body)
            for u in range(2):
                pool.wait_ge(written[u], NG // 2 * per_use)


def grouped_ffn(c, tag, NF, groups, weights, weight_loads=(), fetch=None):
    nc = c.nc
    came = c.wb[:, 0:G]
    xt = c.wb[:, G:2 * G]
    sil = c.work[:, 0:2 * G].rearrange("p (j n) -> p j n", j=2)
    hid = c.work[:, 2 * G:6 * G].rearrange("p (j n) -> p j n", j=4)
    y = c.work[:, 6 * G:7 * G]
    src, dst = row_groups(c.rows_in), row_groups(c.rows_out)
    TB, YB = c.banks[:, 4, :], c.banks[:, 5, :]
    m = {n: c.sem(f"{tag}_{n}") for n in ("loaded", "came", "t_mm", "xt", "up_mm", "silu", "hid", "y_mm", "y", "left")}
    with nc.Block() as block:
        @block.sync
        def _(sp):
            def load(r):
                sp.dma_start(came, src[:, bass.ds(r, 1), :].rearrange("p g n -> p (g n)")).then_inc(m["came"], 16)

            load(0)
            for a, b in weight_loads:
                sp.dma_start(a, b).then_inc(m["loaded"], 16)
            sp.sem_inc(m["left"], 1)

            def body(r, key):
                sp.wait_ge(m["t_mm"], r + 1)
                load(r + 1)
                sp.wait_ge(m["y"], r + 2)
                sp.dma_start(dst[:, bass.ds(r, 1), :].rearrange("p g n -> p (g n)"), y).then_inc(m["left"], 16)

            n = groups(sp, body)
            sp.wait_ge(m["left"], 16 * n + 1)
            sp.wait_ge(m["came"], 16 * n + 16)

        if fetch:
            @block.gpsimd
            def _(pool):
                for n in range(fetch[0]):
                    if n >= 2:
                        pool.wait_ge(m["y_mm"], n)
                    fetch[1](n)
                for v in range(2):
                    pool.wait_ge(fetch[2][v], fetch[0] // 2 * 16)

        @block.tensor
        def _(pe):
            pe.sem_inc(m["y_mm"], 1)

            def transposes(r):
                pe.wait_ge(m["came"], r * 16 + 16)
                for s in range(TG):
                    last = nc.tensor.transpose(TB[:, s * P:(s + 1) * P], came[:, s * P:(s + 1) * P], c.ident[:, :])
                last.then_inc(m["t_mm"], 1)

            def body(r, key):
                gate, up, down = weights(key)
                pe.wait_ge(m["xt"], r + 1)
                if fetch:
                    pe.wait_ge(fetch[2][key[1]], key[0] * 16 + 16)
                for j in range(NF):
                    pe.wait_ge(m["hid"], r * NF + (j + 1))
                    nc.tensor.matmul(c.banks[:, j % 2, :], gate(j), xt, start=True, stop=True)
                    nc.tensor.matmul(c.banks[:, 2 + j % 2, :], up(j), xt, start=True, stop=True).then_inc(m["up_mm"], 1)
                transposes(r + 1)
                pe.wait_ge(m["y"], r + 1)
                pe.wait_ge(m["hid"], r * NF + (NF + 2))
                for s in range(TG):
                    for j in range(NF):
                        last = nc.tensor.matmul(YB[:, s * P:(s + 1) * P], hid[:, j, s * P:(s + 1) * P], down(j),
                                                start=(j == 0), stop=(j == NF - 1))
                last.then_inc(m["y_mm"], 1)

            transposes(0)
            if weight_loads:
                pe.wait_ge(m["loaded"], 16 * len(weight_loads))
            groups(pe, body)

        @block.scalar
        def _(act):
            def body(r, key):
                for j in range(NF):
                    act.wait_ge(m["up_mm"], r * NF + (j + 1))
                    act.wait_ge(m["hid"], r * NF + (j + 1))
                    nc.scalar.activation(sil[:, j % 2, :], c.banks[:, j % 2, :], ACT.Silu).then_inc(m["silu"], 1)

            groups(act, body)

        @block.vector
        def _(dve):
            dve.sem_inc(m["hid"], 2)
            dve.sem_inc(m["y"], 1)

            def body(r, key):
                for j in range(NF):
                    dve.wait_ge(m["silu"], r * NF + (j + 1))
                    dve.wait_ge(m["y_mm"], r + 1)
                    nc.vector.tensor_tensor(hid[:, j, :], sil[:, j % 2, :], c.banks[:, 2 + j % 2, :],
                                            ALU.mult).then_inc(m["hid"], 1)
                dve.wait_ge(m["t_mm"], r + 2)
                nc.vector.tensor_copy(xt, TB).then_inc(m["xt"], 1)
                dve.wait_ge(m["y_mm"], r + 2)
                dve.wait_ge(m["left"], r * 16 + 1)
                nc.vector.tensor_copy(y, YB).then_inc(m["y"], 1)

            dve.wait_ge(m["t_mm"], 1)
            nc.vector.tensor_copy(xt, TB).then_inc(m["xt"], 1)
            groups(dve, body)


def combine(c, tag, K, last_slot, gate=None):
    nc = c.nc
    got = c.work[:, 0:2 * K * G].rearrange("p (u k t n) -> p u k t n", u=2, k=K, t=TG)
    index = c.index[:, :, 0:TG * K]
    slots = c.slots[:, :, :].rearrange("p t k -> p k t")[:, 0:K, :]
    gates = c.token_gates[:, :, :].rearrange("p t k -> p k t")[:, 0:K, :]
    arrived = [c.sem(f"{tag}_arrived{u}") for u in range(2)]
    m = {n: c.sem(f"{tag}_{n}") for n in ("index", "gated", "summed", "t_mm", "x", "go")}
    per_use = 16 * TG * K
    with nc.Block() as block:
        def groups(engine, body):
            with engine.Fori(0, NG // 2) as i:
                for u in range(2):
                    body(i, i * 2 + u, u)

        @block.gpsimd
        def _(pool):
            limit = pool.to_reg(last_slot)

            def body(i, g, u):
                pool.wait_ge(m["index"], g + 1)
                pool.wait_ge(m["t_mm"], g + 1)
                pool.sem_inc(m["go"], 1)
                for t in range(TG):
                    for k in range(K):
                        nc.gpsimd.indirect_dma_start(
                            got[:, u, k, t, :], None, c.rows_out[:, :],
                            bass.IndirectOffsetOnAxis(index[:, u, k * TG + t:k * TG + t + 1], 0),
                            bounds_check=limit, oob_is_err=False).then_inc(arrived[u], 16)

            groups(pool, body)

        @block.vector
        def _(dve):
            dve.sem_inc(m["x"], 2)

            def make_index(g, u):
                nc.vector.tensor_scalar(index[:, u, :].rearrange("p (k t) -> p k t", k=K),
                                        slots[:, :, bass.ds(g * TG, TG)], float(last_slot), None, ALU.min).then_inc(
                    m["index"], 1)

            def take(i, g, u, more):
                dve.wait_ge(arrived[u], i * per_use + per_use)
                if K == 2:
                    nc.vector.tensor_tensor(got[:, u, :, :, :], got[:, u, :, :, :],
                                            gates[:, :, bass.ds(g * TG, TG)].unsqueeze(3).broadcast_to([P, K, TG, P]),
                                            ALU.mult).then_inc(m["gated"], 1)
                    dve.wait_ge(m["gated"], g + 1)
                    nc.vector.tensor_tensor(got[:, u, 0, :, :], got[:, u, 0, :, :], got[:, u, 1, :, :],
                                            ALU.add).then_inc(m["summed"], 1)
                else:
                    dve.sem_inc(m["summed"], 1)
                if more:
                    make_index(g + 2, u)
                dve.wait_ge(m["t_mm"], g + 3)
                at = cols(c.x, g * G)
                if gate is None:
                    nc.vector.tensor_tensor(at, at, c.banks[:, u, :], ALU.add).then_inc(m["x"], 1)
                else:
                    nc.vector.scalar_tensor_tensor(out=at, in0=c.banks[:, u, :], scalar=gate, in1=at, op0=ALU.mult,
                                                   op1=ALU.add).then_inc(m["x"], 1)

            make_index(0, 0)
            make_index(1, 1)
            with dve.Fori(0, NG // 2 - 1) as i:
                for u in range(2):
                    take(i, i * 2 + u, u, True)
            for u in range(2):
                take(NG // 2 - 1, NG - 2 + u, u, False)

        @block.tensor
        def _(pe):
            pe.sem_inc(m["t_mm"], 2)

            def body(i, g, u):
                pe.wait_ge(m["summed"], g + 1)
                pe.wait_ge(m["x"], g + 1)
                for t in range(TG):
                    last = nc.tensor.transpose(c.banks[:, u, t * P:(t + 1) * P], got[:, u, 0, t, :], c.ident[:, :])
                last.then_inc(m["t_mm"], 1)

            groups(pe, body)

def route_expert_choice(c, tag, layer, top2, keep, bias):
    nc = c.nc
    logits = c.banks[:, 0, :].rearrange("p (t e) -> p t e", e=E)
    flat = "p t e -> p (t e)"
    NQ = NT * E // P
    step, max_ready, exp_ready, score_ready, rows_ready, kept_ready, back_ready = (
        c.sem(tag + n) for n in ("_step", "_max", "_exp", "_score", "_rows", "_kept", "_back"))
    sum_in, sum_out = c.sem(tag + "_sum_in"), c.sem(tag + "_sum_out")
    rows = c.wb[:, 0:512].rearrange("p (q b s) -> p q b s", q=NQ, b=2)
    best = c.wb[:, 1024:1088]
    iota = c.wb[:, 1152:1216]
    first = c.wb[:, 1280:1344].bitcast(U32)
    hit = c.wb[:, 1408:1408 + 512].rearrange("p (q b s) -> p q b s", q=NQ, b=2)
    orig = c.wb[:, 2048:2048 + 512].rearrange("p (q b s) -> p q b s", q=NQ, b=2)
    iota_done = c.sem(tag + "_iota")
    with nc.Block() as block:
        @block.gpsimd
        def _(pool):
            nc.gpsimd.iota(c.iota_i[:, :], pattern=[[1, S]], base=0, channel_multiplier=0).then_inc(iota_done, 1)

        @block.vector
        def _(dve):
            link = chain_on(dve, step)
            v = c.t1
            if bias:
                link(nc.vector.tensor_tensor(v[:, :, :], logits, c.bias8[:, :].unsqueeze(1).broadcast_to([P, NT, E]),
                                             ALU.add))
            else:
                link(nc.vector.tensor_copy(v[:, :, :], logits))
            link(nc.vector.tensor_reduce(c.s1[:, :], v[:, :, :], axis=AX.X, op=ALU.max))
            nc.vector.tensor_tensor(v[:, :, :], v[:, :, :], c.s1[:, :].unsqueeze(2).broadcast_to([P, NT, E]),
                                    ALU.subtract).then_inc(max_ready, 1)
            dve.wait_ge(exp_ready, 1)
            link(nc.vector.tensor_reduce(c.s1[:, :], c.t2[:, :, :], axis=AX.X, op=ALU.add))
            link(nc.vector.reciprocal(c.s1[:, :], c.s1[:, :]))
            link(nc.vector.tensor_tensor(c.t3[:, :, :], c.t2[:, :, :],
                                         c.s1[:, :].unsqueeze(2).broadcast_to([P, NT, E]), ALU.mult))
            if top2:
                rank_experts(c, link, c.t3[:, :, :])
                link(nc.vector.tensor_scalar(c.t4[:, :, :], c.rank[:, :, :], 2.0, None, ALU.is_lt))
                link(nc.vector.tensor_tensor(c.t3[:, :, :], c.t3[:, :, :], c.t4[:, :, :], ALU.mult))
                nc.vector.tensor_reduce(c.s1[:, 0:E], c.t3[:, :, :].rearrange("p t e -> p e t"),
                                        axis=AX.X, op=ALU.add).then_inc(sum_in, 1)
                dve.wait_ge(sum_out, 1)
                link(nc.vector.tensor_scalar(c.s1[:, 8:16], c.banks[:, 1, 0:E], 1e-6, None, ALU.add))
                link(nc.vector.reciprocal(c.s1[:, 8:16], c.s1[:, 8:16]))
                link(nc.vector.tensor_tensor(c.t3[:, :, :], c.t3[:, :, :],
                                             c.s1[:, 8:16].unsqueeze(1).broadcast_to([P, NT, E]), ALU.mult))
                link(nc.vector.tensor_scalar(c.t3[:, :, :], c.t3[:, :, :], float(B), None, ALU.mult))
            dve.sem_inc(score_ready, 1)
            dve.wait_ge(rows_ready, 1)
            dve.wait_ge(iota_done, 1)
            link(nc.vector.tensor_copy(iota, c.iota_i[:, :]))
            link(nc.vector.tensor_copy(rows.rearrange("p q b s -> p (q b s)"), c.banks[:, 2, :]))
            link(nc.vector.tensor_copy(orig.rearrange("p q b s -> p (q b s)"), rows.rearrange("p q b s -> p (q b s)")))
            for r in range(keep // 8):
                for q in range(NQ):
                    for b in range(2):
                        k = (q * 2 + b) * 8
                        link(nc.vector.max(best[:, k:k + 8], rows[:, q, b, :]))
                        link(nc.vector.match_replace(rows[:, q, b, :], best[:, k:k + 8], rows[:, q, b, :], -1.0))
            link(nc.vector.tensor_scalar(hit, rows, 0.0, None, ALU.is_lt))
            if keep % 8:
                assert keep % 8 == 1
                for q in range(NQ):
                    for b in range(2):
                        k = (q * 2 + b) * 8
                        link(nc.vector.max(best[:, k:k + 8], rows[:, q, b, :]))
                        link(nc.vector.max_index(first[:, k:k + 8], best[:, k:k + 8], rows[:, q, b, :]))
                        link(nc.vector.tensor_copy(best[:, k:k + 8], first[:, k:k + 8]))
                        link(nc.vector.scalar_tensor_tensor(out=hit[:, q, b, :], in0=iota, scalar=best[:, k:k + 1],
                                                            in1=hit[:, q, b, :], op0=ALU.is_equal, op1=ALU.add))
            if not top2:
                link(nc.vector.tensor_tensor(hit, hit, orig, ALU.mult))
            dve.sem_inc(kept_ready, 1)
            dve.wait_ge(back_ready, 1)
            if top2:
                link(nc.vector.tensor_copy(c.gates[:, :, :].rearrange(flat), c.banks[:, 3, :]))
            else:
                link(nc.vector.tensor_scalar(c.gates[:, :, :].rearrange(flat), c.banks[:, 3, :],
                                             c.tanh_g[:, 4 + layer:5 + layer], None, ALU.mult))

        @block.scalar
        def _(act):
            act.wait_ge(max_ready, 1)
            nc.scalar.activation(c.t2[:, :, :], c.t1[:, :, :], ACT.Exp).then_inc(exp_ready, 1)

        @block.tensor
        def _(pe):
            if top2:
                pe.wait_ge(sum_in, 1)
                nc.tensor.matmul(c.banks[:, 1, 0:E], c.same_pos[:, :], c.s1[:, 0:E],
                                 start=True, stop=True).then_inc(sum_out, 1)
            pe.wait_ge(score_ready, 1)
            t3 = c.t3[:, :, :].rearrange(flat)
            for q in range(NQ):
                last = nc.tensor.transpose(c.banks[:, 2, q * P:(q + 1) * P], t3[:, q * P:(q + 1) * P], c.ident[:, :])
            last.then_inc(rows_ready, 1)
            pe.wait_ge(kept_ready, 1)
            hits = c.wb[:, 1408:1408 + 512]
            for q in range(NQ):
                last = nc.tensor.transpose(c.banks[:, 3, q * P:(q + 1) * P], hits[:, q * P:(q + 1) * P], c.ident[:, :])
            last.then_inc(back_ready, 1)


def expert_ffn(c, tag, NE, NF, gated, up, down, b1=None, b2=None, shared_gate=None, weight_loads=(), next_loads=()):
    nc = c.nc
    GB, UB, YB, BB = 0, 2, 4, 6
    hid = c.work[:, 0:8 * G].rearrange("p (k j n) -> p k j n", k=2, j=4)
    sil = c.work[:, 8 * G:10 * G].rearrange("p (k n) -> p k n", k=2)
    gbs = c.work[:, 10 * G:12 * G].rearrange("p (k n) -> p k n", k=2)
    tmp = c.work[:, 12 * G:14 * G].rearrange("p (k n) -> p k n", k=2)
    total = c.work[:, 14 * G:15 * G]
    gfix = c.gfix
    sum_used = c.sem(tag + "_sum_used")
    loaded = c.sem(tag + "_loaded")
    fetched = c.sem(tag + "_fetched")
    gfix_done = c.sem(tag + "_gfix_done")
    gb_done = c.sem(tag + "_gb_done")
    gbs_done = c.sem(tag + "_gbs_done")
    up_done = c.sem(tag + "_up_done")
    sil_done = c.sem(tag + "_sil_done")
    h_done = c.sem(tag + "_h_done")
    down_done = c.sem(tag + "_down_done")
    tmp_done = c.sem(tag + "_tmp_done")
    x_done = c.sem(tag + "_x_done")
    with nc.Block() as block:
        @block.sync
        def _(sp):
            for dst, src in weight_loads:
                sp.dma_start(dst, src).then_inc(loaded, 16)
            for dst, src in next_loads:
                sp.dma_start(dst, src).then_inc(fetched, 16)
            if weight_loads:
                sp.wait_ge(loaded, 16 * len(weight_loads))
            if next_loads:
                sp.wait_ge(fetched, 16 * len(next_loads))

        @block.tensor
        def _(pe):
            pe.sem_inc(down_done, 2)
            pe.sem_inc(gb_done, 1)
            if weight_loads:
                pe.wait_ge(loaded, 16 * len(weight_loads))

            def down_of(g, e):
                n = g * NE + e
                pe.wait_ge(h_done, n * NF + (NF + 2))
                pe.wait_ge(tmp_done, n + 1)
                for j in range(NF):
                    last = nc.tensor.matmul(c.banks[:, YB + e % 2, :], down(e, j), hid[:, e % 2, j, :],
                                            start=(j == 0), stop=(j == NF - 1))
                last.then_inc(down_done, 1)

            with pe.Fori(0, NG) as g:
                pe.wait_ge(gfix_done, g + 1)
                for e in range(NE):
                    if e < E:
                        pe.wait_ge(gbs_done, g * E + (e + 1))
                        for k in range(TG):
                            last = nc.tensor.matmul(c.banks[:, BB + e % 2, k * P:(k + 1) * P],
                                                    gfix[:, k, e:e + 1].broadcast_to([P, P]), c.ident[:, :],
                                                    start=True, stop=True)
                        last.then_inc(gb_done, 1)
                    for j in range(NF):
                        n = (g * NE + e) * NF + j
                        pe.wait_ge(h_done, n + 1)
                        last = nc.tensor.matmul(c.banks[:, GB + j % 2, :], up(e, j, 0), cols(c.xn, g * G),
                                                start=True, stop=True)
                        if gated:
                            last = nc.tensor.matmul(c.banks[:, UB + j % 2, :], up(e, j, 1), cols(c.xn, g * G),
                                                    start=True, stop=True)
                        last.then_inc(up_done, 1)
                        if j == 0 and e > 0:
                            down_of(g, e - 1)
                down_of(g, NE - 1)

        @block.scalar
        def _(act):
            act.sem_inc(gbs_done, 2)
            if not gated:
                act.sem_inc(h_done, 2)
                if weight_loads:
                    act.wait_ge(loaded, 16 * len(weight_loads))
            with act.Fori(0, NG) as g:
                for e in range(NE):
                    if e < E:
                        act.wait_ge(gb_done, g * E + (e + 2))
                        act.wait_ge(tmp_done, g * NE + (e + 1))
                        nc.scalar.activation(gbs[:, e % 2, :], c.banks[:, BB + e % 2, :], ACT.Copy).then_inc(gbs_done, 1)
                    for j in range(NF):
                        n = (g * NE + e) * NF + j
                        act.wait_ge(up_done, n + 1)
                        if gated:
                            act.wait_ge(h_done, n + 1)
                            nc.scalar.activation(sil[:, j % 2, :], c.banks[:, GB + j % 2, :], ACT.Silu).then_inc(sil_done, 1)
                        else:
                            act.wait_ge(down_done, g * NE + (e + 1))
                            nc.scalar.activation(hid[:, e % 2, j, :], c.banks[:, GB + j % 2, :], ACT.Gelu,
                                                 bias=b1(e, j)).then_inc(h_done, 1)

        @block.vector
        def _(dve):
            dve.sem_inc(tmp_done, 2)
            dve.sem_inc(sum_used, 1)
            if gated:
                dve.sem_inc(h_done, 2)
            if weight_loads:
                dve.wait_ge(loaded, 16 * len(weight_loads))

            def tmp_of(g, e):
                n = g * NE + e
                dve.wait_ge(down_done, n + 3)
                dve.wait_ge(x_done, n + 1)
                y = c.banks[:, YB + e % 2, :]
                if e == E:
                    nc.vector.tensor_scalar(tmp[:, e % 2, :], y, shared_gate, None, ALU.mult).then_inc(tmp_done, 1)
                    return
                dve.wait_ge(gbs_done, g * E + (e + 3))
                if b2 is None:
                    nc.vector.tensor_tensor(tmp[:, e % 2, :], y, gbs[:, e % 2, :], ALU.mult).then_inc(tmp_done, 1)
                else:
                    nc.vector.scalar_tensor_tensor(out=tmp[:, e % 2, :], in0=y, scalar=b2(e), in1=gbs[:, e % 2, :],
                                                   op0=ALU.add, op1=ALU.mult).then_inc(tmp_done, 1)

            with dve.Fori(0, NG) as g:
                for e in range(NE):
                    if gated:
                        for j in range(NF):
                            n = (g * NE + e) * NF + j
                            dve.wait_ge(sil_done, n + 1)
                            dve.wait_ge(down_done, g * NE + (e + 1))
                            nc.vector.tensor_tensor(hid[:, e % 2, j, :], sil[:, j % 2, :], c.banks[:, UB + j % 2, :],
                                                    ALU.mult).then_inc(h_done, 1)
                            if j == 1 and e > 0:
                                tmp_of(g, e - 1)
                    elif e > 0:
                        tmp_of(g, e - 1)
                tmp_of(g, NE - 1)
                dve.wait_ge(x_done, g * NE + (NE + 2))
                nc.vector.tensor_tensor(cols(c.x, g * G), cols(c.x, g * G), total, ALU.add).then_inc(sum_used, 1)

        @block.gpsimd
        def _(pool):
            pool.sem_inc(x_done, 2)
            with pool.Fori(0, NG) as g:
                pool.wait_ge(gb_done, g * E + 1)
                nc.gpsimd.tensor_copy(gfix[:, :, :].rearrange("p k e -> p (k e)"),
                                      c.gates[:, :, :].rearrange("p t e -> p (t e)")[:, bass.ds(g * (TG * E), TG * E)]
                                      ).then_inc(gfix_done, 1)
                for e in range(1, NE):
                    pool.wait_ge(tmp_done, g * NE + (e + 3))
                    if e == 1:
                        pool.wait_ge(sum_used, g + 1)
                        nc.gpsimd.tensor_tensor(total, tmp[:, 0, :], tmp[:, 1, :], ALU.add).then_inc(x_done, 2)
                    else:
                        pool.wait_ge(x_done, g * NE + (e + 2))
                        nc.gpsimd.tensor_tensor(total, total, tmp[:, e % 2, :], ALU.add).then_inc(x_done, 1)


def windowed_product(c, tag, ctxT):
    nc = c.nc
    cb = c.work[:, 0:2 * G].rearrange("p (k n) -> p k n", k=2)
    sq = c.work[:, 2 * G:3 * G]
    y = c.work[:, 3 * G:4 * G]
    total = c.work[:, 4 * G:4 * G + 16]
    ctx_in = [c.sem(tag + f"_ctx_in{k}") for k in range(2)]
    sq_done = c.sem(tag + "_sq_done")
    sum_done = c.sem(tag + "_sum_done")
    y_done = c.sem(tag + "_y_done")
    x_done = c.sem(tag + "_x_done")
    with nc.Block() as block:
        @block.sync
        def _(sp):
            with sp.Fori(0, NG // 2) as i:
                for k in range(2):
                    sp.wait_ge(sq_done, i * 2 + 1)
                    sp.dma_start(cb[:, k, :], cols(ctxT, i * (2 * G) + k * G)).then_inc(ctx_in[k], 16)

        @block.vector
        def _(dve):
            dve.sem_inc(sq_done, 1)
            with dve.Fori(0, NG // 2) as i:
                for k in range(2):
                    dve.wait_ge(ctx_in[k], i * 16 + 16)
                    nc.vector.scalar_tensor_tensor(out=sq, in0=cb[:, k, :], scalar=0.0, in1=cb[:, k, :],
                                                   op0=ALU.max, op1=ALU.mult).then_inc(sq_done, 1)
                    dve.wait_ge(sq_done, i * 2 + (k + 2))
                    nc.vector.tensor_reduce(total[:, 0:BG], sq.rearrange("p (b s) -> p b s", s=S), axis=AX.X,
                                            op=ALU.add).then_inc(sum_done, 1)
                    dve.wait_ge(sum_done, i * 2 + (k + 1))
                    at = cols(c.xn, i * (2 * G) + k * G)
                    nc.vector.scalar_tensor_tensor(out=y.rearrange("p (b s) -> p b s", s=S),
                                                   in0=at.rearrange("p (b s) -> p b s", s=S), scalar=0.0,
                                                   in1=total[:, 0:BG].unsqueeze(2).broadcast_to([P, BG, S]),
                                                   op0=ALU.max, op1=ALU.mult).then_inc(y_done, 1)
                    dve.wait_ge(y_done, i * 2 + (k + 1))
                    xg = cols(c.x, i * (2 * G) + k * G)
                    nc.vector.scalar_tensor_tensor(out=xg, in0=y, scalar=c.tanh_g[:, 1:2], in1=xg,
                                                   op0=ALU.mult, op1=ALU.add).then_inc(x_done, 1)


def mask_rows(c, tag, mask, kind, scale):
    nc = c.nc
    raw = c.wb[:, 0:64].bitcast(I32) if kind == "zero_is_off" else c.wb[:, 0:64]
    val, rest = c.wb[:, 64:128], c.wb[:, 128:192]
    part = [c.wb[:, 192 + 32 * k:224 + 32 * k].bitcast(BF16) for k in range(3)]
    got, step, moved = c.sem(tag + "_mask_in"), c.sem(tag + "_mask_step"), c.sem(tag + "_mask_moved")
    made = c.sem(tag + "_mask_made")
    with nc.Block() as block:
        @block.sync
        def _(sp):
            sp.dma_start(raw, mask).then_inc(got, 16)
            sp.wait_ge(made, 1)
            for k in range(3):
                sp.dma_start(c.mrow[k:k + 1, :], part[k]).then_inc(moved, 16)
            sp.wait_ge(moved, 48)

        @block.vector
        def _(dve):
            link = chain_on(dve, step)
            dve.wait_ge(got, 16)
            if kind == "zero_is_off":
                link(nc.vector.tensor_scalar(val, raw, 0.0, -1e20 * scale, ALU.is_equal, ALU.mult))
            else:
                link(nc.vector.tensor_scalar(val, raw, -1e9, None, ALU.mult))
            link(nc.vector.tensor_copy(part[0], val))
            link(nc.vector.tensor_tensor(rest, val, part[0], ALU.subtract))
            link(nc.vector.tensor_copy(part[1], rest))
            link(nc.vector.tensor_tensor(val, rest, part[1], ALU.subtract))
            link(nc.vector.tensor_copy(part[2], val))
            dve.sem_inc(made, 1)


def attention(c, tag, ctxT, scale, gate, bq=None, bk=None, bv=None, bo=None):
    nc = c.nc
    wq, wk, wv, wo = (c.attn_w[:, k, :] for k in range(4))
    cbf = c.wb[:, 0:2048].rearrange("p (u n) -> p u n", u=2)
    cb = c.wb[:, 0:2048].rearrange("p (u b two s) -> p u b two s", u=2, b=BG, two=2)
    kb = c.wb[:, 2048:6144].rearrange("p (u j n) -> p u j n", u=2, j=4)
    qs = c.wb[:, 6144:7168].rearrange("p (u n) -> p u n", u=2)
    ot = c.wb[:, 7168:8192].rearrange("p (u n) -> p u n", u=2)
    pr = c.work[:, 0:2048].rearrange("p (u n) -> p u n", u=2)
    pt = c.work[:, 2048:4096].rearrange("p (u n) -> p u n", u=2)
    vb = c.work[:, 4096:4096 + 2 * 288].rearrange("p (u a n) -> p u a n", u=2, a=16)
    on = c.work[:, 4800:5056].rearrange("p (u n) -> p u n", u=2)
    rd = c.work[:, 5056:5072]
    nm = c.work[:, 5072:5104].rearrange("p (u h) -> p u h", u=2)
    add = c.work[:, 5120:5632]
    VBANK, OBANK = c.banks[:, 6, :], c.banks[:, 7, :]

    def scores(u):
        return c.banks[:, 2 * u:2 * u + 2, :]

    ctx_in = [c.sem(f"{tag}_ctx_in{p}") for p in range(2)]
    names = ("prep", "mask_fix", "q_mm", "k_mm", "q_done", "k_done", "s_order", "s_mm", "nm_done", "sub_done", "v_mm",
             "v_used", "p_done", "t_mm", "t_used", "av_mm", "rd_done", "on_done", "ot_mm", "ot_done", "wo_mm", "add_done",
             "x_done")
    m = {n: c.sem(f"{tag}_{n}") for n in names}
    PAIRS = NG // 2

    def slots(engine, slot):
        with engine.Fori(0, PAIRS - 1) as i:
            for p in range(2):
                for k in range(TG):
                    slot(i * 2 + p, p, k, True, True)
        for p in range(2):
            for k in range(TG):
                slot(NG - 2 + p, p, k, p == 0, p == 0 or k < 2)

    with nc.Block() as block:
        @block.sync
        def _(sp):
            def load(g, p):
                for two in range(2):
                    sp.dma_start(cb[:, p, :, two, :], cols(ctxT, g * G).rearrange("p (b s) -> p b s", s=S)).then_inc(
                        ctx_in[p], 16)

            load(0, 0)
            load(1, 1)
            with sp.Fori(1, PAIRS) as i:
                for p in range(2):
                    sp.wait_ge(m["v_mm"], i * 8 + (4 * p - 4) + 1)
                    load(i * 2 + p, p)

        @block.gpsimd
        def _(pool):
            start_at_1(pool, m, "mask_fix")
            def fix(g, p):
                nc.gpsimd.tensor_copy(c.mrow_fix[0:3, p, :], c.mrow[0:3, bass.ds(g * G, G)]).then_inc(m["mask_fix"], 1)

            fix(0, 0)
            fix(1, 1)
            with pool.Fori(1, PAIRS) as i:
                for p in range(2):
                    pool.wait_ge(m["s_mm"], i * 8 + (4 * p - 4) + 1)
                    fix(i * 2 + p, p)

        @block.tensor
        def _(pe):
            start_at_1(pe, m, "k_mm", "q_mm", "s_order", "s_mm", "v_mm", "ot_mm", "wo_mm", "t_mm", "av_mm")
            pe.wait_ge(m["prep"], 2)

            def make_keys(g, p, loads):
                pe.wait_ge(ctx_in[p], loads)
                nc.tensor.matmul(VBANK.rearrange("p (b s) -> p b s", s=S), wk, cb[:, p, :, 0, :],
                                 start=True, stop=True).then_inc(m["k_mm"], 1)

            def make_queries(g):
                nc.tensor.matmul(VBANK, wq, cols(c.xn, g * G), start=True, stop=True).then_inc(m["q_mm"], 1)

            def make_scores(g, p, k):
                u, n, tok = k % 2, g * TG + k, k * P
                if k == 0:
                    pe.wait_ge(m["k_done"], g * 4 + 4 + 1)
                    pe.wait_ge(m["q_done"], g + 2)
                    pe.wait_ge(m["mask_fix"], g + 2)
                pe.wait_ge(m["sub_done"], n + 2)
                for w in range(2):
                    for b in range(2):
                        last = nc.tensor.matmul(
                            scores(u)[S * b:S * b + S, w, :].rearrange("p (h k) -> p h k", h=8), c.ones[0:3, 0:S],
                            c.mrow_fix[0:3, p, tok + S * b:tok + S * b + S].unsqueeze(1).broadcast_to([3, 8, S]),
                            start=True, stop=False)
                last.then_inc(m["s_order"], 1)
                pe.wait_ge(m["s_order"], n * 2 + 2)
                for w in range(2):
                    for r in (w, 2 + w):
                        for b in range(2):
                            rows = slice(32 * r, 32 * r + 32)
                            last = nc.tensor.matmul(
                                scores(u)[S * b:S * b + S, r // 2, w * 256:w * 256 + 256].rearrange(
                                    "p (j k) -> p j k", j=4),
                                qs[rows, p, tok + S * b:tok + S * b + S], kb[rows, p, :, tok + S * b:tok + S * b + S],
                                start=False, stop=(w == 1))
                    if w == 0:
                        last.then_inc(m["s_order"], 1)
                        pe.wait_ge(m["s_order"], n * 2 + 2 + 1)
                last.then_inc(m["s_mm"], 1)

            def make_values(p, k):
                for b in range(2):
                    last = nc.tensor.matmul(VBANK[:, b * P:(b + 1) * P], cbf[:, p, (2 * k + b) * P:(2 * k + b + 1) * P],
                                            wv, start=True, stop=True)
                last.then_inc(m["v_mm"], 1)

            def transpose_out(n, u):
                pe.wait_ge(m["on_done"], n + 2)
                nc.tensor.transpose(OBANK[:, 384:512], on[:, u, :], c.ident[:, :]).then_inc(m["ot_mm"], 1)

            def project_out(p):
                nc.tensor.matmul(VBANK, wo, ot[:, p, :], start=True, stop=True).then_inc(m["wo_mm"], 1)

            def slot(g, p, k, more, ahead):
                u, n = k % 2, g * TG + k
                pe.wait_ge(m["p_done"], n + 2)
                for w in range(2):
                    pe.wait_ge(m["t_used"], n * 2 + (w + 1) + 1)
                    for i in range(4):
                        last = nc.tensor.transpose(c.banks[:, 4 + w, i * P:(i + 1) * P],
                                                   pr[:, u, (4 * w + i) * P:(4 * w + i + 1) * P], c.ident[:, :])
                    last.then_inc(m["t_mm"], 1)
                transpose_out(n, 1 - u)
                if k == 0 and more:
                    pe.wait_ge(m["v_used"], n + 2)
                    make_keys(g + 1, 1 - p, g * 16 + (48 if p else 32))
                if k == 1 and more:
                    pe.wait_ge(m["v_used"], n + 2)
                    make_queries(g + 1)
                if k == 2:
                    pe.wait_ge(m["v_used"], n + 2)
                    pe.wait_ge(m["ot_done"], g * TG + 2)
                    project_out(1 - p)
                if ahead:
                    make_scores(g + (k + 2) // TG, (p + (k + 2) // TG) % 2, (k + 2) % TG)
                if more or k + 1 < TG:
                    if k == 0 and more:
                        pe.wait_ge(m["k_done"], g * 4 + 8 + 1)
                    elif k == 1 and more:
                        pe.wait_ge(m["q_done"], g + 2 + 1)
                    elif k == 2:
                        pe.wait_ge(m["add_done"], g + 2)
                    else:
                        pe.wait_ge(m["v_used"], n + 2)
                    make_values((p + (k + 1) // TG) % 2, (k + 1) % TG)
                pe.wait_ge(m["ot_done"], n + 2)
                pe.wait_ge(m["v_used"], n + 2)
                for w in range(2):
                    pe.wait_ge(m["t_used"], n * 2 + (w + 3) + 1)
                    for i in range(4 * w, 4 * w + 4):
                        for b in range(2):
                            last = nc.tensor.matmul(OBANK[S * b:S * b + S, i * 18:i * 18 + 18],
                                                    pt[:, u, i * P + S * b:i * P + S * b + S], vb[:, u, b * 8 + i, :],
                                                    start=True, stop=True)
                last.then_inc(m["av_mm"], 1)

            make_keys(0, 0, 32)
            pe.wait_ge(m["k_done"], 5)
            make_queries(0)
            pe.wait_ge(m["q_done"], 2)
            make_values(0, 0)
            make_scores(0, 0, 0)
            make_scores(0, 0, 1)
            slots(pe, slot)
            transpose_out(NT, 1)
            pe.wait_ge(m["ot_done"], NT + 2)
            pe.wait_ge(m["v_used"], NT + 1)
            project_out(1)

        @block.vector
        def _(dve):
            start_at_1(dve, m, "prep", "on_done", "sub_done", "k_done", "nm_done", "v_used", "rd_done", "x_done")
            nc.vector.tensor_copy(vb[:, 0, :, 16:18], c.half[:, :].unsqueeze(1).broadcast_to([P, 16, 2]))
            nc.vector.memset(on[:, 1, :], 0.0)
            nc.vector.memset(ot[:, 1, :], 0.0)
            nc.vector.tensor_copy(vb[:, 1, :, 16:18], c.half[:, :].unsqueeze(1).broadcast_to([P, 16, 2])).then_inc(
                m["prep"], 1)
            dve.wait_ge(m["prep"], 2)
            dve.sem_inc(m["on_done"], 1)
            dve.sem_inc(m["sub_done"], 2)

            def expand_keys(g, p):
                dve.wait_ge(m["k_mm"], g + 2)
                for j in range(4):
                    nc.vector.tensor_scalar(kb[:, p, j, :], VBANK, bk, c.quad[:, j:j + 1], ALU.add,
                                            ALU.mult).then_inc(m["k_done"], 1)

            def soften(n, u):
                dve.wait_ge(m["s_mm"], n + 2)
                s3 = scores(u).rearrange("p w (h k) -> p (w h) k", k=S)
                nc.vector.tensor_reduce(nm[:, u, :], s3, axis=AX.X, op=ALU.max).then_inc(m["nm_done"], 1)
                dve.wait_ge(m["nm_done"], n + 2)
                nc.vector.tensor_tensor(pr[:, u, :].rearrange("p (h k) -> p h k", k=S), s3,
                                        nm[:, u, :].unsqueeze(2).broadcast_to([P, H, S]),
                                        ALU.subtract).then_inc(m["sub_done"], 1)

            def keep_values(n, u):
                dve.wait_ge(m["v_mm"], n + 2)
                nc.vector.tensor_tensor(vb[:, u, :, 0:16], VBANK[:, 0:256].rearrange("p (a n) -> p a n", n=16),
                                        c.half16[:, :, :].rearrange("p j d -> p (j d)").unsqueeze(1).broadcast_to(
                                            [P, 16, 16]), ALU.mult).then_inc(m["v_used"], 1)

            def normalise(n, u):
                dve.wait_ge(m["av_mm"], n + 2)
                o = OBANK[:, 0:144].rearrange("p (i n) -> p i n", n=18)
                dve.wait_ge(m["on_done"], n + 2)
                nc.vector.reciprocal(rd.rearrange("p (i j) -> p i j", j=2), o[:, :, 16:18]).then_inc(m["rd_done"], 1)
                dve.wait_ge(m["rd_done"], n + 2)
                nc.vector.tensor_tensor(on[:, u, :].rearrange("p (i j d) -> p i j d", i=8, j=2),
                                        o[:, :, 0:16].rearrange("p i (j d) -> p i j d", j=2),
                                        rd.rearrange("p (i j) -> p i j", j=2).unsqueeze(3).broadcast_to([P, 8, 2, HD]),
                                        ALU.mult).then_inc(m["on_done"], 1)

            def slot(g, p, k, more, ahead):
                u, n = k % 2, g * TG + k
                if k == 0 and more:
                    expand_keys(g + 1, 1 - p)
                if ahead:
                    dve.wait_ge(m["t_mm"], n * 2 + 2 + 1)
                    soften(n + 2, u)
                if more or k + 1 < TG:
                    keep_values(n + 1, 1 - u)
                normalise(n, u)
                if k == 2:
                    add_to_x(g - 1, g)

            def add_to_x(g, count):
                dve.wait_ge(m["add_done"], count + 2)
                at = cols(c.xpad, (g + 1) * G)
                nc.vector.tensor_tensor(at, at, add, ALU.add).then_inc(m["x_done"], 1)

            expand_keys(0, 0)
            keep_values(0, 0)
            soften(0, 0)
            soften(1, 1)
            slots(dve, slot)
            add_to_x(NG - 1, NG)

        @block.scalar
        def _(act):
            start_at_1(act, m, "t_used", "p_done", "q_done", "ot_done", "add_done")
            act.sem_inc(m["t_used"], 2)

            def exps(n, u):
                act.wait_ge(m["sub_done"], n + 3 + 1)
                nc.scalar.activation(pr[:, u, :], pr[:, u, :], ACT.Exp).then_inc(m["p_done"], 1)

            def queries(g, p):
                act.wait_ge(m["q_mm"], g + 2)
                nc.scalar.activation(qs[:, p, :], VBANK, ACT.Identity, bias=bq, scale=scale).then_inc(m["q_done"], 1)

            def copies(n, u):
                for w in range(2):
                    act.wait_ge(m["t_mm"], n * 2 + (w + 1) + 1)
                    nc.scalar.activation(pt[:, u, w * G:(w + 1) * G], c.banks[:, 4 + w, :], ACT.Copy).then_inc(
                        m["t_used"], 1)

            def copy_out(n, p, k):
                act.wait_ge(m["ot_mm"], n + 2)
                nc.scalar.activation(ot[:, p, k * P:(k + 1) * P], OBANK[:, 384:512], ACT.Identity, bias=bv).then_inc(
                    m["ot_done"], 1)

            def evacuate_out(g):
                act.wait_ge(m["wo_mm"], g + 2)
                act.wait_ge(m["x_done"], g + 1)
                nc.scalar.activation(add, VBANK, ACT.Identity, bias=bo, scale=gate).then_inc(m["add_done"], 1)

            def slot(g, p, k, more, ahead):
                u, n = k % 2, g * TG + k
                copies(n, u)
                copy_out(n, (p + 1) % 2 if k == 0 else p, (k - 1) % TG)
                if k == 1 and more:
                    queries(g + 1, 1 - p)
                if k == 2:
                    evacuate_out(g)
                if ahead:
                    exps(n + 2, u)

            act.wait_ge(m["prep"], 2)
            queries(0, 0)
            exps(0, 0)
            exps(1, 1)
            slots(act, slot)
            copy_out(NT, 1, TG - 1)
            evacuate_out(NG)


def attention_weights(c, tag, A, layer, block_diagonal, biases):
    nc = c.nc
    got, cleared, step = c.sem(tag + "_w_in"), c.sem(tag + "_w_cleared"), c.sem(tag + "_w_step")
    scale = HD ** -0.5 if not block_diagonal else P ** -0.5
    col = c.attn_b
    with nc.Block() as block:
        @block.gpsimd
        def _(pool):
            nc.gpsimd.memset(c.attn_w[:, :, :], 0.0).then_inc(cleared, 1)
            nc.gpsimd.memset(col[:, :], 0.0).then_inc(cleared, 1)

        @block.sync
        def _(sp):
            n = 0
            sp.wait_ge(cleared, 2)
            for k, w in enumerate(("Wq", "Wk", "Wv", "Wo")):
                src = A[f"L{layer}_xattn_{w}T"]
                if block_diagonal and w != "Wo":
                    for h in range(H):
                        sp.dma_start(c.attn_w[h * HD:(h + 1) * HD, k, h * HD:(h + 1) * HD], src).then_inc(got, 16)
                        n += 1
                else:
                    sp.dma_start(c.attn_w[:, k, :], src).then_inc(got, 16)
                    n += 1
            for k, b in enumerate(biases):
                if b is not None:
                    sp.dma_start(col[:, k:k + 1], A[b].unsqueeze(1)).then_inc(got, 16)
                    n += 1
            sp.wait_ge(got, 16 * n)
            sp.sem_inc(step, 1)

        @block.vector
        def _(dve):
            dve.wait_ge(step, 1)
            nc.vector.tensor_scalar(col[:, 0:1], col[:, 0:1], scale, None, ALU.mult)
            nc.vector.tensor_tensor(col[:, 3:4], col[:, 3:4], c.tanh_g[:, layer:layer + 1], ALU.mult).then_inc(step, 1)
            dve.wait_ge(step, 2)


def two_way_attention(c, tag, A, ctxT, ctx_q):
    nc = c.nc
    wl = c.attn_w
    col = c.cols16
    cb = c.work[:, 0:512]
    ctq = c.work[0:S, 512:1536].rearrange("q (b d) -> q b d", b=BG)
    cc = c.work[:, 1536:2048]
    xg = c.work[:, 2048:2560]
    a = c.work[:, 2560:2816].rearrange("p (k q) -> p k q", q=S)
    at = c.work[0:S, 3072:3584]
    ml = c.work[:, 3584:3588]
    cw = c.work[:, 3588:3592]
    sm = c.work[:, 3592:3596]
    lg = c.work[:, 3600:3664]
    lt = c.work[0:NT, 3712:3840].rearrange("t (b s) -> t b s", b=2)
    lm = c.work[0:NT, 3840:3842]
    wtok = c.work[:, 3904:3968]
    c2q = c.wb
    names = ("w_in", "b_done", "ctx_in", "ctq_in", "cc_done", "xg_done", "s_mm", "m_done", "l_done", "a_sub", "a_exp", "r_done",
             "a_done", "at_mm", "at_done", "c2q_mm", "c2q_done", "rr_done", "s1_done")
    m = {n: c.sem(f"{tag}_{n}") for n in names}
    SB, TB, CB = c.banks[:, 0, :], c.banks[0:S, 1, :], c.banks[:, 2, :]
    with nc.Block() as block:
        @block.sync
        def _(sp):
            sp.dma_start(wl[:, :, :].rearrange("p k n -> p (k n)"), A["L2_xattn_W_lT"]).then_inc(m["w_in"], 16)
            for k, n in enumerate(("L2_xattn_w_cq", "L2_xattn_w_q", "L2_xattn_w_c", "L2_xattn_b_l")):
                sp.dma_start(col[:, k:k + 1], A[n].unsqueeze(1)).then_inc(m["w_in"], 16)
            for k, n in enumerate(("L2_xattn_b_cq", "L2_xattn_b_c", "L2_xattn_b_q")):
                sp.dma_start(col[:, 4 + k:5 + k], A[n].partition_broadcast(P)).then_inc(m["w_in"], 16)
            with sp.Fori(0, NG) as g:
                sp.wait_ge(m["c2q_mm"], g + 1)
                sp.dma_start(cb, cols(ctxT, g * G)).then_inc(m["ctx_in"], 16)
                sp.dma_start(ctq.rearrange("q b d -> q (b d)"), cols(ctx_q, g * (BG * P), BG * P)).then_inc(
                    m["ctq_in"], 16)

        @block.tensor
        def _(pe):
            start_at_1(pe, m, "s_mm", "at_mm", "c2q_mm")
            pe.wait_ge(m["w_in"], 128)
            with pe.Fori(0, NG) as g:
                pe.wait_ge(m["ctx_in"], g * 16 + 16)
                pe.wait_ge(m["cc_done"], g + 2)
                pe.wait_ge(m["xg_done"], g + 2)
                pe.wait_ge(m["a_sub"], g + 1)
                pe.wait_ge(m["l_done"], g + 1)
                for k in range(TG):
                    for b in range(2):
                        t0 = k * P + b * S
                        nc.tensor.matmul(SB[b * S:(b + 1) * S, k * S:(k + 1) * S], cc[:, t0:t0 + S], cb[:, t0:t0 + S],
                                         start=True, stop=True)
                    last = nc.tensor.matmul(SB[:, 256 + k:257 + k], xg[:, k * P:(k + 1) * P], col[:, 2:3],
                                            start=True, stop=True)
                last.then_inc(m["s_mm"], 1)
                pe.wait_ge(m["a_done"], g + 2)
                for k in range(TG):
                    last = nc.tensor.matmul(TB[:, k * P:(k + 1) * P], a[:, k, :], c.ident[:, :], start=True, stop=True)
                last.then_inc(m["at_mm"], 1)
                pe.wait_ge(m["at_done"], g + 2)
                pe.wait_ge(m["ctq_in"], g * 16 + 16)
                pe.wait_ge(m["c2q_done"], g + 1)
                for b in range(BG):
                    last = nc.tensor.matmul(CB[:, b * S:(b + 1) * S], ctq[:, b, :], at[:, b * S:(b + 1) * S],
                                            start=True, stop=True)
                last.then_inc(m["c2q_mm"], 1)

        @block.vector
        def _(dve):
            start_at_1(dve, m, "b_done", "cc_done", "m_done", "l_done", "a_sub", "s1_done", "r_done", "a_done")
            dve.wait_ge(m["w_in"], 128)
            nc.vector.tensor_scalar(col[:, 4:5], col[:, 4:5], col[:, 5:6], col[:, 6:7], ALU.add, ALU.add)
            nc.vector.tensor_tensor(col[:, 7:8], col[:, 3:4], c.tanh_g[:, 2:3], ALU.mult).then_inc(m["b_done"], 1)
            dve.wait_ge(m["b_done"], 2)
            s3 = SB[:, 0:256].rearrange("p (k q) -> p k q", q=S)
            with dve.Fori(0, NG) as g:
                dve.wait_ge(m["s_mm"], g + 1)
                nc.vector.tensor_scalar(cc, cols(c.xn, g * G), col[:, 0:1], col[:, 1:2], ALU.mult,
                                        ALU.add).then_inc(m["cc_done"], 1)
                dve.wait_ge(m["s_mm"], g + 2)
                nc.vector.tensor_reduce(ml, s3, axis=AX.X, op=ALU.max).then_inc(m["m_done"], 1)
                dve.wait_ge(m["m_done"], g + 2)
                nc.vector.scalar_tensor_tensor(out=lg[:, bass.ds(g * TG, TG)], in0=SB[:, 256:260], scalar=col[:, 4:5],
                                               in1=ml, op0=ALU.add, op1=ALU.add).then_inc(m["l_done"], 1)
                dve.wait_ge(m["at_mm"], g + 1)
                nc.vector.tensor_tensor(a, s3, ml.unsqueeze(2).broadcast_to([P, TG, S]),
                                        ALU.subtract).then_inc(m["a_sub"], 1)
                dve.wait_ge(m["a_exp"], g + 2)
                nc.vector.tensor_reduce(sm, a, axis=AX.X, op=ALU.add).then_inc(m["s1_done"], 1)
                dve.wait_ge(m["s1_done"], g + 2)
                nc.vector.reciprocal(sm, sm).then_inc(m["r_done"], 1)
                dve.wait_ge(m["r_done"], g + 2)
                nc.vector.tensor_tensor(a, a, sm.unsqueeze(2).broadcast_to([P, TG, S]), ALU.mult).then_inc(
                    m["a_done"], 1)

        @block.scalar
        def _(act):
            start_at_1(act, m, "xg_done", "a_exp", "at_done", "c2q_done")
            with act.Fori(0, NG) as g:
                act.wait_ge(m["s_mm"], g + 1)
                nc.scalar.activation(xg, cols(c.xn, g * G), ACT.Copy).then_inc(m["xg_done"], 1)
                act.wait_ge(m["a_sub"], g + 2)
                nc.scalar.activation(a, a, ACT.Exp).then_inc(m["a_exp"], 1)
                act.wait_ge(m["at_mm"], g + 2)
                act.wait_ge(m["c2q_mm"], g + 1)
                nc.scalar.activation(at, TB, ACT.Copy).then_inc(m["at_done"], 1)
                act.wait_ge(m["c2q_mm"], g + 2)
                nc.scalar.activation(cols(c2q, g * G), CB, ACT.Copy).then_inc(m["c2q_done"], 1)

    step, lt_mm, lt_sub, lt_exp, lt_done, back = (c.sem(tag + n) for n in ("_st", "_ltm", "_lts", "_lte", "_ltd", "_bk"))
    with nc.Block() as block:
        @block.tensor
        def _(pe):
            nc.tensor.transpose(c.banks[0:NT, 3, 0:P], lg, c.ident[:, :]).then_inc(lt_mm, 1)
            pe.wait_ge(lt_done, 1)
            nc.tensor.transpose(c.banks[:, 4, 0:NT], lt.rearrange("t b s -> t (b s)"),
                                c.ident[0:NT, 0:NT]).then_inc(back, 1)

        @block.scalar
        def _(act):
            act.wait_ge(lt_sub, 1)
            nc.scalar.activation(lt, lt, ACT.Exp).then_inc(lt_exp, 1)

        @block.vector
        def _(dve):
            link = chain_on(dve, step)
            dve.wait_ge(lt_mm, 1)
            raw = c.banks[0:NT, 3, 0:P].rearrange("t (b s) -> t b s", b=2)
            link(nc.vector.tensor_reduce(lm, raw, axis=AX.X, op=ALU.max))
            nc.vector.tensor_tensor(lt, raw, lm.unsqueeze(2).broadcast_to([NT, 2, S]), ALU.subtract).then_inc(lt_sub, 1)
            dve.wait_ge(lt_exp, 1)
            link(nc.vector.tensor_reduce(lm, lt, axis=AX.X, op=ALU.add))
            link(nc.vector.reciprocal(lm, lm))
            nc.vector.tensor_tensor(lt, lt, lm.unsqueeze(2).broadcast_to([NT, 2, S]), ALU.mult).then_inc(lt_done, 1)
            dve.wait_ge(back, 1)
            link(nc.vector.tensor_copy(wtok, c.banks[:, 4, 0:NT]))

    wfix = c.work[:, 4000:4004]
    prod = c.work[:, 4096:4608]
    x3 = c.work[:, 4608:5120]
    x4 = c.work[:, 5120:5632]
    add = c.work[:, 5632:6144]
    qc = c.work[:, 6144:6144 + BG]
    m = {n: c.sem(f"{tag}b_{n}") for n in ("wfix", "bc_mm", "prod", "qc", "x3", "x4", "z_mm", "add", "x")}
    with nc.Block() as block:
        @block.gpsimd
        def _(pool):
            start_at_1(pool, m, "wfix")
            with pool.Fori(0, NG) as g:
                pool.wait_ge(m["bc_mm"], g + 1)
                nc.gpsimd.tensor_copy(wfix, wtok[:, bass.ds(g * TG, TG)]).then_inc(m["wfix"], 1)

        @block.tensor
        def _(pe):
            start_at_1(pe, m, "bc_mm", "z_mm")
            with pe.Fori(0, NG) as g:
                pe.wait_ge(m["wfix"], g + 2)
                pe.wait_ge(m["prod"], g + 1)
                for k in range(TG):
                    last = nc.tensor.matmul(c.banks[:, 5, k * P:(k + 1) * P], wfix[:, k:k + 1].broadcast_to([P, P]),
                                            c.ident[:, :], start=True, stop=True)
                last.then_inc(m["bc_mm"], 1)
                pe.wait_ge(m["add"], g + 1)
                nc.tensor.matmul(c.banks[:, 6, :], wl[:, 0, :], cols(c.xn, g * G), start=True, stop=False)
                nc.tensor.matmul(c.banks[:, 6, :], wl[:, 1, :], cols(c2q, g * G), start=False, stop=False)
                pe.wait_ge(m["x3"], g + 2)
                nc.tensor.matmul(c.banks[:, 6, :], wl[:, 2, :], x3, start=False, stop=False)
                pe.wait_ge(m["x4"], g + 2)
                nc.tensor.matmul(c.banks[:, 6, :], wl[:, 3, :], x4, start=False, stop=True).then_inc(m["z_mm"], 1)

        @block.vector
        def _(dve):
            start_at_1(dve, m, "x3", "prod", "qc", "x4", "x")
            with dve.Fori(0, NG) as g:
                xn = cols(c.xn, g * G)
                dve.wait_ge(m["z_mm"], g + 1)
                nc.vector.tensor_tensor(x3, xn, cols(c2q, g * G), ALU.mult).then_inc(m["x3"], 1)
                dve.wait_ge(m["bc_mm"], g + 2)
                dve.wait_ge(m["qc"], g + 1)
                nc.vector.tensor_tensor(prod, xn, c.banks[:, 5, :], ALU.mult).then_inc(m["prod"], 1)
                dve.wait_ge(m["prod"], g + 2)
                dve.wait_ge(m["x4"], g + 1)
                nc.vector.tensor_reduce(qc, prod.rearrange("p (b s) -> p b s", s=S), axis=AX.X, op=ALU.add).then_inc(
                    m["qc"], 1)
                dve.wait_ge(m["qc"], g + 2)
                nc.vector.tensor_tensor(x4.rearrange("p (b s) -> p b s", s=S), xn.rearrange("p (b s) -> p b s", s=S),
                                        qc.unsqueeze(2).broadcast_to([P, BG, S]), ALU.mult).then_inc(m["x4"], 1)
                dve.wait_ge(m["add"], g + 2)
                nc.vector.tensor_tensor(cols(c.x, g * G), cols(c.x, g * G), add, ALU.add).then_inc(m["x"], 1)

        @block.scalar
        def _(act):
            start_at_1(act, m, "add")
            with act.Fori(0, NG) as g:
                act.wait_ge(m["z_mm"], g + 2)
                act.wait_ge(m["x"], g + 1)
                nc.scalar.activation(add, c.banks[:, 6, :], ACT.Identity, bias=col[:, 7:8],
                                     scale=c.tanh_g[:, 2:3]).then_inc(m["add"], 1)


def small_ffn(c, tag, A):
    nc = c.nc
    F = 32
    w1 = c.wa[:, 0:256]
    w2 = c.wa[:, 256:512].rearrange("p (j n) -> p j n", j=2)
    b1, b2 = c.wa[:, 512:514], c.wa[0:E, 640:768]
    wide = c.work[:, 0:1024].rearrange("p (k e f) -> p k e f", k=TG, e=E)
    narrow = c.work[:, 1024:1056].rearrange("p (k e) -> p k e", k=TG)
    hg = c.work[:, 1536:2560].rearrange("p (j n) -> p j n", j=2)
    hm = c.work[:, 2560:3584].rearrange("p (j n) -> p j n", j=2)
    mt = c.work[0:E, 3584:4096]
    m = {n: c.sem(f"{tag}_{n}") for n in ("w_in", "wide", "narrow", "h_mm", "mask_mm", "mt_mm", "hg", "hm", "mt", "y_mm", "x")}
    with nc.Block() as block:
        @block.sync
        def _(sp):
            sp.dma_start(w1, A["L3_ffn_W1T"]).then_inc(m["w_in"], 16)
            sp.dma_start(c.wa[:, 256:512], A["L3_ffn_W2T"]).then_inc(m["w_in"], 16)
            sp.dma_start(b1, A["L3_ffn_b1T"]).then_inc(m["w_in"], 16)
            sp.dma_start(b2, A["L3_ffn_b2"]).then_inc(m["w_in"], 16)

        @block.gpsimd
        def _(pool):
            start_at_1(pool, m, "narrow")
            with pool.Fori(0, NG) as g:
                pool.wait_ge(m["mt_mm"], g + 1)
                pool.wait_ge(m["wide"], g + 1)
                flat = c.gates[:, :, :].rearrange("p t e -> p (t e)")[:, bass.ds(g * (TG * E), TG * E)]
                nc.gpsimd.tensor_copy(narrow.rearrange("p k e -> p (k e)"), flat).then_inc(m["narrow"], 1)

        @block.tensor
        def _(pe):
            start_at_1(pe, m, "h_mm", "mask_mm", "mt_mm", "y_mm")
            pe.wait_ge(m["w_in"], 64)
            with pe.Fori(0, NG) as g:
                for j in range(2):
                    pe.wait_ge(m["hg"], g * 2 + j + 1)
                    nc.tensor.matmul(c.banks[:, j, :], w1[:, j * P:(j + 1) * P], cols(c.xn, g * G),
                                     start=True, stop=True).then_inc(m["h_mm"], 1)
                pe.wait_ge(m["wide"], g + 2)
                for j in range(2):
                    pe.wait_ge(m["hm"], g * 2 + j + 1)
                    for k in range(TG):
                        last = nc.tensor.matmul(c.banks[:, 2 + j, k * P:(k + 1) * P],
                                                wide[:, k, 4 * j:4 * j + 4, :].rearrange("p e f -> p (e f)"),
                                                c.ident[:, :], start=True, stop=True)
                    last.then_inc(m["mask_mm"], 1)
                pe.wait_ge(m["mt"], g + 1)
                for k in range(TG):
                    last = nc.tensor.matmul(c.banks[0:E, 4, k * P:(k + 1) * P], narrow[:, k, :], c.ident[:, :],
                                            start=True, stop=True)
                last.then_inc(m["mt_mm"], 1)
                pe.wait_ge(m["x"], g + 1)
                for j in range(2):
                    pe.wait_ge(m["hm"], g * 2 + j + 2)
                    nc.tensor.matmul(c.banks[:, 5, :], w2[:, j, :], hm[:, j, :], start=(j == 0), stop=False)
                pe.wait_ge(m["mt"], g + 2)
                nc.tensor.matmul(c.banks[:, 5, :], b2, mt, start=False, stop=True).then_inc(m["y_mm"], 1)

        @block.scalar
        def _(act):
            start_at_1(act, m, "wide", "hg", "mt")
            act.wait_ge(m["w_in"], 64)
            with act.Fori(0, NG) as g:
                act.wait_ge(m["narrow"], g + 2)
                act.wait_ge(m["mask_mm"], g * 2 + 1)
                nc.scalar.activation(wide.rearrange("p k e f -> p (k e) f"),
                                     narrow.rearrange("p k e -> p (k e)").unsqueeze(2).broadcast_to([P, TG * E, F]),
                                     ACT.Copy).then_inc(m["wide"], 1)
                for j in range(2):
                    act.wait_ge(m["h_mm"], g * 2 + j + 2)
                    act.wait_ge(m["hm"], g * 2 + j + 1)
                    nc.scalar.activation(hg[:, j, :], c.banks[:, j, :], ACT.Gelu, bias=b1[:, j:j + 1]).then_inc(
                        m["hg"], 1)
                act.wait_ge(m["mt_mm"], g + 2)
                act.wait_ge(m["y_mm"], g + 1)
                nc.scalar.activation(mt, c.banks[0:E, 4, :], ACT.Copy).then_inc(m["mt"], 1)

        @block.vector
        def _(dve):
            start_at_1(dve, m, "hm", "x")
            with dve.Fori(0, NG) as g:
                for j in range(2):
                    dve.wait_ge(m["hg"], g * 2 + j + 2)
                    dve.wait_ge(m["mask_mm"], g * 2 + j + 2)
                    dve.wait_ge(m["y_mm"], g + 1)
                    nc.vector.tensor_tensor(hm[:, j, :], hg[:, j, :], c.banks[:, 2 + j, :], ALU.mult).then_inc(m["hm"], 1)
                dve.wait_ge(m["y_mm"], g + 2)
                xg = cols(c.x, g * G)
                nc.vector.scalar_tensor_tensor(out=xg, in0=c.banks[:, 5, :], scalar=c.tanh_g[:, 7:8], in1=xg,
                                               op0=ALU.mult, op1=ALU.add).then_inc(m["x"], 1)


def store(c, out):
    nc = c.nc
    stored = c.sem("stored")
    with nc.Block() as block:
        @block.sync
        def _(sp):
            for k in range(4):
                sp.dma_start(out[:, k * 2048:(k + 1) * 2048], c.x[:, k * 2048:(k + 1) * 2048]).then_inc(stored, 16)
            sp.wait_ge(stored, 64)


def small_loads(c, tag, loads):
    nc = c.nc
    got = c.sem(tag + "_got")
    with nc.Block() as block:
        @block.sync
        def _(sp):
            for dst, src in loads:
                sp.dma_start(dst, src).then_inc(got, 16)
            sp.wait_ge(got, 16 * len(loads))


def zero_rows(c):
    nc = c.nc
    zero = c.wa[:, 4096:8192]
    cleared = c.sem("zero_made")
    rows = c.rows_in.rearrange("(p r) d -> p (r d)", p=P)
    n = rows.shape[1]
    with nc.Block() as block:
        @block.gpsimd
        def _(pool):
            nc.gpsimd.memset(zero, 0.0).then_inc(cleared, 1)

        @block.sync
        def _(sp):
            sp.wait_ge(cleared, 1)
            for at in range(0, n, 4096):
                w = min(4096, n - at)
                sp.dma_start(rows[:, at:at + w], zero[:, 0:w]).then_inc(c.zeroed, 16)


ZEROING = -(-(L0_GROUPS + 1) * G // 4096)


def program(nc, A, out):
    with ExitStack() as ctx:
        c = Chip(nc, ctx)
        setup(c, A)
        c.router_w = c.sb("router_w", [P, E])
        c.bias8 = c.sb("bias8", [P, E])
        c.rank = c.sb("rank", [P, NT, E])
        c.t1, c.t2, c.t3, c.t4, c.t2x = (c.sb(f"route{k}", [P, NT, E]) for k in range(5))
        c.m_b = c.sb("chosen", [P, NT, E], BF16)
        c.s1, c.s2, c.s3 = (c.sb(f"per_token{k}", [P, NT]) for k in range(3))
        c.gfix = c.sb("gfix", [P, TG, E])
        c.iota_i = c.sb("iota_i", [P, S], I32)

        c.slots = c.sb("slots", [P, NT, 2])
        c.token_gates = c.sb("token_gates", [P, NT, 2])
        c.index = c.sb("index", [P, 2, TG * 2], U32)
        c.per_expert = c.sb("per_expert", [P, 3, E])
        c.weight_rows = c.sb("weight_rows", [P, L2_GROUPS], U32)
        c.rows_in = nc.dram_tensor("rows_in", ((L0_GROUPS + 1) * G, P), F32, kind="Internal").ap()
        c.rows_out = nc.dram_tensor("rows_out", (L0_GROUPS * G, P), F32, kind="Internal").ap()
        c.zeroed = nc.alloc_semaphore(name="zeroed")

        def on(k):
            return START <= k < STOP

        c.attn_w = c.sb("attn_w", [P, 4, P])
        c.attn_b = c.sb("attn_b", [P, 4])
        c.mrow = c.wa[:, 0:4096].bitcast(BF16)
        c.mrow_fix = c.sb("mrow_fix", [P, 2, G], BF16)

        def attend(layer, scale, mask, kind, biases, block_diagonal):
            t = f"a{layer}"
            attention_weights(c, t, A, layer, block_diagonal, biases)
            mask_rows(c, t, mask, kind, scale)
            col = [c.attn_b[:, k:k + 1] for k in range(4)]
            attention(c, t, A["ctxT"], scale, c.tanh_g[:, layer:layer + 1], *col)

        zero_rows(c)
        layer_norm(c, "n0", c.x, c.xn)
        attend(0, P ** -0.5, A["mask_if1"], "zero_is_off", (None, None, None, "L0_xattn_bo"), True)
        small_loads(c, "l0f_affine", [(c.cols16[:, 0:1], A["L0_ffn_ln_gamma"].unsqueeze(1)),
                                      (c.cols16[:, 1:2], A["L0_ffn_ln_beta"].unsqueeze(1))])
        layer_norm(c, "n1a", c.x, c.xn)
        layer_norm(c, "n1b", c.xn, c.xn, (c.cols16[:, 0:1], c.cols16[:, 1:2]))
        router(c, "l0", A["L0_ffn_router_wT"])
        route_top2_capacity(c, "l0")
        w12 = c.wa[:, 0:8192].rearrange("p (e f) -> p e f", e=E)
        w3 = c.wa[:, 8192:12288].rearrange("p (e j n) -> p e j n", e=E, j=4)
        dispatch(c, "l0d", 2, E * L0_CAP - 1, zeroed=True)

        def l0_groups(engine, body):
            per = L0_GROUPS // E
            for e in range(E):
                with engine.Fori(0, per) as q:
                    body(q + e * per, e)
            return L0_GROUPS

        grouped_ffn(c, "l0f", 4, l0_groups,
                    lambda e: (lambda j: w12[:, e, j * P:(j + 1) * P], lambda j: w12[:, e, (4 + j) * P:(5 + j) * P],
                               lambda j: w3[:, e, j, :]),
                    weight_loads=[(c.wa[:, 0:8192], A["L0_ffn_w12T"]), (c.wa[:, 8192:12288], A["L0_ffn_w3T"])])
        combine(c, "l0c", 2, E * L0_CAP - 1)
        c.recycle_semaphores()
        layer_norm(c, "n2", c.x, c.xn)
        windowed_product(c, "l1x", A["ctxT"])
        c.recycle_semaphores()
        layer_norm(c, "n3", c.x, c.xn)
        router(c, "l1", A["L1_ffn_router_wT"])
        route_expert_choice(c, "l1", 1, False, S * 2 // E + 1, False)
        w1 = c.wb[:, 0:4096].rearrange("p (e f) -> p e f", e=E)
        w2 = c.wb[:, 4096:8192].rearrange("p (e j n) -> p e j n", e=E, j=4)
        b1 = c.cols16[:, 2:34].rearrange("p (e j) -> p e j", e=E)
        expert_ffn(c, "l1f", E, 4, False,
                   lambda e, j, k: w1[:, e, j * P:(j + 1) * P], lambda e, j: w2[:, e, j, :],
                   b1=lambda e, j: b1[:, e, j:j + 1], b2=lambda e: c.cols16[:, 34 + e:35 + e],
                   weight_loads=[(c.wb[:, 0:4096], A["L1_ffn_w1T"]), (c.wb[:, 4096:8192], A["L1_ffn_w2T"]),
                                 (c.cols16[:, 2:34], A["L1_ffn_b1T"]), (c.cols16[:, 34:42], A["L1_ffn_b2T"])])
        layer_norm(c, "n4", c.x, c.xn)
        two_way_attention(c, "bi", A, A["ctxT"], A["ctx_q"])
        c.recycle_semaphores()
        layer_norm(c, "n5", c.x, c.xn)
        router(c, "l2", A["L2_ffn_routerT"])
        route_argmax(c, "l2")
        small_loads(c, "l2s", [(c.wa[:, 0:768], A["L2_ffn_shared"])])
        sh = c.wa[:, 0:768]
        dispatch(c, "l2d", 1, L2_GROUPS * G - 1,
                 shared=(sh[:, 0:256], sh[:, 256:512], sh[:, 512:768].rearrange("p (j n) -> p j n", j=2),
                         c.tanh_g[:, 6:7]))
        arrived = [c.sem(f"l2w_arrived{v}") for v in range(2)]

        def l2_fetch(n):
            v = n % 2
            nc.gpsimd.indirect_dma_start(c.wa[:, 1024 + 768 * v:1024 + 768 * v + 768], None, A["L2_ffn_rows"],
                                         bass.IndirectOffsetOnAxis(c.weight_rows[:, n:n + 1], 0),
                                         bounds_check=E * P - 1, oob_is_err=False).then_inc(arrived[v], 16)

        def l2_groups(engine, body):
            with engine.Fori(0, L2_GROUPS // 2) as i:
                for v in range(2):
                    body(i * 2 + v, (i, v))
            return L2_GROUPS

        def l2_weights(key):
            w = c.wa[:, 1024 + 768 * key[1]:1024 + 768 * key[1] + 768]
            return (lambda j: w[:, j * P:(j + 1) * P], lambda j: w[:, (2 + j) * P:(3 + j) * P],
                    lambda j: w[:, (4 + j) * P:(5 + j) * P])

        grouped_ffn(c, "l2f", 2, l2_groups, l2_weights, fetch=(L2_GROUPS, l2_fetch, arrived))
        combine(c, "l2c", 1, L2_GROUPS * G - 1, gate=c.tanh_g[:, 6:7])
        c.recycle_semaphores()
        layer_norm(c, "n6", c.x, c.xn)
        attend(3, HD ** -0.5, A["mask_fk0"], "one_is_off",
               ("L3_xattn_bq", "L3_xattn_bk", "L3_xattn_bv", "L3_xattn_bo"), False)
        layer_norm(c, "n7", c.x, c.xn)
        router(c, "l3", A["L3_ffn_w_gate_w"], A["L3_ffn_w_gate_b"])
        route_expert_choice(c, "l3", 3, True, S // 2, True)
        small_ffn(c, "l3f", A)
        store(c, out)


def kernel(**inputs):
    import numpy as _np
    import concourse.bacc as _bacc
    from concourse import mybir as _mybir
    from concourse.bass_utils import run_bass_kernel_spmd as _run

    v = {k: _np.asarray(a) for k, a in inputs.items()}

    def tiles_last(w):
        e, o, f = w.shape
        return w.reshape(e, o, f // 128, 128).transpose(3, 0, 2, 1).reshape(128, -1)

    def down_rows(w):
        e, o, f = w.shape
        return w.reshape(e, o, f // 128, 128).transpose(0, 3, 2, 1).reshape(e, 128, -1)

    def tiles_first(w):
        e, f, o = w.shape
        return w.reshape(e, f // 128, 128, o).transpose(2, 0, 1, 3).reshape(128, -1)

    lay = {
        "xT": v["x"].reshape(8192, 128).T,
        "ctxT": v["ctx_1024"].reshape(8192, 128).T,
        "ctx_q": v["ctx_1024"].transpose(1, 0, 2).reshape(64, -1),
        "L2_xattn_W_lT": v["L2_xattn_W_l"].reshape(128, 4, 128).transpose(2, 1, 0).reshape(128, -1),
        "L2_xattn_b_cq": v["L2_xattn_b_cq"].reshape(1),
        "L2_xattn_b_c": v["L2_xattn_b_c"].reshape(1),
        "L2_xattn_b_q": v["L2_xattn_b_q"].reshape(1),
        "L3_ffn_W1T": v["L3_ffn_W1"].transpose(1, 0, 2).reshape(128, -1),
        "L3_ffn_W2T": v["L3_ffn_W2"].reshape(2, 128, 128).transpose(1, 0, 2).reshape(128, -1),
        "L3_ffn_b1T": v["L3_ffn_b1"].reshape(2, 128).T,
        "L0_ffn_router_wT": v["L0_ffn_router_w"].T,
        "L0_ffn_w12T": v["L0_ffn_w12"].transpose(2, 0, 1).reshape(128, -1),
        "L0_ffn_w3T": tiles_last(v["L0_ffn_w3"]),
        "L1_ffn_router_wT": v["L1_ffn_router_w"].T,
        "L1_ffn_w1T": v["L1_ffn_w1"].transpose(1, 0, 2).reshape(128, -1),
        "L1_ffn_w2T": tiles_first(v["L1_ffn_w2"]),
        "L1_ffn_b1T": v["L1_ffn_b1"].reshape(8, 4, 128).transpose(2, 0, 1).reshape(128, -1),
        "L1_ffn_b2T": v["L1_ffn_b2"].T,
        "L2_ffn_routerT": v["L2_ffn_router"].T,
        "L2_ffn_rows": _np.concatenate([v["L2_ffn_gate"].transpose(0, 2, 1), v["L2_ffn_up"].transpose(0, 2, 1),
                                        down_rows(v["L2_ffn_down"])], axis=2).reshape(1024, 768),
        "L2_ffn_shared": _np.concatenate([v["L2_ffn_w_gate_s"].T, v["L2_ffn_w_up_s"].T,
                                          down_rows(v["L2_ffn_w_down_s"][None])[0]], axis=1),
    }
    for w in ("Wq", "Wk", "Wv", "Wo"):
        lay[f"L0_xattn_{w}T"] = v[f"L0_xattn_{w}"].T
        lay[f"L3_xattn_{w}T"] = v[f"L3_xattn_{w.lower()}"]
    lay["mask_if1"] = v["mask_Bx1x1xS2_if1"].reshape(128, 64)
    lay["mask_fk0"] = v["mask_Bx1x1xS2_fk0"].reshape(128, 64)
    for name in ("L0_xattn_bo", "L3_xattn_bq", "L3_xattn_bk", "L3_xattn_bv", "L3_xattn_bo",
                 "L2_xattn_w_cq", "L2_xattn_w_q", "L2_xattn_w_c", "L2_xattn_b_l", "L3_ffn_w_gate_w", "L3_ffn_w_gate_b",
                 "L3_ffn_b2", "g_xattn", "g_ffn", "L0_ffn_ln_gamma", "L0_ffn_ln_beta"):
        lay[name] = v[name]

    nc = _bacc.Bacc("TRN2", target_bir_lowering=False, num_devices=1)
    arrays, A = {}, {}
    for name, a in lay.items():
        a = _np.ascontiguousarray(a)
        arrays[f"in_{name}"] = a
        A[name] = nc.dram_tensor(f"in_{name}", a.shape, _mybir.dt.from_np(a.dtype), kind="ExternalInput").ap()
    out = nc.dram_tensor("out_0_dram", (128, 8192), _mybir.dt.float32, kind="ExternalOutput").ap()
    program(nc, A, out)
    r = _run(nc, [arrays], core_ids=[0])
    return _np.ascontiguousarray(r.results[0]["out_0_dram"].T).reshape(128, 64, 128)
```

```python
from contextlib import ExitStack

import concourse.bass as bass
from concourse import mybir

F32 = mybir.dt.float32
BF16 = mybir.dt.bfloat16
I32 = mybir.dt.int32
U32 = mybir.dt.uint32
ALU = mybir.AluOpType
ACT = mybir.ActivationFunctionType
AX = mybir.AxisListType

P = 128
B, S = 128, 64
T = B * S
NT = T // P
G = 512
NG = T // G
TG = G // P
BG = G // S
E = 8
H, HD = 16, 8
EPS = 1e-5
L0_CAP = -(-T * 2 * 5 // (4 * E))
L0_GROUPS = E * L0_CAP // G
assert L0_CAP % G == 0 and L0_GROUPS // E % 2 == 1
L2_BUFFERS = 4
L2_GROUPS = (NG + E) // L2_BUFFERS * L2_BUFFERS
assert L2_GROUPS >= NG + E - 1
L1_KEEP = S * 2 // E + 1
SUMS_AT = 14 * G
BEYOND = float(2 ** 20)


class Chip:

    def __init__(self, nc, ctx):
        self.nc, self.ctx = nc, ctx
        self.sems = []

    def sb(self, name, shape, dt=F32):
        return self.ctx.enter_context(self.nc.sbuf_tensor(name, shape, dt))

    def sem(self, name):
        handle = self.nc.alloc_semaphore(name=name)
        self.sems.append(handle)
        return handle

    def recycle_semaphores(self):
        self.nc.clear_and_free_semaphores(self.sems)
        self.sems = []
        self.nc.all_engine_barrier()


def cols(t, at, n=G):
    return t[:, bass.ds(at, n)]


def over(ap, shape):
    return ap.broadcast_to(shape)


def start_at_1(engine, m, *names):
    for name in names:
        engine.sem_inc(m[name], 1)


def setup(c, A):
    nc = c.nc
    c.xpad = c.sb("x", [P, G + T])
    c.x = c.xpad[:, G:G + T]
    c.xn = c.sb("xn", [P, T])
    c.wa = c.sb("weights_a", [P, 12288])
    c.wb = c.sb("weights_b", [P, 8192])
    c.work = c.sb("work", [P, 8192])
    c.avg = c.sb("avg", [P, P])
    c.ident = c.sb("ident", [P, P])
    c.same_pos = c.sb("same_pos", [P, P])
    c.before = c.sb("before", [P, P], BF16)
    c.before_seq = c.sb("before_seq", [P, P], BF16)
    c.ones = c.sb("ones", [P, P], BF16)
    c.lower = c.sb("lower", [P, E, E])
    c.half = c.sb("half", [P, 2])
    c.half16 = c.sb("half16", [P, 2, HD])
    c.quad = c.sb("quad", [P, 4])
    c.eps = c.sb("eps", [P, 1])
    c.gate_in = c.sb("gate_in", [P, 8])
    c.tanh_g = c.sb("tanh_g", [P, 8])
    c.gates = c.sb("gates", [P, NT, E])
    c.cols16 = c.sb("cols16", [P, 64])
    c.banks = c.ctx.enter_context(nc.psum_tensor("banks", [P, 8, G], F32))
    x_in = c.sem("x_in")
    small_in = c.sem("small_in")
    filled = c.sem("filled")
    tanhed = c.sem("tanhed")
    with nc.Block() as block:
        @block.sync
        def _(sp):
            for k in range(4):
                sp.dma_start(c.x[:, k * 2048:(k + 1) * 2048], A["xT"][:, k * 2048:(k + 1) * 2048]).then_inc(x_in, 16)
            sp.wait_ge(x_in, 64)

        @block.scalar
        def _(act):
            act.dma_start(c.gate_in[:, 0:4], A["g_xattn"].partition_broadcast(P)).then_inc(small_in, 16)
            act.dma_start(c.gate_in[:, 4:8], A["g_ffn"].partition_broadcast(P)).then_inc(small_in, 16)
            act.wait_ge(small_in, 32)
            nc.scalar.activation(c.tanh_g[:, :], c.gate_in[:, :], ACT.Tanh).then_inc(tanhed, 1)

        @block.gpsimd
        def _(pool):
            done = [0]

            def put(ins):
                done[0] += 1
                ins.then_inc(filled, 1)
                pool.wait_ge(filled, done[0])

            def keep(t, pattern, base, mult, cmp, fill=0.0):
                put(nc.gpsimd.affine_select(out=t, in_=t, compare_op=cmp, fill=fill, base=base,
                                            pattern=pattern, channel_multiplier=mult))

            put(nc.gpsimd.memset(c.avg[:, :], 1.0 / P))
            put(nc.gpsimd.memset(c.xpad[:, 0:G], 0.0))
            put(nc.gpsimd.memset(c.eps[:, :], EPS))
            put(nc.gpsimd.memset(c.ones[:, :], 1.0))
            put(nc.gpsimd.memset(c.ident[:, :], 0.0))
            keep(c.ident[:, :], [[-1, P]], 0, 1, ALU.not_equal, 1.0)
            put(nc.gpsimd.memset(c.same_pos[:, :], 0.0))
            for off in (-S, 0, S):
                keep(c.same_pos[:, :], [[-1, P]], off, 1, ALU.not_equal, 1.0)
            put(nc.gpsimd.memset(c.before[:, :], 1.0))
            keep(c.before[:, :], [[1, P]], -1, -1, ALU.is_ge)
            put(nc.gpsimd.memset(c.before_seq[:, :], 1.0))
            keep(c.before_seq[:, :], [[1, P]], -1, -1, ALU.is_ge)
            put(nc.gpsimd.memset(c.before_seq[0:S, S:P], 0.0))
            put(nc.gpsimd.memset(c.lower[:, :, :], 1.0))
            keep(c.lower[:, :, :], [[1, E], [-1, E]], -1, 0, ALU.is_ge)
            put(nc.gpsimd.memset(c.half[:, :], 1.0))
            keep(c.half[:, :], [[-S, 2]], 0, 1, ALU.is_ge)
            keep(c.half[:, :], [[S, 2]], S - 1, -1, ALU.is_ge)
            put(nc.gpsimd.memset(c.half16[:, :, :], 1.0))
            keep(c.half16[:, :, :], [[-S, 2], [0, HD]], 0, 1, ALU.is_ge)
            keep(c.half16[:, :, :], [[S, 2], [0, HD]], S - 1, -1, ALU.is_ge)
            put(nc.gpsimd.memset(c.quad[:, :], 0.0))
            for q in range(4):
                rows = c.quad[32 * q:32 * q + 32, :]
                put(nc.gpsimd.memset(rows, 1.0))
                keep(rows, [[-HD, 4]], 0, 1, ALU.is_ge)
                keep(rows, [[HD, 4]], HD - 1, -1, ALU.is_ge)


def layer_norm(c, tag, src, dst, twice=None, meanwhile=()):
    nc = c.nc
    U, AHEAD = 4, 3
    sq = c.work[:, 0:U * G].rearrange("p (u n) -> p u n", u=U)
    fix = c.work[:, U * G:U * G + U * TG].rearrange("p (u k) -> p u k", u=U)
    rs, va, nw, first = (c.work[:, 2176 + 64 * k:2240 + 64 * k] for k in range(4))
    mean, var, wide = c.banks[:, 0:U, :], c.banks[:, 4, 0:NT], c.banks[:, 0:U, :]
    m = {n: c.sem(f"{tag}_{n}") for n in ("mean", "xc", "sq", "var", "ln", "exp", "step", "rs", "fix", "wide", "scaled",
                                          "out")}
    sync_work, gpsimd_work = meanwhile or (None, None)

    def slots(engine, slot):
        with engine.Fori(0, NG // U - 1) as i:
            for u in range(U):
                slot(i * U + u, u, True)
        for u in range(U):
            slot(NG - U + u, u, u + AHEAD < U)

    with nc.Block() as block:
        @block.tensor
        def _(pe):
            pe.sem_inc(m["var"], U)
            pe.sem_inc(m["wide"], U)

            def take_mean(s, u):
                pe.wait_ge(m["xc"], s + 1)
                nc.tensor.matmul(mean[:, u, :], c.avg[:, :], cols(src, s * G), start=True,
                                 stop=True).then_inc(m["mean"], 1)

            def variance(s, u, more):
                pe.wait_ge(m["sq"], s + 1)
                for k in range(TG):
                    last = nc.tensor.matmul(var[:, bass.ds(s * TG + k, 1)], sq[:, u, k * P:(k + 1) * P],
                                            c.avg[:, 0:1], start=True, stop=True)
                last.then_inc(m["var"], 1)
                if more:
                    take_mean(s + AHEAD, (u + AHEAD) % U)

            def widen(s, u, more):
                pe.wait_ge(m["fix"], s + 1)
                pe.wait_ge(m["out"], s + 1)
                for k in range(TG):
                    last = nc.tensor.matmul(wide[:, u, k * P:(k + 1) * P], fix[:, u, k:k + 1].broadcast_to([P, P]),
                                            c.ident[:, :], start=True, stop=True)
                last.then_inc(m["wide"], 1)

            for s in range(AHEAD):
                take_mean(s, s)
            slots(pe, variance)
            slots(pe, widen)

        @block.vector
        def _(dve):
            dve.sem_inc(m["xc"], U)
            dve.sem_inc(m["out"], U)
            link = chain_on(dve, m["step"])

            def centre(s, u):
                dve.wait_ge(m["mean"], s + 1)
                nc.vector.tensor_tensor(cols(dst, s * G), cols(src, s * G), mean[:, u, :],
                                        ALU.subtract).then_inc(m["xc"], 1)

            def scale(s, u, more):
                dve.wait_ge(m["wide"], s + (U + 1))
                at = cols(dst, s * G)
                if twice is None:
                    nc.vector.tensor_tensor(at, at, wide[:, u, :], ALU.mult).then_inc(m["out"], 1)
                else:
                    nc.vector.scalar_tensor_tensor(out=at, in0=at, scalar=twice[0], in1=wide[:, u, :], op0=ALU.mult,
                                                   op1=ALU.mult).then_inc(m["out"], 1)

            for s in range(AHEAD):
                centre(s, s)
            with dve.Fori(0, NG // U - 1) as i:
                for u in range(U):
                    centre(i * U + u + AHEAD, (u + AHEAD) % U)
            for s in range(NG - U + AHEAD, NG):
                centre(s, s % U)
            for k in range(2 if twice else 1):
                dve.wait_ge(m["exp"], k + 1)
                link(nc.vector.tensor_tensor(nw, rs, rs, ALU.mult))
                link(nc.vector.tensor_tensor(nw, nw, va, ALU.mult))
                link(nc.vector.tensor_scalar(nw, nw, -0.5, 1.5, ALU.mult, ALU.add))
                if twice and k == 0:
                    link(nc.vector.tensor_tensor(rs, rs, nw, ALU.mult))
                    link(nc.vector.tensor_copy(first, rs))
                    link(nc.vector.tensor_tensor(nw, rs, rs, ALU.mult))
                    nc.vector.tensor_tensor(nw, nw, var, ALU.mult).then_inc(m["rs"], 1)
                elif twice:
                    link(nc.vector.tensor_tensor(rs, rs, nw, ALU.mult))
                    nc.vector.tensor_tensor(rs, rs, first, ALU.mult).then_inc(m["rs"], 1)
                else:
                    nc.vector.tensor_tensor(rs, rs, nw, ALU.mult).then_inc(m["rs"], 1)
            slots(dve, scale)

        @block.scalar
        def _(act):
            def square(s, u):
                act.wait_ge(m["xc"], s + (U + 1))
                act.wait_ge(m["var"], s + 1)
                nc.scalar.activation(sq[:, u, :], cols(dst, s * G), ACT.Square).then_inc(m["sq"], 1)

            def fixed(s, u, more):
                act.wait_ge(m["wide"], s + 1)
                nc.scalar.activation(fix[:, u, :], rs[:, bass.ds(s * TG, TG)], ACT.Copy).then_inc(m["fix"], 1)

            def shift(s, u, more):
                act.wait_ge(m["out"], s + (U + 1))
                at = cols(dst, s * G)
                nc.scalar.activation(at, at, ACT.Identity, bias=twice[1]).then_inc(m["scaled"], 1)

            for s in range(AHEAD):
                square(s, s)
            with act.Fori(0, NG // U - 1) as i:
                for u in range(U):
                    square(i * U + u + AHEAD, (u + AHEAD) % U)
            for s in range(NG - U + AHEAD, NG):
                square(s, s % U)
            act.wait_ge(m["var"], NG + U)
            for k in range(2 if twice else 1):
                nc.scalar.activation(va, nw if k else var, ACT.Identity, bias=c.eps[:, :]).then_inc(m["ln"], 1)
                act.wait_ge(m["ln"], 2 * k + 1)
                nc.scalar.activation(rs, va, ACT.Ln).then_inc(m["ln"], 1)
                act.wait_ge(m["ln"], 2 * k + 2)
                nc.scalar.activation(rs, rs, ACT.Exp, scale=-0.5).then_inc(m["exp"], 1)
                act.wait_ge(m["rs"], k + 1)
            if twice is None:
                slots(act, fixed)
            else:
                for s in range(U):
                    fixed(s, s, True)
                with act.Fori(1, NG // U) as i:
                    for u in range(U):
                        fixed(i * U + u, u, True)
                        shift(i * U + (u - U), u, True)
                for s in range(NG - U, NG):
                    shift(s, s % U, False)

        if meanwhile:
            @block.sync
            def _(sp):
                sync_work(sp)

            @block.gpsimd
            def _(pool):
                gpsimd_work(pool)


def router(c, tag, w_in, bias=None):
    nc = c.nc
    w = c.router_w
    w_loaded = c.sem(tag + "_router_loaded")
    logits_done = c.sem(tag + "_logits_done")
    with nc.Block() as block:
        @block.sync
        def _(sp):
            sp.dma_start(w[:, :], w_in).then_inc(w_loaded, 16)
            if bias is not None:
                sp.dma_start(c.bias8[:, :], bias.partition_broadcast(P)).then_inc(w_loaded, 16)
            sp.wait_ge(w_loaded, 16 if bias is None else 32)

        @block.tensor
        def _(pe):
            pe.wait_ge(w_loaded, 16 if bias is None else 32)
            for t in range(NT):
                last = nc.tensor.matmul(c.banks[:, 0, t * E:(t + 1) * E], c.xn[:, t * P:(t + 1) * P], w[:, :],
                                        start=True, stop=True)
            last.then_inc(logits_done, 1)


def chain_on(engine, sem):
    n = [0]

    def link(ins):
        n[0] += 1
        ins.then_inc(sem, 1)
        engine.wait_ge(sem, n[0])
    return link


def rank_experts(c, link, v):
    nc = c.nc
    gt = c.wb[:, 0:4096].rearrange("p (t e f) -> p t e f", t=NT, e=E)
    eq = c.wb[:, 4096:8192].rearrange("p (t e f) -> p t e f", t=NT, e=E)
    other = v.unsqueeze(2).broadcast_to([P, NT, E, E])
    own = v.unsqueeze(3).broadcast_to([P, NT, E, E])
    link(nc.vector.tensor_tensor(gt, other, own, ALU.is_gt))
    link(nc.vector.tensor_tensor(eq, other, own, ALU.is_equal))
    link(nc.vector.tensor_tensor(eq, eq, c.lower[:, :, :].unsqueeze(1).broadcast_to([P, NT, E, E]), ALU.mult))
    link(nc.vector.tensor_tensor(gt, gt, eq, ALU.add))
    link(nc.vector.tensor_reduce(c.rank[:, :, :], gt, axis=AX.X, op=ALU.add))


def running_counts(c, link, ready):
    nc = c.nc
    flat = "p t e -> p (t e)"
    tot, run, one = c.t2x, c.t4, c.rank
    ready()
    link(nc.vector.tensor_copy(tot[:, :, :].rearrange(flat), c.banks[:, 2, :]))
    link(nc.vector.memset(one[:, :, :], 1.0))
    for e in range(E):
        link(nc.vector.tensor_tensor_scan(run[:, :, e], one[:, :, e], tot[:, :, e], 0.0, ALU.mult, ALU.add))
    link(nc.vector.tensor_copy(c.per_expert[:, 0, :], run[:, NT - 1, :]))
    link(nc.vector.tensor_tensor(run[:, :, :], run[:, :, :], tot[:, :, :], ALU.subtract))
    link(nc.vector.tensor_tensor(run[:, :, :].rearrange(flat), run[:, :, :].rearrange(flat), c.banks[:, 1, :], ALU.add))


def count_chosen(c, pe, chosen, counted):
    nc = c.nc
    chose = c.m_b[:, :, :].rearrange("p t e -> p (t e)")
    pe.wait_ge(chosen, 1)
    nc.tensor.matmul(c.banks[:, 1, :], c.before[:, :], chose, start=True, stop=True)
    nc.tensor.matmul(c.banks[:, 2, :], c.ones[:, :], chose, start=True, stop=True).then_inc(counted, 1)


def pick(c, link, out, one_hot, values):
    nc = c.nc
    link(nc.vector.tensor_tensor(c.t2x[:, :, :], one_hot, values, ALU.mult))
    link(nc.vector.tensor_reduce(out, c.t2x[:, :, :], axis=AX.X, op=ALU.add))


def route_top2_capacity(c, tag):
    nc = c.nc
    cap = L0_CAP
    logits = c.banks[:, 0, :].rearrange("p (t e) -> p t e", e=E)
    step = c.sem(tag + "_step")
    gap_ready, exp_ready, chosen, counted = (c.sem(tag + n) for n in ("_gap", "_exp", "_chosen", "_counted"))
    with nc.Block() as block:
        @block.vector
        def _(dve):
            link = chain_on(dve, step)
            v, oh = c.t1, (c.t2, c.t3)
            link(nc.vector.tensor_scalar(v[:, :, :], logits, 1e4, -1e4, ALU.min, ALU.max))
            rank_experts(c, link, v[:, :, :])
            nc.vector.tensor_scalar(c.m_b[:, :, :], c.rank[:, :, :], 2.0, None, ALU.is_lt).then_inc(chosen, 1)
            for k in range(2):
                link(nc.vector.tensor_scalar(oh[k][:, :, :], c.rank[:, :, :], float(k), None, ALU.is_equal))
            pick(c, link, c.s1[:, :], oh[0][:, :, :], v[:, :, :])
            pick(c, link, c.s2[:, :], oh[1][:, :, :], v[:, :, :])
            nc.vector.tensor_tensor(c.s2[:, :], c.s2[:, :], c.s1[:, :], ALU.subtract).then_inc(gap_ready, 1)
            running_counts(c, link, lambda: dve.wait_ge(counted, 1))
            dve.wait_ge(exp_ready, 1)
            link(nc.vector.tensor_scalar(c.s1[:, :], c.s3[:, :], 1.0, 1e-12, ALU.add, ALU.add))
            link(nc.vector.reciprocal(c.s1[:, :], c.s1[:, :]))
            link(nc.vector.tensor_scalar(c.s1[:, :], c.s1[:, :], c.tanh_g[:, 4:5], None, ALU.mult))
            link(nc.vector.tensor_tensor(c.s3[:, :], c.s3[:, :], c.s1[:, :], ALU.mult))
            link(nc.vector.tensor_reduce(c.per_expert[:, 0, :], c.lower[:, :, :], axis=AX.X, op=ALU.add))
            link(nc.vector.tensor_scalar(c.per_expert[:, 0, :], c.per_expert[:, 0, :], float(cap), None, ALU.mult))
            for k, gate in enumerate((c.s1, c.s3)):
                pick(c, link, c.s2[:, :], oh[k][:, :, :], c.t4[:, :, :])
                link(nc.vector.tensor_scalar(c.s2[:, :], c.s2[:, :], float(cap), None, ALU.is_lt))
                link(nc.vector.tensor_tensor(c.token_gates[:, :, k], gate[:, :], c.s2[:, :], ALU.mult))
                link(nc.vector.tensor_scalar(c.s2[:, :], c.s2[:, :], -BEYOND, BEYOND, ALU.mult, ALU.add))
                pick(c, link, c.slots[:, :, k], oh[k][:, :, :], c.t4[:, :, :])
                link(nc.vector.tensor_tensor(c.s2[:, :], c.s2[:, :], c.slots[:, :, k], ALU.add))
                pick(c, link, c.slots[:, :, k], oh[k][:, :, :],
                     c.per_expert[:, 0, :].unsqueeze(1).broadcast_to([P, NT, E]))
                link(nc.vector.tensor_tensor(c.slots[:, :, k], c.slots[:, :, k], c.s2[:, :], ALU.add))

        @block.scalar
        def _(act):
            act.wait_ge(gap_ready, 1)
            nc.scalar.activation(c.s3[:, :], c.s2[:, :], ACT.Exp).then_inc(exp_ready, 1)

        @block.tensor
        def _(pe):
            count_chosen(c, pe, chosen, counted)


def route_argmax(c, tag):
    nc = c.nc
    logits = c.banks[:, 0, :].rearrange("p (t e) -> p t e", e=E)
    step, chosen, counted = (c.sem(tag + n) for n in ("_step", "_chosen", "_counted"))
    numbered = c.sem(tag + "_numbered")
    at = c.wb[:, 0:L2_GROUPS]
    row = c.wb[:, 64:65]
    past = c.wb[:, 128:128 + L2_GROUPS * E]
    full = c.wb[:, 512:512 + E * NG].rearrange("p (e g) -> p e g", e=E)
    with nc.Block() as block:
        @block.gpsimd
        def _(pool):
            nc.gpsimd.iota(c.iota_i[:, 0:32], pattern=[[1, 32]], base=0, channel_multiplier=0).then_inc(numbered, 1)
            nc.gpsimd.iota(c.iota_i[:, 32:33], pattern=[[0, 1]], base=0, channel_multiplier=1).then_inc(numbered, 1)

        @block.vector
        def _(dve):
            link = chain_on(dve, step)
            link(nc.vector.tensor_copy(c.t1[:, :, :], logits))
            rank_experts(c, link, c.t1[:, :, :])
            nc.vector.tensor_scalar(c.m_b[:, :, :], c.rank[:, :, :], 1.0, None, ALU.is_lt).then_inc(chosen, 1)
            link(nc.vector.tensor_scalar(c.t3[:, :, :], c.rank[:, :, :], 0.0, None, ALU.is_equal))
            running_counts(c, link, lambda: dve.wait_ge(counted, 1))
            dve.wait_ge(numbered, 2)
            link(nc.vector.tensor_copy(at, c.iota_i[:, 0:L2_GROUPS]))
            link(nc.vector.tensor_copy(row, c.iota_i[:, 32:33]))
            tokens, ends, groups = (c.per_expert[:, k, :] for k in range(3))
            link(nc.vector.tensor_scalar(c.s1[:, 0:NG], at[:, 0:NG], float(G), None, ALU.mult))
            link(nc.vector.tensor_tensor(full, tokens.unsqueeze(2).broadcast_to([P, E, NG]),
                                         c.s1[:, 0:NG].unsqueeze(1).broadcast_to([P, E, NG]), ALU.is_gt))
            link(nc.vector.tensor_reduce(groups, full, axis=AX.X, op=ALU.add))
            link(nc.vector.memset(c.s2[:, 0:E], 1.0))
            link(nc.vector.tensor_tensor_scan(ends, c.s2[:, 0:E], groups, 0.0, ALU.mult, ALU.add))
            p3 = past.rearrange("p (g e) -> p g e", e=E)
            link(nc.vector.tensor_tensor(p3, ends.unsqueeze(1).broadcast_to([P, L2_GROUPS, E]),
                                         at.unsqueeze(2).broadcast_to([P, L2_GROUPS, E]), ALU.is_le))
            link(nc.vector.tensor_reduce(at, p3, axis=AX.X, op=ALU.add))
            link(nc.vector.tensor_scalar(at, at, float(E - 1), float(P), ALU.min, ALU.mult))
            link(nc.vector.tensor_scalar(c.weight_rows[:, :], at, row, None, ALU.add))
            link(nc.vector.tensor_tensor(ends, ends, groups, ALU.subtract))
            link(nc.vector.tensor_scalar(ends, ends, float(G), None, ALU.mult))
            link(nc.vector.tensor_tensor(c.t4[:, :, :], c.t4[:, :, :], ends.unsqueeze(1).broadcast_to([P, NT, E]),
                                         ALU.add))
            pick(c, link, c.slots[:, :, 0], c.t3[:, :, :], c.t4[:, :, :])

        @block.tensor
        def _(pe):
            count_chosen(c, pe, chosen, counted)


def row_groups(dram):
    return dram.rearrange("(g p s) d -> p g (s d)", p=P, s=TG)


def dispatch(c, tag, K, last_slot, shared=None, zeroed=False):
    nc = c.nc
    fix = c.work[:, 0:2 * G].rearrange("p (u n) -> p u n", u=2)
    rows = c.wb[:, 0:2 * G].rearrange("p (u k n) -> p u k n", u=2, k=TG)
    sil = c.work[:, 2 * G:4 * G].rearrange("p (j n) -> p j n", j=2)
    hid = c.work[:, 4 * G:8 * G].rearrange("p (u j n) -> p u j n", u=2, j=2)
    index = c.index[:, :, 0:TG * K]
    written = [c.sem(f"{tag}_written{u}") for u in range(2)]
    m = {n: c.sem(f"{tag}_{n}") for n in ("fix", "t_mm", "rows", "index", "up_mm", "silu", "hid", "y_mm", "x", "go")}
    per_use = 16 * TG * K
    slots = c.slots[:, :, :].rearrange("p t k -> p k t")[:, 0:K, :]
    with nc.Block() as block:
        def groups(engine, body):
            with engine.Fori(0, NG // 2) as i:
                for u in range(2):
                    body(i, i * 2 + u, u)

        def peeled(engine, body):
            for u in range(2):
                body(0, u, u, True)
            with engine.Fori(1, NG // 2) as i:
                for u in range(2):
                    body(i, i * 2 + u, u, False)

        if shared:
            @block.scalar
            def _(act):
                def body(i, g, u):
                    act.wait_ge(m["hid"], g * 2 + 1)
                    for j in range(2):
                        act.wait_ge(m["up_mm"], g * 2 + (j + 1))
                        nc.scalar.activation(sil[:, j, :], c.banks[:, 2 + j, :], ACT.Silu).then_inc(m["silu"], 1)

                groups(act, body)

        @block.tensor
        def _(pe):
            start_at_1(pe, m, "t_mm", "y_mm")
            start_at_1(pe, m, "t_mm", "y_mm")

            def down(g, u):
                pe.wait_ge(m["hid"], g * 2 + 3)
                pe.wait_ge(m["x"], g + 1)
                for j in range(2):
                    last = nc.tensor.matmul(c.banks[:, 6, :], shared[2][:, j, :], hid[:, u, j, :],
                                            start=(j == 0), stop=(j == 1))
                last.then_inc(m["y_mm"], 1)

            def body(i, g, u, first):
                pe.wait_ge(m["fix"], g + 1)
                pe.wait_ge(m["rows"], g + 1)
                for k in range(TG):
                    last = nc.tensor.transpose(c.banks[:, u, k * P:(k + 1) * P], fix[:, u, k * P:(k + 1) * P],
                                               c.ident[:, :])
                last.then_inc(m["t_mm"], 1)
                if shared:
                    pe.wait_ge(m["hid"], g * 2 + 1)
                    for j in range(2):
                        nc.tensor.matmul(c.banks[:, 2 + j, :], shared[0][:, j * P:(j + 1) * P], cols(c.xn, g * G),
                                         start=True, stop=True)
                        nc.tensor.matmul(c.banks[:, 4 + j, :], shared[1][:, j * P:(j + 1) * P], cols(c.xn, g * G),
                                         start=True, stop=True).then_inc(m["up_mm"], 1)
                    if u or not first:
                        down(g - 1, 1 - u)

            peeled(pe, body)
            if shared:
                down(NG - 1, 1)

        @block.vector
        def _(dve):
            start_at_1(dve, m, "rows", "hid", "x")
            dve.sem_inc(m["rows"], 1)

            def add_to_x(g):
                dve.wait_ge(m["y_mm"], g + 3)
                at = cols(c.x, g * G)
                nc.vector.scalar_tensor_tensor(out=at, in0=c.banks[:, 6, :], scalar=shared[3], in1=at,
                                               op0=ALU.mult, op1=ALU.add).then_inc(m["x"], 1)

            def body(i, g, u, first):
                dve.wait_ge(m["t_mm"], g + 1)
                nc.vector.tensor_copy(fix[:, u, :], cols(c.xn, g * G)).then_inc(m["fix"], 1)
                if not first:
                    dve.wait_ge(written[u], i * per_use)
                nc.vector.tensor_copy(index[:, u, :].rearrange("p (k t) -> p k t", k=K),
                                      slots[:, :, bass.ds(g * TG, TG)]).then_inc(m["index"], 1)
                dve.wait_ge(m["t_mm"], g + 3)
                nc.vector.tensor_copy(rows[:, u, :, :].rearrange("p k n -> p (k n)"), c.banks[:, u, :]).then_inc(
                    m["rows"], 1)
                if shared:
                    for j in range(2):
                        dve.wait_ge(m["silu"], g * 2 + (j + 1))
                        dve.wait_ge(m["y_mm"], g + 1)
                        nc.vector.tensor_tensor(hid[:, u, j, :], sil[:, j, :], c.banks[:, 4 + j, :], ALU.mult).then_inc(
                            m["hid"], 1)
                    if u or not first:
                        add_to_x(g - 1)

            peeled(dve, body)
            if shared:
                add_to_x(NG - 1)

        @block.gpsimd
        def _(pool):
            limit = pool.to_reg(last_slot)
            if zeroed:
                pool.wait_ge(c.zeroed, 16 * ZEROING)

            def body(i, g, u):
                pool.wait_ge(m["index"], g + 1)
                pool.wait_ge(m["rows"], g + 3)
                pool.sem_inc(m["go"], 1)
                for t in range(TG):
                    for k in range(K):
                        nc.gpsimd.indirect_dma_start(
                            c.rows_in[:, :], bass.IndirectOffsetOnAxis(index[:, u, k * TG + t:k * TG + t + 1], 0),
                            rows[:, u, t, :], None, bounds_check=limit, oob_is_err=False).then_inc(written[u], 16)

            groups(pool, body)
            for u in range(2):
                pool.wait_ge(written[u], NG // 2 * per_use)


def grouped_ffn(c, tag, NF, groups, weights, loaded=None, fetch=None, meanwhile=None):
    nc = c.nc
    came = c.wb[:, 0:G]
    xt = c.wb[:, G:3 * G].rearrange("p (u n) -> p u n", u=2)
    sil = c.work[:, 0:2 * G].rearrange("p (j n) -> p j n", j=2)
    hid = c.work[:, 2 * G:10 * G].rearrange("p (u j n) -> p u j n", u=2, j=4)
    y = c.work[:, 10 * G:11 * G]
    src, dst = row_groups(c.rows_in), row_groups(c.rows_out)
    TB, YB = c.banks[:, 4, :], c.banks[:, 5, :]
    m = {n: c.sem(f"{tag}_{n}") for n in (
        "came", "t_mm", "xt", "up_mm", "silu",
        "hid",
        "y_mm",
        "y",
        "left")}
    with nc.Block() as block:
        @block.sync
        def _(sp):
            sp.sem_inc(m["left"], 1)

            def load(r):
                sp.dma_start(came, src[:, bass.ds(r, 1), :].rearrange("p g n -> p (g n)")).then_inc(m["came"], 16)

            def store(r):
                sp.wait_ge(m["y"], r + 2)
                sp.dma_start(dst[:, bass.ds(r, 1), :].rearrange("p g n -> p (g n)"), y).then_inc(m["left"], 16)

            def body(r, u, key, before):
                sp.wait_ge(m["t_mm"], r + 1)
                load(r + 1)
                if before is not None:
                    store(r - 1)

            load(0)
            r, u, key = groups(sp, body)
            store(r)
            sp.wait_ge(m["left"], 16 * (r + 1) + 1)
            sp.wait_ge(m["came"], 16 * (r + 2))

        if meanwhile:
            @block.gpsimd
            def _(pool):
                meanwhile(pool)

        if fetch:
            @block.gpsimd
            def _(pool):
                buffers = len(fetch[2])
                for n in range(fetch[0]):
                    if n >= buffers:
                        pool.wait_ge(m["y_mm"], n - buffers + 3)
                    fetch[1](n)
                for v in range(buffers):
                    pool.wait_ge(fetch[2][v], fetch[0] // buffers * 16)

        @block.tensor
        def _(pe):
            start_at_1(pe, m, "y_mm")
            pe.sem_inc(m["y_mm"], 1)

            def transposes(r):
                pe.wait_ge(m["came"], r * 16 + 16)
                for s in range(TG):
                    last = nc.tensor.transpose(TB[:, s * P:(s + 1) * P], came[:, s * P:(s + 1) * P], c.ident[:, :])
                last.then_inc(m["t_mm"], 1)

            def down_of(r, u, key):
                down = weights(key)[2]
                pe.wait_ge(m["y"], r + 1)
                pe.wait_ge(m["hid"], r * NF + (NF + 2))
                for s in range(TG):
                    for j in range(NF):
                        last = nc.tensor.matmul(YB[:, s * P:(s + 1) * P], hid[:, u, j, s * P:(s + 1) * P], down(j),
                                                start=(j == 0), stop=(j == NF - 1))
                last.then_inc(m["y_mm"], 1)

            def body(r, u, key, before):
                gate, up, down = weights(key)
                pe.wait_ge(m["xt"], r + 1)
                if fetch:
                    pe.wait_ge(fetch[2][key[1]], key[0] * 16 + 16)
                for j in range(NF):
                    pe.wait_ge(m["hid"], r * NF + (j + 1))
                    nc.tensor.matmul(c.banks[:, j % 2, :], gate(j), xt[:, u, :], start=True, stop=True)
                    nc.tensor.matmul(c.banks[:, 2 + j % 2, :], up(j), xt[:, u, :], start=True, stop=True).then_inc(
                        m["up_mm"], 1)
                    if j == 1:
                        transposes(r + 1)
                        if before is not None:
                            down_of(r - 1, 1 - u, before)

            transposes(0)
            if loaded:
                pe.wait_ge(*loaded)
            down_of(*groups(pe, body))

        @block.scalar
        def _(act):
            def body(r, u, key, before):
                for j in range(NF):
                    act.wait_ge(m["up_mm"], r * NF + (j + 1))
                    act.wait_ge(m["hid"], r * NF + (j + 1))
                    nc.scalar.activation(sil[:, j % 2, :], c.banks[:, j % 2, :], ACT.Silu).then_inc(m["silu"], 1)

            groups(act, body)

        @block.vector
        def _(dve):
            start_at_1(dve, m, "hid", "y")
            dve.sem_inc(m["hid"], 1)

            def copy_rows(r, u):
                dve.wait_ge(m["t_mm"], r + 1)
                nc.vector.tensor_copy(xt[:, u, :], TB).then_inc(m["xt"], 1)

            def copy_y(r):
                dve.wait_ge(m["y_mm"], r + 3)
                dve.wait_ge(m["left"], r * 16 + 1)
                nc.vector.tensor_copy(y, YB).then_inc(m["y"], 1)

            def body(r, u, key, before):
                for j in range(NF):
                    dve.wait_ge(m["silu"], r * NF + (j + 1))
                    dve.wait_ge(m["y_mm"], r + 1)
                    nc.vector.tensor_tensor(hid[:, u, j, :], sil[:, j % 2, :], c.banks[:, 2 + j % 2, :],
                                            ALU.mult).then_inc(m["hid"], 1)
                    if j == 1:
                        copy_rows(r + 1, 1 - u)
                        if before is not None:
                            copy_y(r - 1)

            copy_rows(0, 0)
            r, u, key = groups(dve, body)
            copy_y(r)


def combine(c, tag, K, last_slot, gate=None):
    nc = c.nc
    got = c.work[:, 0:2 * K * G].rearrange("p (u k t n) -> p u k t n", u=2, k=K, t=TG)
    index = c.index[:, :, 0:TG * K]
    slots = c.slots[:, :, :].rearrange("p t k -> p k t")[:, 0:K, :]
    gates = c.token_gates[:, :, :].rearrange("p t k -> p k t")[:, 0:K, :]
    arrived = [c.sem(f"{tag}_arrived{u}") for u in range(2)]
    m = {n: c.sem(f"{tag}_{n}") for n in ("index", "gated", "summed", "t_mm", "x", "go")}
    per_use = 16 * TG * K
    with nc.Block() as block:
        def groups(engine, body):
            with engine.Fori(0, NG // 2) as i:
                for u in range(2):
                    body(i, i * 2 + u, u)

        @block.gpsimd
        def _(pool):
            limit = pool.to_reg(last_slot)

            def body(i, g, u):
                pool.wait_ge(m["index"], g + 1)
                pool.wait_ge(m["t_mm"], g + 1)
                pool.sem_inc(m["go"], 1)
                for t in range(TG):
                    for k in range(K):
                        nc.gpsimd.indirect_dma_start(
                            got[:, u, k, t, :], None, c.rows_out[:, :],
                            bass.IndirectOffsetOnAxis(index[:, u, k * TG + t:k * TG + t + 1], 0),
                            bounds_check=limit, oob_is_err=False).then_inc(arrived[u], 16)

            groups(pool, body)

        @block.vector
        def _(dve):
            dve.sem_inc(m["x"], 2)

            def make_index(g, u):
                nc.vector.tensor_scalar(index[:, u, :].rearrange("p (k t) -> p k t", k=K),
                                        slots[:, :, bass.ds(g * TG, TG)], float(last_slot), None, ALU.min).then_inc(
                    m["index"], 1)

            def take(i, g, u, more):
                dve.wait_ge(arrived[u], i * per_use + per_use)
                if K == 2:
                    nc.vector.tensor_tensor(got[:, u, :, :, :], got[:, u, :, :, :],
                                            gates[:, :, bass.ds(g * TG, TG)].unsqueeze(3).broadcast_to([P, K, TG, P]),
                                            ALU.mult).then_inc(m["gated"], 1)
                    dve.wait_ge(m["gated"], g + 1)
                    nc.vector.tensor_tensor(got[:, u, 0, :, :], got[:, u, 0, :, :], got[:, u, 1, :, :],
                                            ALU.add).then_inc(m["summed"], 1)
                else:
                    dve.sem_inc(m["summed"], 1)
                if more:
                    make_index(g + 2, u)
                dve.wait_ge(m["t_mm"], g + 3)
                at = cols(c.x, g * G)
                if gate is None:
                    nc.vector.tensor_tensor(at, at, c.banks[:, u, :], ALU.add).then_inc(m["x"], 1)
                else:
                    nc.vector.scalar_tensor_tensor(out=at, in0=c.banks[:, u, :], scalar=gate, in1=at, op0=ALU.mult,
                                                   op1=ALU.add).then_inc(m["x"], 1)

            make_index(0, 0)
            make_index(1, 1)
            with dve.Fori(0, NG // 2 - 1) as i:
                for u in range(2):
                    take(i, i * 2 + u, u, True)
            for u in range(2):
                take(NG // 2 - 1, NG - 2 + u, u, False)

        @block.tensor
        def _(pe):
            pe.sem_inc(m["t_mm"], 2)

            def body(i, g, u):
                pe.wait_ge(m["summed"], g + 1)
                pe.wait_ge(m["x"], g + 1)
                for t in range(TG):
                    last = nc.tensor.transpose(c.banks[:, u, t * P:(t + 1) * P], got[:, u, 0, t, :], c.ident[:, :])
                last.then_inc(m["t_mm"], 1)

            groups(pe, body)

def route_expert_choice(c, tag, layer, top2, keep, bias):
    nc = c.nc
    logits = c.banks[:, 0, :].rearrange("p (t e) -> p t e", e=E)
    flat = "p t e -> p (t e)"
    NQ = NT * E // P
    step, max_ready, exp_ready, score_ready, rows_ready, kept_ready, back_ready = (
        c.sem(tag + n) for n in ("_step", "_max", "_exp", "_score", "_rows", "_kept", "_back"))
    sum_in, sum_out = c.sem(tag + "_sum_in"), c.sem(tag + "_sum_out")
    rows = c.work[:, 0:512].rearrange("p (q b s) -> p q b s", q=NQ, b=2)
    best = c.work[:, 1024:1088]
    iota = c.work[:, 1152:1216]
    first = c.work[:, 1280:1344].bitcast(U32)
    hit = c.work[:, 1408:1408 + 512].rearrange("p (q b s) -> p q b s", q=NQ, b=2)
    orig = c.work[:, 2048:2048 + 512].rearrange("p (q b s) -> p q b s", q=NQ, b=2)
    iota_done, chosen, placed = (c.sem(tag + n) for n in ("_iota", "_chosen", "_placed"))
    with nc.Block() as block:
        @block.gpsimd
        def _(pool):
            nc.gpsimd.iota(c.iota_i[:, :], pattern=[[1, S]], base=0, channel_multiplier=0).then_inc(iota_done, 1)

        @block.vector
        def _(dve):
            link = chain_on(dve, step)
            v = c.t1
            if bias:
                link(nc.vector.tensor_tensor(v[:, :, :], logits, c.bias8[:, :].unsqueeze(1).broadcast_to([P, NT, E]),
                                             ALU.add))
            else:
                link(nc.vector.tensor_copy(v[:, :, :], logits))
            link(nc.vector.tensor_reduce(c.s1[:, :], v[:, :, :], axis=AX.X, op=ALU.max))
            nc.vector.tensor_tensor(v[:, :, :], v[:, :, :], c.s1[:, :].unsqueeze(2).broadcast_to([P, NT, E]),
                                    ALU.subtract).then_inc(max_ready, 1)
            dve.wait_ge(exp_ready, 1)
            link(nc.vector.tensor_reduce(c.s1[:, :], c.t2[:, :, :], axis=AX.X, op=ALU.add))
            link(nc.vector.reciprocal(c.s1[:, :], c.s1[:, :]))
            link(nc.vector.tensor_tensor(c.t3[:, :, :], c.t2[:, :, :],
                                         c.s1[:, :].unsqueeze(2).broadcast_to([P, NT, E]), ALU.mult))
            if top2:
                rank_experts(c, link, c.t3[:, :, :])
                link(nc.vector.tensor_scalar(c.t4[:, :, :], c.rank[:, :, :], 2.0, None, ALU.is_lt))
                link(nc.vector.tensor_tensor(c.t3[:, :, :], c.t3[:, :, :], c.t4[:, :, :], ALU.mult))
                nc.vector.tensor_reduce(c.s1[:, 0:E], c.t3[:, :, :].rearrange("p t e -> p e t"),
                                        axis=AX.X, op=ALU.add).then_inc(sum_in, 1)
                dve.wait_ge(sum_out, 1)
                link(nc.vector.tensor_scalar(c.s1[:, 8:16], c.banks[:, 1, 0:E], 1e-6, None, ALU.add))
                link(nc.vector.reciprocal(c.s1[:, 8:16], c.s1[:, 8:16]))
                link(nc.vector.tensor_tensor(c.t3[:, :, :], c.t3[:, :, :],
                                             c.s1[:, 8:16].unsqueeze(1).broadcast_to([P, NT, E]), ALU.mult))
                link(nc.vector.tensor_scalar(c.t3[:, :, :], c.t3[:, :, :], float(B), None, ALU.mult))
            dve.sem_inc(score_ready, 1)
            dve.wait_ge(rows_ready, 1)
            dve.wait_ge(iota_done, 1)
            link(nc.vector.tensor_copy(iota, c.iota_i[:, :]))
            link(nc.vector.tensor_copy(rows.rearrange("p q b s -> p (q b s)"), c.banks[:, 2, :]))
            link(nc.vector.tensor_copy(orig.rearrange("p q b s -> p (q b s)"), rows.rearrange("p q b s -> p (q b s)")))
            for r in range(keep // 8):
                for q in range(NQ):
                    for b in range(2):
                        k = (q * 2 + b) * 8
                        link(nc.vector.max(best[:, k:k + 8], rows[:, q, b, :]))
                        link(nc.vector.match_replace(rows[:, q, b, :], best[:, k:k + 8], rows[:, q, b, :], -1.0))
            link(nc.vector.tensor_scalar(hit, rows, 0.0, None, ALU.is_lt))
            if keep % 8:
                assert keep % 8 == 1
                for q in range(NQ):
                    for b in range(2):
                        k = (q * 2 + b) * 8
                        link(nc.vector.max(best[:, k:k + 8], rows[:, q, b, :]))
                        link(nc.vector.max_index(first[:, k:k + 8], best[:, k:k + 8], rows[:, q, b, :]))
                        link(nc.vector.tensor_copy(best[:, k:k + 8], first[:, k:k + 8]))
                        link(nc.vector.scalar_tensor_tensor(out=hit[:, q, b, :], in0=iota, scalar=best[:, k:k + 1],
                                                            in1=hit[:, q, b, :], op0=ALU.is_equal, op1=ALU.add))
            if not top2:
                link(nc.vector.tensor_tensor(hit, hit, orig, ALU.mult))
            dve.sem_inc(kept_ready, 1)
            dve.wait_ge(back_ready, 1)
            if top2:
                link(nc.vector.tensor_copy(c.gates[:, :, :].rearrange(flat), c.banks[:, 3, :]))
            else:
                link(nc.vector.tensor_scalar(c.t2[:, :, :].rearrange(flat), c.banks[:, 3, :], 0.0, None, ALU.is_gt))
                nc.vector.tensor_copy(c.m_b[:, :, :], c.t2[:, :, :]).then_inc(chosen, 1)
                dve.wait_ge(placed, 1)
                link(nc.vector.scalar_tensor_tensor(out=c.t1[:, :, :].rearrange(flat), in0=c.banks[:, 4, :], scalar=1.0,
                                                    in1=c.t2[:, :, :].rearrange(flat), op0=ALU.add, op1=ALU.mult))
                link(nc.vector.tensor_scalar(c.t1[:, :, :], c.t1[:, :, :], -1.0, None, ALU.add))
                link(nc.vector.tensor_copy(c.t3[:, 0:3, :].rearrange("p t e -> p (t e)"), iota[:, 0:3 * E]))
                link(nc.vector.tensor_scalar(c.gates[:, :, :].rearrange(flat), c.banks[:, 3, :],
                                             c.tanh_g[:, 4 + layer:5 + layer], None, ALU.mult))

        @block.scalar
        def _(act):
            act.wait_ge(max_ready, 1)
            nc.scalar.activation(c.t2[:, :, :], c.t1[:, :, :], ACT.Exp).then_inc(exp_ready, 1)

        @block.tensor
        def _(pe):
            if top2:
                pe.wait_ge(sum_in, 1)
                nc.tensor.matmul(c.banks[:, 1, 0:E], c.same_pos[:, :], c.s1[:, 0:E],
                                 start=True, stop=True).then_inc(sum_out, 1)
            pe.wait_ge(score_ready, 1)
            t3 = c.t3[:, :, :].rearrange(flat)
            for q in range(NQ):
                last = nc.tensor.transpose(c.banks[:, 2, q * P:(q + 1) * P], t3[:, q * P:(q + 1) * P], c.ident[:, :])
            last.then_inc(rows_ready, 1)
            pe.wait_ge(kept_ready, 1)
            hits = c.work[:, 1408:1408 + 512]
            for q in range(NQ):
                last = nc.tensor.transpose(c.banks[:, 3, q * P:(q + 1) * P], hits[:, q * P:(q + 1) * P], c.ident[:, :])
            last.then_inc(back_ready, 1)
            if not top2:
                pe.wait_ge(chosen, 1)
                nc.tensor.matmul(c.banks[:, 4, :], c.before_seq[:, :], c.m_b[:, :, :].rearrange(flat),
                                 start=True, stop=True).then_inc(placed, 1)


def chosen_ffn(c, tag, pos, number, weights, loaded):
    nc = c.nc
    w1, w2, b1, b2 = weights
    J, CH = L1_KEEP, 8
    R, HR, N = E * J, E * J // 2, 2 * CH * J
    NC = NT // CH
    size = 2 * CH * R
    xg = c.wa[:, 0:2 * size].rearrange("p (u s e j) -> p u s e j", u=2, s=2 * CH, e=E)
    yt = c.wa[:, 2 * size:4 * size].rearrange("p (u s e j) -> p u s e j", u=2, s=2 * CH, e=E)
    hid = c.wa[:, 4 * size:4 * size + 8 * N].rearrange("p (u j n) -> p u j n", u=2, j=4)
    at = [0]

    def take(n):
        at[0] += n
        return c.work[:, at[0] - n:at[0]]

    fix = take(2 * G).rearrange("p (u n) -> p u n", u=2)
    xt = take(2 * P).rearrange("p (u n) -> p u n", u=2)
    sel = take(2 * R).rearrange("p (u e j) -> p u e j", u=2, e=E)
    hot = take(R).rearrange("p (e j) -> p e j", e=E)
    gated = take(2 * R).rearrange("p (u e j) -> p u e j", u=2, e=E)
    back = take(4 * P)[0:HR, :].rearrange("p (u h n) -> p u h n", u=2, h=2)
    ys = take(8 * P)[0:HR, :].rearrange("p (u b h n) -> p u b h n", u=2, b=2, h=2)
    YB, OB, TB, XB, ZB = c.banks[:, 2, 0:N], c.banks[:, 3, 0:P], c.banks[:, 4, :], c.banks[:, 5:7, 0:R], c.banks[:, 7, :]
    m = {n: c.sem(f"{tag}_{n}") for n in (
        "fix",
        "t_mm",
        "t_used",
        "sel", "x_mm",
        "x_used",
        "hot", "gated",
        "up_mm", "hid",
        "y_mm",
        "y",
        "z_mm",
        "z_used",
        "o_mm",
        "o_used")}
    flat_pos = pos.rearrange("p t e -> p (t e)")
    flat_gates = c.gates[:, :, :].rearrange("p t e -> p (t e)")

    def steps(engine, step):
        for k in range(CH):
            step(-1, k, 1, "D")
        for k in range(CH):
            step(0, k, 0, "DF")
        with engine.Fori(0, NC // 2 - 1) as i:
            for q in range(2):
                for k in range(CH):
                    step(i * 2 + (1 + q), k, 1 - q, "DFC")
        for k in range(CH):
            step(NC - 1, k, 1, "FC")
        for k in range(CH):
            step(NC, k, 0, "C")

    with nc.Block() as block:
        @block.tensor
        def _(pe):
            start_at_1(pe, m, "t_mm", "z_mm", "x_mm", "y_mm", "o_mm")
            start_at_1(pe, m, "x_mm", "y_mm", "o_mm")
            pe.wait_ge(*loaded)

            def step(ch, k, par, stages):
                n, u = ch * CH + k, k % 2

                def up(j):
                    pe.wait_ge(m["hid"], n * 4 + (j + 1))
                    nc.tensor.matmul(c.banks[:, j % 2, 0:N].rearrange("p (s j) -> p s j", j=J),
                                     w1[:, k, j * P:(j + 1) * P], xg[:, par, :, k, :],
                                     start=True, stop=True).then_inc(m["up_mm"], 1)

                if "F" in stages:
                    if k == 0:
                        pe.wait_ge(m["x_used"], n + 9)
                    up(0)
                    up(1)
                pe.wait_ge(m["t_used"], n + 9)
                if "D" in stages:
                    if k % TG == 0:
                        pe.wait_ge(m["fix"], ch * 2 + (3 + k // TG))
                    last = nc.tensor.transpose(TB[:, 0:P], fix[:, k // TG, (k % TG) * P:(k % TG + 1) * P], c.ident[:, :])
                if "C" in stages:
                    pe.wait_ge(m["gated"], n - 6)
                    for h in range(2):
                        last = nc.tensor.transpose(
                            TB[0:HR, (1 + h) * P:(2 + h) * P],
                            gated[:, u, :, :].rearrange("p e j -> p (e j)")[:, h * HR:(h + 1) * HR], c.ident[:, :])
                last.then_inc(m["t_mm"], 1)
                if "C" in stages:
                    if k == 0:
                        pe.wait_ge(m["y"], n + 1)
                    pe.wait_ge(m["z_used"], n - 7)
                    for b in range(2):
                        for h in range(2):
                            last = nc.tensor.transpose(
                                ZB[0:HR, (2 * b + h) * P:(2 * b + h + 1) * P],
                                yt[:, 1 - par, 2 * k + b, :, :].rearrange("p e j -> p (e j)")[:, h * HR:(h + 1) * HR],
                                c.ident[:, :])
                    last.then_inc(m["z_mm"], 1)
                if "F" in stages:
                    up(2)
                    up(3)
                if "D" in stages:
                    pe.wait_ge(m["t_used"], n + 10)
                    pe.wait_ge(m["sel"], n + 9)
                    pe.wait_ge(m["x_used"], n + 9)
                    for b in range(2):
                        rows = slice(S * b, S * b + S)
                        last = nc.tensor.matmul(XB[:, b, :], xt[rows, u, :],
                                                sel[rows, u, :, :].rearrange("p e j -> p (e j)"), start=True, stop=True)
                    last.then_inc(m["x_mm"], 1)
                if "C" in stages:
                    pe.wait_ge(m["t_used"], n + 10)
                    pe.wait_ge(m["z_used"], n - 6)
                    pe.wait_ge(m["o_used"], n - 7)
                    for b in range(2):
                        for h in range(2):
                            last = nc.tensor.matmul(OB[:, S * b:S * b + S], ys[:, u, b, h, :],
                                                    back[:, u, h, S * b:S * b + S], start=(h == 0), stop=(h == 1))
                    last.then_inc(m["o_mm"], 1)
                if "F" in stages:
                    pe.wait_ge(m["hid"], n * 4 + 6)
                    pe.wait_ge(m["y"], n + 1)
                    for j in range(4):
                        last = nc.tensor.matmul(YB, w2[:, k, j, :], hid[:, u, j, :], start=(j == 0), stop=(j == 3))
                    last.then_inc(m["y_mm"], 1)

            steps(pe, step)

        @block.scalar
        def _(act):
            act.wait_ge(*loaded)
            act.sem_inc(m["hid"], 2)
            act.sem_inc(m["z_used"], 1)

            def step(ch, k, par, stages):
                n, u = ch * CH + k, k % 2

                def gelu(j):
                    act.wait_ge(m["up_mm"], n * 4 + (j + 1))
                    if j == 0:
                        act.wait_ge(m["y_mm"], n + 1)
                    nc.scalar.activation(hid[:, u, j, :], c.banks[:, j % 2, 0:N], ACT.Gelu,
                                         bias=b1[:, k, j:j + 1]).then_inc(m["hid"], 1)

                if "D" in stages and k % TG == 0:
                    act.wait_ge(m["t_mm"], n + 9)
                    nc.scalar.activation(fix[:, k // TG, :], cols(c.xn, ch * (2 * G) + (2 + k // TG) * G),
                                         ACT.Copy).then_inc(m["fix"], 1)
                if "F" in stages:
                    gelu(0)
                    gelu(1)
                if "C" in stages:
                    act.wait_ge(m["z_mm"], n - 6)
                    act.wait_ge(m["o_mm"], n - 7)
                    nc.scalar.activation(ys[:, u, :, :, :].rearrange("p b h n -> p (b h n)"), ZB[0:HR, :],
                                         ACT.Copy).then_inc(m["z_used"], 1)
                if "F" in stages:
                    gelu(2)
                    gelu(3)

            steps(act, step)

        @block.vector
        def _(dve):
            start_at_1(dve, m, "t_used", "x_used", "y", "o_used", "gated")
            dve.wait_ge(*loaded)
            places = number.unsqueeze(1).broadcast_to([P, E, J])

            def is_place(out, tile):
                return nc.vector.tensor_tensor(out, flat_pos[:, bass.ds(tile * E, E)].unsqueeze(2).broadcast_to([P, E, J]),
                                               places, ALU.is_equal)

            def keep_output(ch, k, par, stages):
                n = ch * CH + k
                dve.wait_ge(m["y_mm"], n + 3)
                if k == 0 and "C" in stages:
                    dve.wait_ge(m["z_mm"], n - 7)
                nc.vector.tensor_scalar(yt[:, par, :, k, :], YB.rearrange("p (s j) -> p s j", j=J), b2[:, k:k + 1],
                                        None, ALU.add).then_inc(m["y"], 1)

            def step(ch, k, par, stages):
                n, u = ch * CH + k, k % 2
                if "D" in stages:
                    dve.wait_ge(m["x_mm"], n + 9)
                    is_place(sel[:, u, :, :], n + CH).then_inc(m["sel"], 1)
                if "C" in stages:
                    dve.wait_ge(m["gated"], n - 7)
                    is_place(hot, n - CH).then_inc(m["hot"], 1)
                    dve.wait_ge(m["hot"], n - 7)
                    dve.wait_ge(m["t_mm"], n + 8)
                    nc.vector.tensor_tensor(gated[:, u, :, :], hot,
                                            flat_gates[:, bass.ds(n * E - CH * E, E)].unsqueeze(2).broadcast_to([P, E, J]),
                                            ALU.mult).then_inc(m["gated"], 1)
                if k > 0 and "F" in stages:
                    keep_output(ch, k - 1, par, stages)
                if k == 0 and "C" in stages:
                    keep_output(ch - 1, CH - 1, 1 - par, stages)
                dve.wait_ge(m["t_mm"], n + 10)
                if "D" in stages:
                    last = nc.vector.tensor_copy(xt[:, u, :], TB[:, 0:P])
                if "C" in stages:
                    dve.wait_ge(m["o_mm"], n - 7)
                    last = nc.vector.tensor_copy(back[:, u, :, :].rearrange("p h n -> p (h n)"), TB[0:HR, P:3 * P])
                last.then_inc(m["t_used"], 1)
                if "D" in stages:
                    dve.wait_ge(m["x_mm"], n + 11)
                    if k == 0 and "C" in stages:
                        dve.wait_ge(m["up_mm"], n * 4)
                    nc.vector.tensor_copy(xg[:, 1 - par, 2 * k:2 * k + 2, :, :].rearrange("p s e j -> p s (e j)"),
                                          XB).then_inc(m["x_used"], 1)
                if "C" in stages:
                    dve.wait_ge(m["o_mm"], n - 5)
                    x = cols(c.x, n * P - CH * P, P)
                    nc.vector.tensor_tensor(x, x, OB, ALU.add).then_inc(m["o_used"], 1)

            steps(dve, step)

def context_sums(c, tag, ctxT):
    nc = c.nc
    cb = c.work[:, 11 * G:13 * G].rearrange("p (u n) -> p u n", u=2)
    sq = c.work[:, 13 * G:14 * G]
    rows = sq.rearrange("p (b s) -> p b s", s=S)
    halves = [S >> k for k in range(1, S.bit_length())]
    ctx_in = [c.sem(f"{tag}_ctx_in{u}") for u in range(2)]
    m = {n: c.sem(f"{tag}_{n}") for n in (
        "relu",
        "square", "fold",
        "sum",
        "go")}

    def gpsimd_work(pool):
        start_at_1(pool, m, "relu", "sum")
        with pool.Fori(0, NG // 2) as i:
            for u in range(2):
                pool.wait_ge(m["sum"], i * 2 + 1)
                pool.sem_inc(m["go"], 1)
                pool.dma_start(cb[:, u, :], cols(ctxT, i * (2 * G) + u * G)).then_inc(ctx_in[u], 16)
            for u in range(2):
                g = i * 2 + u
                pool.wait_ge(ctx_in[u], i * 16 + 16)
                pool.wait_ge(m["sum"], g + 1)
                pool.sem_inc(m["go"], 1)
                nc.gpsimd.tensor_scalar(sq, cb[:, u, :], 0.0, None, ALU.max).then_inc(m["relu"], 1)
                pool.wait_ge(m["relu"], g + 2)
                nc.gpsimd.tensor_tensor(sq, sq, cb[:, u, :], ALU.mult).then_inc(m["square"], 1)
                pool.wait_ge(m["square"], g + 1)
                for k, half in enumerate(halves):
                    nc.gpsimd.tensor_tensor(rows[:, :, 0:half], rows[:, :, 0:half], rows[:, :, half:2 * half],
                                            ALU.add).then_inc(m["fold"], 1)
                    pool.wait_ge(m["fold"], g * len(halves) + (k + 1))
                nc.gpsimd.tensor_copy(c.work[:, bass.ds(i * (2 * BG) + (SUMS_AT + u * BG), BG)],
                                      rows[:, :, 0]).then_inc(m["sum"], 1)

    return gpsimd_work


def windowed_product(c, tag):
    nc = c.nc
    y = c.work[:, 0:2 * G].rearrange("p (u n) -> p u n", u=2)
    product, added = c.sem(tag + "_product"), c.sem(tag + "_added")
    with nc.Block() as block:
        @block.vector
        def _(dve):
            dve.sem_inc(added, 2)

            def multiply(g, u):
                dve.wait_ge(added, g + 1)
                nc.vector.scalar_tensor_tensor(
                    out=y[:, u, :].rearrange("p (b s) -> p b s", s=S),
                    in0=cols(c.xn, g * G).rearrange("p (b s) -> p b s", s=S), scalar=0.0,
                    in1=c.work[:, bass.ds(g * BG + SUMS_AT, BG)].unsqueeze(2).broadcast_to([P, BG, S]),
                    op0=ALU.max, op1=ALU.mult).then_inc(product, 1)

            def add_to_x(g, u):
                dve.wait_ge(product, g + 1)
                x = cols(c.x, g * G)
                nc.vector.scalar_tensor_tensor(out=x, in0=y[:, u, :], scalar=c.tanh_g[:, 1:2], in1=x,
                                               op0=ALU.mult, op1=ALU.add).then_inc(added, 1)

            multiply(0, 0)
            with dve.Fori(0, NG // 2 - 1) as i:
                for u in range(2):
                    multiply(i * 2 + (u + 1), 1 - u)
                    add_to_x(i * 2 + u, u)
            multiply(NG - 1, 1)
            add_to_x(NG - 2, 0)
            add_to_x(NG - 1, 1)


def attention(c, tag, ctxT, scale, gate, bq=None, bk=None, bv=None, bo=None):
    nc = c.nc
    wq, wk, wv, wo = (c.attn_w[:, k, :] for k in range(4))
    cbf = c.wb[:, 0:2048].rearrange("p (u n) -> p u n", u=2)
    cb = c.wb[:, 0:2048].rearrange("p (u b two s) -> p u b two s", u=2, b=BG, two=2)
    kb = c.wb[:, 2048:6144].rearrange("p (u j n) -> p u j n", u=2, j=4)
    qs = c.wb[:, 6144:7168].rearrange("p (u n) -> p u n", u=2)
    ot = c.wb[:, 7168:8192].rearrange("p (u n) -> p u n", u=2)
    pr = c.work[:, 0:2048].rearrange("p (u n) -> p u n", u=2)
    pt = c.work[:, 2048:4096].rearrange("p (u n) -> p u n", u=2)
    vb = c.work[:, 4096:4096 + 2 * 288].rearrange("p (u a n) -> p u a n", u=2, a=16)
    on = c.work[:, 4800:5056].rearrange("p (u n) -> p u n", u=2)
    rd = c.work[:, 5056:5072]
    nm = c.work[:, 5072:5104].rearrange("p (u h) -> p u h", u=2)
    add = c.work[:, 5120:5632]
    VBANK, OBANK = c.banks[:, 6, :], c.banks[:, 7, :]

    def values_of(u):
        return vb[:, u, :, :].rearrange("p (b i) n -> p b i n", b=2)

    def scores(u):
        return c.banks[:, 2 * u:2 * u + 2, :]

    ctx_in = [c.sem(f"{tag}_ctx_in{p}") for p in range(2)]
    names = ("prep", "mask_fix", "q_mm", "k_mm", "q_done", "k_done", "s_order", "s_mm", "nm_done", "sub_done", "v_mm",
             "v_used", "p_done", "t_mm", "t_used", "av_mm", "rd_done", "on_done", "ot_mm", "ot_done", "wo_mm", "add_done",
             "x_done")
    m = {n: c.sem(f"{tag}_{n}") for n in names}
    PAIRS = NG // 2

    def slots(engine, slot):
        with engine.Fori(0, PAIRS - 1) as i:
            for p in range(2):
                for k in range(TG):
                    slot(i * 2 + p, p, k, True, True)
        for p in range(2):
            for k in range(TG):
                slot(NG - 2 + p, p, k, p == 0, p == 0 or k < 2)

    with nc.Block() as block:
        @block.sync
        def _(sp):
            def load(g, p):
                for two in range(2):
                    sp.dma_start(cb[:, p, :, two, :], cols(ctxT, g * G).rearrange("p (b s) -> p b s", s=S)).then_inc(
                        ctx_in[p], 16)

            load(0, 0)
            load(1, 1)
            with sp.Fori(1, PAIRS) as i:
                for p in range(2):
                    sp.wait_ge(m["v_mm"], i * 8 + (4 * p - 4) + 1)
                    load(i * 2 + p, p)

        @block.gpsimd
        def _(pool):
            start_at_1(pool, m, "mask_fix")
            def fix(g, p):
                nc.gpsimd.tensor_copy(c.mrow_fix[0:3, p, :], c.mrow[0:3, bass.ds(g * G, G)]).then_inc(m["mask_fix"], 1)

            fix(0, 0)
            fix(1, 1)
            with pool.Fori(1, PAIRS) as i:
                for p in range(2):
                    pool.wait_ge(m["s_mm"], i * 8 + (4 * p - 4) + 1)
                    fix(i * 2 + p, p)

        @block.tensor
        def _(pe):
            start_at_1(pe, m, "k_mm", "q_mm", "s_order", "s_mm", "v_mm", "ot_mm", "wo_mm", "t_mm", "av_mm")
            pe.wait_ge(m["prep"], 2)

            def make_keys(g, p, loads):
                pe.wait_ge(ctx_in[p], loads)
                nc.tensor.matmul(VBANK.rearrange("p (b s) -> p b s", s=S), wk, cb[:, p, :, 0, :],
                                 start=True, stop=True).then_inc(m["k_mm"], 1)

            def make_queries(g):
                nc.tensor.matmul(VBANK, wq, cols(c.xn, g * G), start=True, stop=True).then_inc(m["q_mm"], 1)

            def put_mask(g, p, k):
                u, n, tok = k % 2, g * TG + k, k * P
                if k == 0:
                    pe.wait_ge(m["mask_fix"], g + 2)
                pe.wait_ge(m["sub_done"], n + 2)
                for w in range(2):
                    for b in range(2):
                        last = nc.tensor.matmul(
                            scores(u)[S * b:S * b + S, w, :].rearrange("p (h k) -> p h k", h=8), c.ones[0:3, 0:S],
                            c.mrow_fix[0:3, p, tok + S * b:tok + S * b + S].unsqueeze(1).broadcast_to([3, 8, S]),
                            start=True, stop=False)
                last.then_inc(m["s_order"], 1)

            def add_scores(g, p, k, w):
                u, n, tok = k % 2, g * TG + k, k * P
                if k == 0 and w == 0:
                    pe.wait_ge(m["k_done"], g * 4 + 4 + 1)
                    pe.wait_ge(m["q_done"], g + 2)
                pe.wait_ge(m["s_order"], n * 2 + (w + 2))
                for r in (w, 2 + w):
                    for b in range(2):
                        rows = slice(32 * r, 32 * r + 32)
                        last = nc.tensor.matmul(
                            scores(u)[S * b:S * b + S, r // 2, w * 256:w * 256 + 256].rearrange("p (j k) -> p j k", j=4),
                            qs[rows, p, tok + S * b:tok + S * b + S], kb[rows, p, :, tok + S * b:tok + S * b + S],
                            start=False, stop=(w == 1))
                last.then_inc(m["s_mm"] if w else m["s_order"], 1)

            def make_values(p, k):
                for b in range(2):
                    last = nc.tensor.matmul(VBANK[:, b * P:(b + 1) * P], cbf[:, p, (2 * k + b) * P:(2 * k + b + 1) * P],
                                            wv, start=True, stop=True)
                last.then_inc(m["v_mm"], 1)

            def transpose_out(n, u):
                pe.wait_ge(m["on_done"], n + 2)
                nc.tensor.transpose(OBANK[:, 384:512], on[:, u, :], c.ident[:, :]).then_inc(m["ot_mm"], 1)

            def project_out(p):
                nc.tensor.matmul(VBANK, wo, ot[:, p, :], start=True, stop=True).then_inc(m["wo_mm"], 1)

            def slot(g, p, k, more, ahead):
                u, n = k % 2, g * TG + k
                ahead_of = (g + (k + 2) // TG, (p + (k + 2) // TG) % 2, (k + 2) % TG)
                pe.wait_ge(m["p_done"], n + 2)
                for w in range(2):
                    pe.wait_ge(m["t_used"], n * 2 + (w + 1) + 1)
                    for i in range(4):
                        last = nc.tensor.transpose(c.banks[:, 4 + w, i * P:(i + 1) * P],
                                                   pr[:, u, (4 * w + i) * P:(4 * w + i + 1) * P], c.ident[:, :])
                    last.then_inc(m["t_mm"], 1)
                if ahead:
                    put_mask(*ahead_of)
                if k == 0 and more:
                    pe.wait_ge(m["v_used"], n + 2)
                    make_keys(g + 1, 1 - p, g * 16 + (48 if p else 32))
                if k == 1 and more:
                    pe.wait_ge(m["v_used"], n + 2)
                    make_queries(g + 1)
                if k == 2:
                    pe.wait_ge(m["v_used"], n + 2)
                    pe.wait_ge(m["ot_done"], g * TG + 2)
                    project_out(1 - p)
                transpose_out(n, 1 - u)
                if ahead:
                    add_scores(*ahead_of, 0)
                pe.wait_ge(m["ot_done"], n + 2)
                pe.wait_ge(m["v_used"], n + 2)
                pe.wait_ge(m["t_used"], n * 2 + (0 + 3) + 1)
                for i in range(4 * 0, 4 * 0 + 4):
                    last = nc.tensor.matmul(OBANK[:, i * 36:i * 36 + 36].rearrange("p (b n) -> p b n", b=2),
                                            pt[:, u, i * P:(i + 1) * P], values_of(u)[:, :, i, :],
                                            start=True, stop=True)
                if ahead:
                    add_scores(*ahead_of, 1)
                pe.wait_ge(m["t_used"], n * 2 + (1 + 3) + 1)
                for i in range(4 * 1, 4 * 1 + 4):
                    last = nc.tensor.matmul(OBANK[:, i * 36:i * 36 + 36].rearrange("p (b n) -> p b n", b=2),
                                            pt[:, u, i * P:(i + 1) * P], values_of(u)[:, :, i, :],
                                            start=True, stop=True)
                last.then_inc(m["av_mm"], 1)

                if more or k + 1 < TG:
                    if k == 0 and more:
                        pe.wait_ge(m["k_done"], g * 4 + 8 + 1)
                    elif k == 1 and more:
                        pe.wait_ge(m["q_done"], g + 2 + 1)
                    elif k == 2:
                        pe.wait_ge(m["add_done"], g + 2)
                    else:
                        pe.wait_ge(m["v_used"], n + 2)
                    make_values((p + (k + 1) // TG) % 2, (k + 1) % TG)

            make_keys(0, 0, 32)
            pe.wait_ge(m["k_done"], 5)
            make_queries(0)
            pe.wait_ge(m["q_done"], 2)
            make_values(0, 0)
            for k in range(2):
                put_mask(0, 0, k)
                add_scores(0, 0, k, 0)
                add_scores(0, 0, k, 1)
            slots(pe, slot)
            transpose_out(NT, 1)
            pe.wait_ge(m["ot_done"], NT + 2)
            pe.wait_ge(m["v_used"], NT + 1)
            project_out(1)

        @block.vector
        def _(dve):
            start_at_1(dve, m, "prep", "on_done", "sub_done", "k_done", "nm_done", "v_used", "rd_done", "x_done")
            nc.vector.tensor_copy(vb[:, 0, :, 16:18], c.half[:, :].unsqueeze(1).broadcast_to([P, 16, 2]))
            nc.vector.memset(on[:, 1, :], 0.0)
            nc.vector.memset(ot[:, 1, :], 0.0)
            nc.vector.tensor_copy(vb[:, 1, :, 16:18], c.half[:, :].unsqueeze(1).broadcast_to([P, 16, 2])).then_inc(
                m["prep"], 1)
            dve.wait_ge(m["prep"], 2)
            dve.sem_inc(m["on_done"], 1)
            dve.sem_inc(m["sub_done"], 2)

            def expand_keys(g, p):
                dve.wait_ge(m["k_mm"], g + 2)
                for j in range(4):
                    nc.vector.tensor_scalar(kb[:, p, j, :], VBANK, bk, c.quad[:, j:j + 1], ALU.add,
                                            ALU.mult).then_inc(m["k_done"], 1)

            def soften(n, u):
                dve.wait_ge(m["s_mm"], n + 2)
                s3 = scores(u).rearrange("p w (h k) -> p (w h) k", k=S)
                nc.vector.tensor_reduce(nm[:, u, :], s3, axis=AX.X, op=ALU.max).then_inc(m["nm_done"], 1)
                dve.wait_ge(m["nm_done"], n + 2)
                nc.vector.tensor_tensor(pr[:, u, :].rearrange("p (h k) -> p h k", k=S), s3,
                                        nm[:, u, :].unsqueeze(2).broadcast_to([P, H, S]),
                                        ALU.subtract).then_inc(m["sub_done"], 1)

            def keep_values(n, u):
                dve.wait_ge(m["v_mm"], n + 2)
                nc.vector.tensor_tensor(vb[:, u, :, 0:16], VBANK[:, 0:256].rearrange("p (a n) -> p a n", n=16),
                                        c.half16[:, :, :].rearrange("p j d -> p (j d)").unsqueeze(1).broadcast_to(
                                            [P, 16, 16]), ALU.mult).then_inc(m["v_used"], 1)

            def normalise(n, u):
                dve.wait_ge(m["av_mm"], n + 2)
                dve.wait_ge(m["on_done"], n + 2)
                o = [OBANK[S * b:S * b + S, 0:288].rearrange("p (i b n) -> p i b n", b=2, n=18)[:, :, b, :]
                     for b in range(2)]
                for b in range(2):
                    last = nc.vector.reciprocal(rd[S * b:S * b + S, :].rearrange("p (i j) -> p i j", j=2),
                                                o[b][:, :, 16:18])
                last.then_inc(m["rd_done"], 1)
                dve.wait_ge(m["rd_done"], n + 2)
                for b in range(2):
                    rows = slice(S * b, S * b + S)
                    last = nc.vector.tensor_tensor(
                        on[rows, u, :].rearrange("p (i j d) -> p i j d", i=8, j=2),
                        o[b][:, :, 0:16].rearrange("p i (j d) -> p i j d", j=2),
                        rd[rows, :].rearrange("p (i j) -> p i j", j=2).unsqueeze(3).broadcast_to([S, 8, 2, HD]),
                        ALU.mult)
                last.then_inc(m["on_done"], 1)

            def slot(g, p, k, more, ahead):
                u, n = k % 2, g * TG + k
                if k == 0 and more:
                    expand_keys(g + 1, 1 - p)
                if ahead:
                    dve.wait_ge(m["t_mm"], n * 2 + 2 + 1)
                    soften(n + 2, u)
                if more or k + 1 < TG:
                    keep_values(n + 1, 1 - u)
                normalise(n, u)
                if k == 2:
                    add_to_x(g - 1, g)

            def add_to_x(g, count):
                dve.wait_ge(m["add_done"], count + 2)
                at = cols(c.xpad, (g + 1) * G)
                nc.vector.tensor_tensor(at, at, add, ALU.add).then_inc(m["x_done"], 1)

            expand_keys(0, 0)
            keep_values(0, 0)
            soften(0, 0)
            soften(1, 1)
            slots(dve, slot)
            add_to_x(NG - 1, NG)

        @block.scalar
        def _(act):
            start_at_1(act, m, "t_used", "p_done", "q_done", "ot_done", "add_done")
            act.sem_inc(m["t_used"], 2)

            def exps(n, u):
                act.wait_ge(m["sub_done"], n + 3 + 1)
                nc.scalar.activation(pr[:, u, :], pr[:, u, :], ACT.Exp).then_inc(m["p_done"], 1)

            def queries(g, p):
                act.wait_ge(m["q_mm"], g + 2)
                nc.scalar.activation(qs[:, p, :], VBANK, ACT.Identity, bias=bq, scale=scale).then_inc(m["q_done"], 1)

            def copies(n, u):
                for w in range(2):
                    act.wait_ge(m["t_mm"], n * 2 + (w + 1) + 1)
                    nc.scalar.activation(pt[:, u, w * G:(w + 1) * G], c.banks[:, 4 + w, :], ACT.Copy).then_inc(
                        m["t_used"], 1)

            def copy_out(n, p, k):
                act.wait_ge(m["ot_mm"], n + 2)
                nc.scalar.activation(ot[:, p, k * P:(k + 1) * P], OBANK[:, 384:512], ACT.Identity, bias=bv).then_inc(
                    m["ot_done"], 1)

            def evacuate_out(g):
                act.wait_ge(m["wo_mm"], g + 2)
                act.wait_ge(m["x_done"], g + 1)
                nc.scalar.activation(add, VBANK, ACT.Identity, bias=bo, scale=gate).then_inc(m["add_done"], 1)

            def slot(g, p, k, more, ahead):
                u, n = k % 2, g * TG + k
                copies(n, u)
                copy_out(n, (p + 1) % 2 if k == 0 else p, (k - 1) % TG)
                if k == 1 and more:
                    queries(g + 1, 1 - p)
                if k == 2:
                    evacuate_out(g)
                if ahead:
                    exps(n + 2, u)

            act.wait_ge(m["prep"], 2)
            queries(0, 0)
            exps(0, 0)
            exps(1, 1)
            slots(act, slot)
            copy_out(NT, 1, TG - 1)
            evacuate_out(NG)


def prepare_attention(c, tag, A, layer, block_diagonal, biases, mask, kind):
    nc = c.nc
    cleared, got, step, mask_in, made, moved = (
        c.sem(tag + n) for n in ("_w_cleared", "_w_in", "_w_step", "_mask_in", "_mask_made", "_mask_moved"))
    scale = HD ** -0.5 if not block_diagonal else P ** -0.5
    col = c.attn_b
    raw = c.wb[:, 0:64].bitcast(I32) if kind == "zero_is_off" else c.wb[:, 0:64]
    val, rest, back = c.wb[:, 64:128], c.wb[:, 128:192], c.wb[:, 320:384]
    part = [c.wb[:, 192 + 32 * k:224 + 32 * k].bitcast(BF16) for k in range(3)]
    loads = []
    for k, w in enumerate(("Wq", "Wk", "Wv", "Wo")):
        src = A[f"L{layer}_xattn_{w}T"]
        if block_diagonal and w != "Wo":
            loads += [(c.attn_w[h * HD:(h + 1) * HD, k, h * HD:(h + 1) * HD], src) for h in range(H)]
        else:
            loads.append((c.attn_w[:, k, :], src))
    loads += [(col[:, k:k + 1], A[b].unsqueeze(1)) for k, b in enumerate(biases) if b is not None]

    def sync_work(sp):
        sp.dma_start(raw, mask).then_inc(mask_in, 16)
        sp.wait_ge(cleared, 2)
        for dst, src in loads:
            sp.dma_start(dst, src).then_inc(got, 16)
        sp.wait_ge(made, 1)
        for k in range(3):
            sp.dma_start(c.mrow[k:k + 1, :], part[k]).then_inc(moved, 16)
        sp.wait_ge(moved, 48)

    def gpsimd_work(pool):
        link = chain_on(pool, step)
        nc.gpsimd.memset(c.attn_w[:, :, :], 0.0).then_inc(cleared, 1)
        nc.gpsimd.memset(col[:, :], 0.0).then_inc(cleared, 1)
        pool.wait_ge(mask_in, 16)
        if kind == "zero_is_off":
            link(nc.gpsimd.tensor_scalar(val, raw, 0.0, -1e20 * scale, ALU.is_equal, ALU.mult))
        else:
            link(nc.gpsimd.tensor_scalar(val, raw, -1e9, None, ALU.mult))
        link(nc.gpsimd.tensor_copy(part[0], val))
        link(nc.gpsimd.tensor_copy(back, part[0]))
        link(nc.gpsimd.tensor_tensor(rest, val, back, ALU.subtract))
        link(nc.gpsimd.tensor_copy(part[1], rest))
        link(nc.gpsimd.tensor_copy(back, part[1]))
        link(nc.gpsimd.tensor_tensor(rest, rest, back, ALU.subtract))
        nc.gpsimd.tensor_copy(part[2], rest).then_inc(made, 1)
        pool.wait_ge(got, 16 * len(loads))
        link(nc.gpsimd.tensor_scalar(col[:, 0:1], col[:, 0:1], scale, None, ALU.mult))
        link(nc.gpsimd.tensor_tensor(col[:, 3:4], col[:, 3:4], c.tanh_g[:, layer:layer + 1], ALU.mult))

    return sync_work, gpsimd_work


def two_way_attention(c, tag, A, ctxT, ctx_tiles):
    nc = c.nc
    wl = c.attn_w
    col = c.cols16
    cb = c.wa[:, 0:2 * G].rearrange("p (u n) -> p u n", u=2)
    ctq = c.wa[:, 2 * G:4 * G].rearrange("q (u k d) -> q u k d", u=2, k=TG)
    ident16 = c.wa[:, 4 * G:4 * G + 64].bitcast(BF16)
    apart = c.wa[:, 4 * G + 64:4 * G + 128].bitcast(BF16)
    cc = c.wa[:, 6 * G:8 * G].rearrange("p (u n) -> p u n", u=2)
    xg = c.wa[:, 8 * G:10 * G].rearrange("p (u n) -> p u n", u=2)
    at = c.wa[:, 10 * G:12 * G].rearrange("p (u n) -> p u n", u=2)
    a = c.wa[:, 12 * G:14 * G].rearrange("p (u k q) -> p u k q", u=2, k=TG)
    ml = c.work[:, 3584:3592].rearrange("p (u k) -> p u k", u=2)
    sm = c.work[:, 3592:3600].rearrange("p (u k) -> p u k", u=2)
    lg = c.work[:, 3600:3664]
    lt = c.work[0:NT, 3712:3840].rearrange("t (b s) -> t b s", b=2)
    lm = c.work[0:NT, 3840:3842]
    wtok = c.work[:, 3904:3968]
    c2q = c.wb
    names = ("w_in", "b_done", "cc_done", "xg_done", "s_mm", "m_done", "l_done", "a_sub", "a_exp", "r_done",
             "a_done", "at_mm", "at_done", "c2q_mm", "c2q_done", "s1_done")
    m = {n: c.sem(f"{tag}_{n}") for n in names}
    ctx_in = [c.sem(f"{tag}_ctx_in{u}") for u in range(2)]
    ctq_in = [c.sem(f"{tag}_ctq_in{u}") for u in range(2)]
    TB, CB = c.banks[:, 1, :], c.banks[:, 2, :]

    def SB(u):
        return c.banks[:, 3 * u, :]

    def WB(u):
        return c.banks[:, 4 + u, 0:TG]

    def groups(engine, body):
        with engine.Fori(0, NG // 2 - 1) as i:
            for u in range(2):
                body(i * 2 + u, u, i * 16 + 16, i * 16 + (32 if u else 16), True)
        body(NG - 2, 0, NG * 8, NG * 8, True)
        body(NG - 1, 1, NG * 8, 0, False)

    with nc.Block() as block:
        @block.sync
        def _(sp):
            def load(g, u, wait):
                if wait:
                    sp.wait_ge(m["s_mm"], g + 1)
                sp.dma_start(cb[:, u, :], cols(ctxT, g * G)).then_inc(ctx_in[u], 16)
                if wait:
                    sp.wait_ge(m["c2q_mm"], g + 1)
                sp.dma_start(ctq[:, u, :, :].rearrange("q k d -> q (k d)"), cols(ctx_tiles, g * G)).then_inc(
                    ctq_in[u], 16)

            load(0, 0, False)
            load(1, 1, False)
            sp.dma_start(wl[:, :, :].rearrange("p k n -> p (k n)"), A["L2_xattn_W_lT"]).then_inc(m["w_in"], 16)
            for k, n in enumerate(("L2_xattn_w_cq", "L2_xattn_w_q", "L2_xattn_w_c", "L2_xattn_b_l")):
                sp.dma_start(col[:, k:k + 1], A[n].unsqueeze(1)).then_inc(m["w_in"], 16)
            for k, n in enumerate(("L2_xattn_b_cq", "L2_xattn_b_c", "L2_xattn_b_q")):
                sp.dma_start(col[:, 4 + k:5 + k], A[n].partition_broadcast(P)).then_inc(m["w_in"], 16)
            with sp.Fori(1, NG // 2) as i:
                for u in range(2):
                    load(i * 2 + u, u, True)

        @block.tensor
        def _(pe):
            start_at_1(pe, m, "s_mm", "at_mm", "c2q_mm")
            start_at_1(pe, m, "s_mm", "at_mm", "c2q_mm")
            pe.wait_ge(m["w_in"], 128)
            pe.wait_ge(m["b_done"], 2)

            def scores(g, u, loads):
                pe.wait_ge(ctx_in[u], loads)
                pe.wait_ge(m["cc_done"], g + 1)
                pe.wait_ge(m["xg_done"], g + 1)
                pe.wait_ge(m["a_sub"], g + 1)
                pe.wait_ge(m["l_done"], g + 1)
                for k in range(TG):
                    tile = slice(k * P, (k + 1) * P)
                    nc.tensor.matmul(SB(u)[:, tile], cc[:, u, tile], cb[:, u, tile], start=True, stop=False)
                    nc.tensor.matmul(SB(u)[:, tile], ident16, apart, start=False, stop=True)
                for k in range(TG):
                    last = nc.tensor.matmul(WB(u)[:, k:k + 1], xg[:, u, k * P:(k + 1) * P], col[:, 2:3],
                                            start=True, stop=True)
                last.then_inc(m["s_mm"], 1)

            def body(g, u, loads, next_loads, more):
                if more:
                    scores(g + 1, 1 - u, next_loads)
                pe.wait_ge(m["a_done"], g + 3)
                pe.wait_ge(m["at_done"], g + 1)
                for k in range(TG):
                    last = nc.tensor.transpose(TB[:, k * P:(k + 1) * P], a[:, u, k, :], c.ident[:, :])
                last.then_inc(m["at_mm"], 1)
                pe.wait_ge(m["at_done"], g + 2)
                pe.wait_ge(ctq_in[u], loads)
                pe.wait_ge(m["c2q_done"], g + 1)
                for k in range(TG):
                    last = nc.tensor.matmul(CB[:, k * P:(k + 1) * P], ctq[:, u, k, :], at[:, u, k * P:(k + 1) * P],
                                            start=True, stop=True)
                last.then_inc(m["c2q_mm"], 1)

            scores(0, 0, 16)
            groups(pe, body)

        @block.vector
        def _(dve):
            start_at_1(dve, m, "b_done", "l_done", "m_done", "a_sub", "s1_done", "r_done", "a_done")
            start_at_1(dve, m, "l_done", "m_done", "a_sub", "s1_done", "r_done", "a_done")
            dve.wait_ge(m["w_in"], 128)
            nc.vector.tensor_scalar(col[:, 4:5], col[:, 4:5], col[:, 5:6], col[:, 6:7], ALU.add, ALU.add)
            nc.vector.tensor_copy(ident16, c.ident[:, :])
            nc.vector.memset(apart[0:S, S:P], -1e30)
            nc.vector.memset(apart[S:P, 0:S], -1e30)
            nc.vector.memset(apart[0:S, 0:S], 0.0)
            nc.vector.memset(apart[S:P, S:P], 0.0)
            nc.vector.tensor_tensor(col[:, 7:8], col[:, 3:4], c.tanh_g[:, 2:3], ALU.mult).then_inc(m["b_done"], 1)
            dve.wait_ge(m["b_done"], 2)

            def make_cc(g, u):
                dve.wait_ge(m["s_mm"], g + 1)
                nc.vector.tensor_scalar(cc[:, u, :], cols(c.xn, g * G), col[:, 0:1], col[:, 1:2], ALU.mult,
                                        ALU.add).then_inc(m["cc_done"], 1)

            def soften(g, u, ahead):
                s3 = SB(u).rearrange("p (k q) -> p k q", k=TG)
                av, mu, su = a[:, u, :, :], ml[:, u, :], sm[:, u, :]
                dve.wait_ge(m["s_mm"], g + 3)
                nc.vector.tensor_reduce(mu, s3, axis=AX.X, op=ALU.max).then_inc(m["m_done"], 1)
                dve.wait_ge(m["m_done"], g + 3)
                nc.vector.scalar_tensor_tensor(out=lg[:, bass.ds(g * TG, TG)], in0=WB(u), scalar=col[:, 4:5],
                                               in1=mu, op0=ALU.add, op1=ALU.add).then_inc(m["l_done"], 1)
                dve.wait_ge(m["at_mm"], g + 1)
                nc.vector.tensor_tensor(av, s3, mu.unsqueeze(2).broadcast_to([P, TG, P]),
                                        ALU.subtract).then_inc(m["a_sub"], 1)
                if ahead:
                    make_cc(g + 1, 1 - u)
                dve.wait_ge(m["a_exp"], g + 1)
                nc.vector.tensor_reduce(su, av, axis=AX.X, op=ALU.add).then_inc(m["s1_done"], 1)
                dve.wait_ge(m["s1_done"], g + 3)
                nc.vector.reciprocal(su, su).then_inc(m["r_done"], 1)
                dve.wait_ge(m["r_done"], g + 3)
                nc.vector.tensor_tensor(av, av, su.unsqueeze(2).broadcast_to([P, TG, P]), ALU.mult).then_inc(
                    m["a_done"], 1)

            def body(g, u, loads, next_loads, more):
                if more:
                    soften(g + 1, 1 - u, not isinstance(g, int))

            make_cc(0, 0)
            soften(0, 0, True)
            groups(dve, body)

        @block.scalar
        def _(act):
            start_at_1(act, m, "at_done", "c2q_done")

            def copy_x(g, u):
                act.wait_ge(m["s_mm"], g + 1)
                nc.scalar.activation(xg[:, u, :], cols(c.xn, g * G), ACT.Copy).then_inc(m["xg_done"], 1)

            def exps(g, u):
                act.wait_ge(m["a_sub"], g + 3)
                nc.scalar.activation(a[:, u, :, :], a[:, u, :, :], ACT.Exp).then_inc(m["a_exp"], 1)

            def body(g, u, loads, next_loads, more):
                act.wait_ge(m["at_mm"], g + 3)
                act.wait_ge(m["c2q_mm"], g + 1)
                nc.scalar.activation(at[:, u, :], TB, ACT.Copy).then_inc(m["at_done"], 1)
                if more:
                    exps(g + 1, 1 - u)
                if not isinstance(g, int):
                    copy_x(g + 2, u)
                act.wait_ge(m["c2q_mm"], g + 3)
                nc.scalar.activation(cols(c2q, g * G), CB, ACT.Copy).then_inc(m["c2q_done"], 1)

            copy_x(0, 0)
            copy_x(1, 1)
            exps(0, 0)
            groups(act, body)

    step, lt_mm, lt_sub, lt_exp, lt_done, back = (c.sem(tag + n) for n in ("_st", "_ltm", "_lts", "_lte", "_ltd", "_bk"))
    with nc.Block() as block:
        @block.tensor
        def _(pe):
            nc.tensor.transpose(c.banks[0:NT, 3, 0:P], lg, c.ident[:, :]).then_inc(lt_mm, 1)
            pe.wait_ge(lt_done, 1)
            nc.tensor.transpose(c.banks[:, 4, 0:NT], lt.rearrange("t b s -> t (b s)"),
                                c.ident[0:NT, 0:NT]).then_inc(back, 1)

        @block.scalar
        def _(act):
            act.wait_ge(lt_sub, 1)
            nc.scalar.activation(lt, lt, ACT.Exp).then_inc(lt_exp, 1)

        @block.vector
        def _(dve):
            link = chain_on(dve, step)
            dve.wait_ge(lt_mm, 1)
            raw = c.banks[0:NT, 3, 0:P].rearrange("t (b s) -> t b s", b=2)
            link(nc.vector.tensor_reduce(lm, raw, axis=AX.X, op=ALU.max))
            nc.vector.tensor_tensor(lt, raw, lm.unsqueeze(2).broadcast_to([NT, 2, S]), ALU.subtract).then_inc(lt_sub, 1)
            dve.wait_ge(lt_exp, 1)
            link(nc.vector.tensor_reduce(lm, lt, axis=AX.X, op=ALU.add))
            link(nc.vector.reciprocal(lm, lm))
            nc.vector.tensor_tensor(lt, lt, lm.unsqueeze(2).broadcast_to([NT, 2, S]), ALU.mult).then_inc(lt_done, 1)
            dve.wait_ge(back, 1)
            link(nc.vector.tensor_copy(wtok, c.banks[:, 4, 0:NT]))

    wfix = c.work[:, 4000:4008].rearrange("p (u k) -> p u k", u=2)
    prod = c.work[:, 4096:4608]
    x3 = c.work[:, 4608:5632].rearrange("p (u n) -> p u n", u=2)
    x4 = c.work[:, 5632:6656].rearrange("p (u n) -> p u n", u=2)
    add = c.work[:, 6656:7168]
    qc = c.work[:, 7168:7168 + BG]
    m = {n: c.sem(f"{tag}b_{n}") for n in (
        "wfix",
        "bc_mm",
        "prod",
        "qc", "x3", "x4",
        "z_mm",
        "add",
        "x")}

    def groups(engine, body):
        with engine.Fori(0, NG // 2 - 1) as i:
            for u in range(2):
                body(i * 2 + u, u, True)
        body(NG - 2, 0, True)
        body(NG - 1, 1, False)

    with nc.Block() as block:
        @block.gpsimd
        def _(pool):
            with pool.Fori(0, NG // 2) as i:
                for u in range(2):
                    pool.wait_ge(m["bc_mm"], i * 2 + (u + 1))
                    nc.gpsimd.tensor_copy(wfix[:, u, :], wtok[:, bass.ds(i * (2 * TG) + u * TG, TG)]).then_inc(
                        m["wfix"], 1)

        @block.tensor
        def _(pe):
            start_at_1(pe, m, "bc_mm", "z_mm")
            start_at_1(pe, m, "bc_mm", "z_mm")

            def spread(g, u):
                pe.wait_ge(m["wfix"], g + 1)
                pe.wait_ge(m["prod"], g + 1)
                for k in range(TG):
                    last = nc.tensor.matmul(c.banks[:, 5, k * P:(k + 1) * P], wfix[:, u, k:k + 1].broadcast_to([P, P]),
                                            c.ident[:, :], start=True, stop=True)
                last.then_inc(m["bc_mm"], 1)

            def body(g, u, more):
                z = c.banks[:, 6 + u, :]
                pe.wait_ge(m["add"], g + 1)
                nc.tensor.matmul(z, wl[:, 0, :], cols(c.xn, g * G), start=True, stop=False)
                nc.tensor.matmul(z, wl[:, 1, :], cols(c2q, g * G), start=False, stop=False)
                pe.wait_ge(m["x3"], g + 1)
                nc.tensor.matmul(z, wl[:, 2, :], x3[:, u, :], start=False, stop=False)
                pe.wait_ge(m["x4"], g + 1)
                nc.tensor.matmul(z, wl[:, 3, :], x4[:, u, :], start=False, stop=True).then_inc(m["z_mm"], 1)
                if not isinstance(g, int):
                    spread(g + 2, u)

            spread(0, 0)
            spread(1, 1)
            groups(pe, body)

        @block.vector
        def _(dve):
            start_at_1(dve, m, "prod", "x")

            def multiply(g, u):
                xn = cols(c.xn, g * G)
                seq = "p (b s) -> p b s"
                dve.wait_ge(m["z_mm"], g + 1)
                nc.vector.tensor_tensor(x3[:, u, :], xn, cols(c2q, g * G), ALU.mult).then_inc(m["x3"], 1)
                dve.wait_ge(m["bc_mm"], g + 3)
                nc.vector.tensor_tensor(prod, xn, c.banks[:, 5, :], ALU.mult).then_inc(m["prod"], 1)
                dve.wait_ge(m["prod"], g + 2)
                nc.vector.tensor_reduce(qc, prod.rearrange(seq, s=S), axis=AX.X, op=ALU.add).then_inc(m["qc"], 1)
                dve.wait_ge(m["qc"], g + 1)
                nc.vector.tensor_tensor(x4[:, u, :].rearrange(seq, s=S), xn.rearrange(seq, s=S),
                                        qc.unsqueeze(2).broadcast_to([P, BG, S]), ALU.mult).then_inc(m["x4"], 1)

            def body(g, u, more):
                if more:
                    multiply(g + 1, 1 - u)
                dve.wait_ge(m["add"], g + 3)
                nc.vector.tensor_tensor(cols(c.x, g * G), cols(c.x, g * G), add, ALU.add).then_inc(m["x"], 1)

            multiply(0, 0)
            groups(dve, body)

        @block.scalar
        def _(act):
            start_at_1(act, m, "add")
            act.sem_inc(m["add"], 1)
            with act.Fori(0, NG // 2) as i:
                for u in range(2):
                    act.wait_ge(m["z_mm"], i * 2 + (u + 3))
                    act.wait_ge(m["x"], i * 2 + (u + 1))
                    nc.scalar.activation(add, c.banks[:, 6 + u, :], ACT.Identity, bias=col[:, 7:8],
                                         scale=c.tanh_g[:, 2:3]).then_inc(m["add"], 1)


def small_ffn(c, tag, A):
    nc = c.nc
    F = 32
    w1 = c.wa[:, 0:256]
    w2 = c.wa[:, 256:512].rearrange("p (j n) -> p j n", j=2)
    b1, b2 = c.wa[:, 512:514], c.wa[0:E, 640:768]
    spread = c.wa[0:E, 1024:1152].bitcast(BF16).rearrange("e (j n) -> e j n", j=2)
    chosen = c.work[:, 0:64].rearrange("p (u k e) -> p u k e", u=2, k=TG)
    mt = c.work[0:E, G:3 * G].rearrange("e (u n) -> e u n", u=2)
    mt16 = c.work[0:E, 3 * G:4 * G].bitcast(BF16).rearrange("e (u n) -> e u n", u=2)
    hg = c.work[:, 4 * G:8 * G].rearrange("p (u j n) -> p u j n", u=2, j=2)
    hm = c.work[:, 8 * G:10 * G].rearrange("p (j n) -> p j n", j=2)
    got = c.sem(f"{tag}_weights_in")
    m = {n: c.sem(f"{tag}_{n}") for n in (
        "spread", "chosen",
        "mt_mm",
        "mt",
        "mt16", "h_mm",
        "hg",
        "wide_mm",
        "hm",
        "y_mm",
        "x")}

    def groups(engine, body):
        with engine.Fori(0, NG // 2 - 1) as i:
            for u in range(2):
                body(i * 2 + u, u, True)
        body(NG - 2, 0, True)
        body(NG - 1, 1, False)

    with nc.Block() as block:
        @block.sync
        def _(sp):
            sp.dma_start(w1, A["L3_ffn_W1T"]).then_inc(got, 16)
            sp.dma_start(c.wa[:, 256:512], A["L3_ffn_W2T"]).then_inc(got, 16)
            sp.dma_start(b1, A["L3_ffn_b1T"]).then_inc(got, 16)
            sp.dma_start(b2, A["L3_ffn_b2"]).then_inc(got, 16)

        @block.gpsimd
        def _(pool):
            nc.gpsimd.memset(spread, 1.0).then_inc(m["spread"], 1)
            pool.wait_ge(m["spread"], 1)
            for n, (base, mult, step) in enumerate(((0, -F, 1), (F - 1, F, -1))):
                nc.gpsimd.affine_select(out=spread, in_=spread, compare_op=ALU.is_ge, fill=0.0, base=base,
                                        pattern=[[step * P, 2], [step, P]], channel_multiplier=mult).then_inc(
                    m["spread"], 1)
                pool.wait_ge(m["spread"], n + 2)

            def body(g, u, more):
                pool.wait_ge(m["mt_mm"], g + 1)
                flat = c.gates[:, :, :].rearrange("p t e -> p (t e)")[:, bass.ds(g * (TG * E), TG * E)]
                nc.gpsimd.tensor_copy(chosen[:, u, :, :].rearrange("p k e -> p (k e)"), flat).then_inc(m["chosen"], 1)

            with pool.Fori(0, NG // 2) as i:
                for u in range(2):
                    body(i * 2 + u, u, True)

        @block.tensor
        def _(pe):
            start_at_1(pe, m, "mt_mm", "y_mm")
            start_at_1(pe, m, "mt_mm", "y_mm")
            pe.wait_ge(got, 64)
            pe.wait_ge(m["spread"], 3)

            def begin(g, u):
                pe.wait_ge(m["chosen"], g + 1)
                pe.wait_ge(m["mt"], g + 1)
                for k in range(TG):
                    last = nc.tensor.matmul(c.banks[0:E, 4, k * P:(k + 1) * P], chosen[:, u, k, :], c.ident[:, :],
                                            start=True, stop=True)
                last.then_inc(m["mt_mm"], 1)
                for j in range(2):
                    pe.wait_ge(m["hg"], g * 2 + (j + 1))
                    nc.tensor.matmul(c.banks[:, j, :], w1[:, j * P:(j + 1) * P], cols(c.xn, g * G),
                                     start=True, stop=True).then_inc(m["h_mm"], 1)

            def body(g, u, more):
                pe.wait_ge(m["mt16"], g + 1)
                for j in range(2):
                    pe.wait_ge(m["hm"], g * 2 + (j + 1))
                    nc.tensor.matmul(c.banks[:, 2 + j, :], spread[:, j, :], mt16[:, u, :],
                                     start=True, stop=True).then_inc(m["wide_mm"], 1)
                if more:
                    begin(g + 1, 1 - u)
                pe.wait_ge(m["x"], g + 1)
                pe.wait_ge(m["hm"], g * 2 + 4)
                for j in range(2):
                    nc.tensor.matmul(c.banks[:, 5, :], w2[:, j, :], hm[:, j, :], start=(j == 0), stop=False)
                nc.tensor.matmul(c.banks[:, 5, :], b2, mt[:, u, :], start=False, stop=True).then_inc(m["y_mm"], 1)

            begin(0, 0)
            groups(pe, body)

        @block.scalar
        def _(act):
            start_at_1(act, m, "mt", "hg")
            act.sem_inc(m["hg"], 1)
            act.wait_ge(got, 64)

            def begin(g, u):
                act.wait_ge(m["mt_mm"], g + 3)
                act.wait_ge(m["y_mm"], g + 1)
                nc.scalar.activation(mt[:, u, :], c.banks[0:E, 4, :], ACT.Copy).then_inc(m["mt"], 1)
                for j in range(2):
                    act.wait_ge(m["h_mm"], g * 2 + (j + 1))
                    nc.scalar.activation(hg[:, u, j, :], c.banks[:, j, :], ACT.Gelu, bias=b1[:, j:j + 1]).then_inc(
                        m["hg"], 1)

            def body(g, u, more):
                if more:
                    begin(g + 1, 1 - u)

            begin(0, 0)
            groups(act, body)

        @block.vector
        def _(dve):
            start_at_1(dve, m, "hm", "x")
            dve.sem_inc(m["hm"], 1)

            def round_masks(g, u):
                dve.wait_ge(m["mt"], g + 2)
                nc.vector.tensor_copy(mt16[:, u, :], mt[:, u, :]).then_inc(m["mt16"], 1)

            def body(g, u, more):
                for j in range(2):
                    dve.wait_ge(m["hg"], g * 2 + (j + 3))
                    dve.wait_ge(m["wide_mm"], g * 2 + (j + 1))
                    dve.wait_ge(m["y_mm"], g + 2)
                    nc.vector.tensor_tensor(hm[:, j, :], hg[:, u, j, :], c.banks[:, 2 + j, :], ALU.mult).then_inc(
                        m["hm"], 1)
                if more:
                    round_masks(g + 1, 1 - u)
                dve.wait_ge(m["y_mm"], g + 3)
                xg = cols(c.x, g * G)
                nc.vector.scalar_tensor_tensor(out=xg, in0=c.banks[:, 5, :], scalar=c.tanh_g[:, 7:8], in1=xg,
                                               op0=ALU.mult, op1=ALU.add).then_inc(m["x"], 1)

            round_masks(0, 0)
            groups(dve, body)


def store(c, out):
    nc = c.nc
    stored = c.sem("stored")
    with nc.Block() as block:
        @block.sync
        def _(sp):
            for k in range(4):
                sp.dma_start(out[:, k * 2048:(k + 1) * 2048], c.x[:, k * 2048:(k + 1) * 2048]).then_inc(stored, 16)
            sp.wait_ge(stored, 64)


def begin_loads(c, tag, loads):
    nc = c.nc
    got = c.sem(tag + "_got")
    with nc.Block() as block:
        @block.sync
        def _(sp):
            for dst, src in loads:
                sp.dma_start(dst, src).then_inc(got, 16)
    return got, 16 * len(loads)


def small_loads(c, tag, loads):
    nc = c.nc
    got = c.sem(tag + "_got")
    with nc.Block() as block:
        @block.sync
        def _(sp):
            for dst, src in loads:
                sp.dma_start(dst, src).then_inc(got, 16)
            sp.wait_ge(got, 16 * len(loads))


def zero_rows(c):
    nc = c.nc
    zero = c.wa[:, 4096:8192]
    cleared = c.sem("zero_made")
    rows = c.rows_in.rearrange("(p r) d -> p (r d)", p=P)
    n = rows.shape[1]
    with nc.Block() as block:
        @block.gpsimd
        def _(pool):
            nc.gpsimd.memset(zero, 0.0).then_inc(cleared, 1)

        @block.sync
        def _(sp):
            sp.wait_ge(cleared, 1)
            for at in range(0, n, 4096):
                w = min(4096, n - at)
                sp.dma_start(rows[:, at:at + w], zero[:, 0:w]).then_inc(c.zeroed, 16)


ZEROING = -(-(L0_GROUPS + 1) * G // 4096)


def program(nc, A, out):
    with ExitStack() as ctx:
        c = Chip(nc, ctx)
        setup(c, A)
        c.router_w = c.sb("router_w", [P, E])
        c.bias8 = c.sb("bias8", [P, E])
        c.rank = c.sb("rank", [P, NT, E])
        c.t1, c.t2, c.t3, c.t4, c.t2x = (c.sb(f"route{k}", [P, NT, E]) for k in range(5))
        c.m_b = c.sb("chosen", [P, NT, E], BF16)
        c.s1, c.s2, c.s3 = (c.sb(f"per_token{k}", [P, NT]) for k in range(3))
        c.iota_i = c.sb("iota_i", [P, S], I32)

        c.slots = c.sb("slots", [P, NT, 2])
        c.token_gates = c.sb("token_gates", [P, NT, 2])
        c.index = c.sb("index", [P, 2, TG * 2], U32)
        c.per_expert = c.sb("per_expert", [P, 3, E])
        c.weight_rows = c.sb("weight_rows", [P, L2_GROUPS], U32)
        c.rows_in = nc.dram_tensor("rows_in", ((L0_GROUPS + 1) * G, P), F32, kind="Internal").ap()
        c.rows_out = nc.dram_tensor("rows_out", (L0_GROUPS * G, P), F32, kind="Internal").ap()
        c.zeroed = nc.alloc_semaphore(name="zeroed")


        c.attn_w = c.sb("attn_w", [P, 4, P])
        c.attn_b = c.sb("attn_b", [P, 4])
        c.mrow = c.wa[:, 0:4096].bitcast(BF16)
        c.mrow_fix = c.sb("mrow_fix", [P, 2, G], BF16)

        def attend(layer, scale, mask, kind, biases, block_diagonal):
            t = f"a{layer}"
            layer_norm(c, f"n{2 * layer}", c.x, c.xn,
                       meanwhile=prepare_attention(c, t, A, layer, block_diagonal, biases, mask, kind))
            col = [c.attn_b[:, k:k + 1] for k in range(4)]
            attention(c, t, A["ctxT"], scale, c.tanh_g[:, layer:layer + 1], *col)

        zero_rows(c)
        attend(0, P ** -0.5, A["mask_if1"], "zero_is_off", (None, None, None, "L0_xattn_bo"), True)
        small_loads(c, "l0f_affine", [(c.cols16[:, 0:1], A["L0_ffn_ln_gamma"].unsqueeze(1)),
                                      (c.cols16[:, 1:2], A["L0_ffn_ln_beta"].unsqueeze(1))])
        loaded = begin_loads(c, "l0w", [(c.wa[:, 0:8192], A["L0_ffn_w12T"]), (c.wa[:, 8192:12288], A["L0_ffn_w3T"])])
        layer_norm(c, "n1", c.x, c.xn, (c.cols16[:, 0:1], c.cols16[:, 1:2]))
        router(c, "l0", A["L0_ffn_router_wT"])
        route_top2_capacity(c, "l0")
        w12 = c.wa[:, 0:8192].rearrange("p (e f) -> p e f", e=E)
        w3 = c.wa[:, 8192:12288].rearrange("p (e j n) -> p e j n", e=E, j=4)
        dispatch(c, "l0d", 2, E * L0_CAP - 1, zeroed=True)

        def l0_groups(engine, body):
            per = L0_GROUPS // E
            for e in range(E):
                body(e * per, e * per % 2, e, e - 1 if e else None)
                with engine.Fori(0, (per - 1) // 2) as q:
                    for k in (1, 2):
                        body(q * 2 + (e * per + k), (e * per + k) % 2, e, e)
            return L0_GROUPS - 1, (L0_GROUPS - 1) % 2, E - 1

        grouped_ffn(c, "l0f", 4, l0_groups,
                    lambda e: (lambda j: w12[:, e, j * P:(j + 1) * P], lambda j: w12[:, e, (4 + j) * P:(5 + j) * P],
                               lambda j: w3[:, e, j, :]),
                    loaded=loaded, meanwhile=context_sums(c, "l1s", A["ctxT"]))
        combine(c, "l0c", 2, E * L0_CAP - 1)
        c.recycle_semaphores()
        layer_norm(c, "n2", c.x, c.xn)
        windowed_product(c, "l1x")
        c.recycle_semaphores()
        loaded = begin_loads(c, "l1w", [(c.wb[:, 0:4096], A["L1_ffn_w1T"]), (c.wb[:, 4096:8192], A["L1_ffn_w2T"]),
                                        (c.cols16[:, 2:34], A["L1_ffn_b1T"]), (c.cols16[:, 34:42], A["L1_ffn_b2T"])])
        layer_norm(c, "n3", c.x, c.xn)
        router(c, "l1", A["L1_ffn_router_wT"])
        route_expert_choice(c, "l1", 1, False, S * 2 // E + 1, False)
        w1 = c.wb[:, 0:4096].rearrange("p (e f) -> p e f", e=E)
        w2 = c.wb[:, 4096:8192].rearrange("p (e j n) -> p e j n", e=E, j=4)
        b1 = c.cols16[:, 2:34].rearrange("p (e j) -> p e j", e=E)
        chosen_ffn(c, "l1f", c.t1[:, :, :], c.t3[:, 0:3, :].rearrange("p t e -> p (t e)")[:, 0:L1_KEEP],
                   (w1, w2, b1, c.cols16[:, 34:42]), loaded)
        layer_norm(c, "n4", c.x, c.xn)
        two_way_attention(c, "bi", A, A["ctxT"], A["ctx_tiles"])
        c.recycle_semaphores()
        layer_norm(c, "n5", c.x, c.xn)
        router(c, "l2", A["L2_ffn_routerT"])
        route_argmax(c, "l2")
        small_loads(c, "l2s", [(c.wa[:, 0:768], A["L2_ffn_shared"])])
        sh = c.wa[:, 0:768]
        dispatch(c, "l2d", 1, L2_GROUPS * G - 1,
                 shared=(sh[:, 0:256], sh[:, 256:512], sh[:, 512:768].rearrange("p (j n) -> p j n", j=2),
                         c.tanh_g[:, 6:7]))
        arrived = [c.sem(f"l2w_arrived{v}") for v in range(L2_BUFFERS)]

        def l2_fetch(n):
            v = n % L2_BUFFERS
            nc.gpsimd.indirect_dma_start(c.wa[:, 1024 + 768 * v:1024 + 768 * v + 768], None, A["L2_ffn_rows"],
                                         bass.IndirectOffsetOnAxis(c.weight_rows[:, n:n + 1], 0),
                                         bounds_check=E * P - 1, oob_is_err=False).then_inc(arrived[v], 16)

        def l2_groups(engine, body):
            n = L2_BUFFERS
            for v in range(n):
                body(v, v % 2, (0, v), (0, v - 1) if v else None)
            with engine.Fori(1, L2_GROUPS // n) as i:
                for v in range(n):
                    body(i * n + v, v % 2, (i, v), (i, (v - 1) % n))
            return L2_GROUPS - 1, 1, (L2_GROUPS // n - 1, n - 1)

        def l2_weights(key):
            w = c.wa[:, 1024 + 768 * key[1]:1024 + 768 * key[1] + 768]
            return (lambda j: w[:, j * P:(j + 1) * P], lambda j: w[:, (2 + j) * P:(3 + j) * P],
                    lambda j: w[:, (4 + j) * P:(5 + j) * P])

        grouped_ffn(c, "l2f", 2, l2_groups, l2_weights, fetch=(L2_GROUPS, l2_fetch, arrived))
        combine(c, "l2c", 1, L2_GROUPS * G - 1, gate=c.tanh_g[:, 6:7])
        c.recycle_semaphores()
        attend(3, HD ** -0.5, A["mask_fk0"], "one_is_off",
               ("L3_xattn_bq", "L3_xattn_bk", "L3_xattn_bv", "L3_xattn_bo"), False)
        layer_norm(c, "n7", c.x, c.xn)
        router(c, "l3", A["L3_ffn_w_gate_w"], A["L3_ffn_w_gate_b"])
        route_expert_choice(c, "l3", 3, True, S // 2, True)
        small_ffn(c, "l3f", A)
        store(c, out)


def kernel(**inputs):
    import numpy as _np
    import concourse.bacc as _bacc
    from concourse import mybir as _mybir
    from concourse.bass_utils import run_bass_kernel_spmd as _run

    v = {k: _np.asarray(a) for k, a in inputs.items()}

    def tiles_last(w):
        e, o, f = w.shape
        return w.reshape(e, o, f // 128, 128).transpose(3, 0, 2, 1).reshape(128, -1)

    def down_rows(w):
        e, o, f = w.shape
        return w.reshape(e, o, f // 128, 128).transpose(0, 3, 2, 1).reshape(e, 128, -1)

    def tiles_first(w):
        e, f, o = w.shape
        return w.reshape(e, f // 128, 128, o).transpose(2, 0, 1, 3).reshape(128, -1)

    lay = {
        "xT": v["x"].reshape(8192, 128).T,
        "ctxT": v["ctx_1024"].reshape(8192, 128).T,
        "ctx_tiles": v["ctx_1024"].reshape(64, 128, 128).transpose(1, 0, 2).reshape(128, -1),
        "L2_xattn_W_lT": v["L2_xattn_W_l"].reshape(128, 4, 128).transpose(2, 1, 0).reshape(128, -1),
        "L2_xattn_b_cq": v["L2_xattn_b_cq"].reshape(1),
        "L2_xattn_b_c": v["L2_xattn_b_c"].reshape(1),
        "L2_xattn_b_q": v["L2_xattn_b_q"].reshape(1),
        "L3_ffn_W1T": v["L3_ffn_W1"].transpose(1, 0, 2).reshape(128, -1),
        "L3_ffn_W2T": v["L3_ffn_W2"].reshape(2, 128, 128).transpose(1, 0, 2).reshape(128, -1),
        "L3_ffn_b1T": v["L3_ffn_b1"].reshape(2, 128).T,
        "L0_ffn_router_wT": v["L0_ffn_router_w"].T,
        "L0_ffn_w12T": v["L0_ffn_w12"].transpose(2, 0, 1).reshape(128, -1),
        "L0_ffn_w3T": tiles_last(v["L0_ffn_w3"]),
        "L1_ffn_router_wT": v["L1_ffn_router_w"].T,
        "L1_ffn_w1T": v["L1_ffn_w1"].transpose(1, 0, 2).reshape(128, -1),
        "L1_ffn_w2T": tiles_first(v["L1_ffn_w2"]),
        "L1_ffn_b1T": v["L1_ffn_b1"].reshape(8, 4, 128).transpose(2, 0, 1).reshape(128, -1),
        "L1_ffn_b2T": v["L1_ffn_b2"].T,
        "L2_ffn_routerT": v["L2_ffn_router"].T,
        "L2_ffn_rows": _np.concatenate([v["L2_ffn_gate"].transpose(0, 2, 1), v["L2_ffn_up"].transpose(0, 2, 1),
                                        down_rows(v["L2_ffn_down"])], axis=2).reshape(1024, 768),
        "L2_ffn_shared": _np.concatenate([v["L2_ffn_w_gate_s"].T, v["L2_ffn_w_up_s"].T,
                                          down_rows(v["L2_ffn_w_down_s"][None])[0]], axis=1),
    }
    for w in ("Wq", "Wk", "Wv", "Wo"):
        lay[f"L0_xattn_{w}T"] = v[f"L0_xattn_{w}"].T
        lay[f"L3_xattn_{w}T"] = v[f"L3_xattn_{w.lower()}"]
    lay["mask_if1"] = v["mask_Bx1x1xS2_if1"].reshape(128, 64)
    lay["mask_fk0"] = v["mask_Bx1x1xS2_fk0"].reshape(128, 64)
    for name in ("L0_xattn_bo", "L3_xattn_bq", "L3_xattn_bk", "L3_xattn_bv", "L3_xattn_bo",
                 "L2_xattn_w_cq", "L2_xattn_w_q", "L2_xattn_w_c", "L2_xattn_b_l", "L3_ffn_w_gate_w", "L3_ffn_w_gate_b",
                 "L3_ffn_b2", "g_xattn", "g_ffn", "L0_ffn_ln_gamma", "L0_ffn_ln_beta"):
        lay[name] = v[name]

    nc = _bacc.Bacc("TRN2", target_bir_lowering=False, num_devices=1)
    arrays, A = {}, {}
    for name, a in lay.items():
        a = _np.ascontiguousarray(a)
        arrays[f"in_{name}"] = a
        A[name] = nc.dram_tensor(f"in_{name}", a.shape, _mybir.dt.from_np(a.dtype), kind="ExternalInput").ap()
    out = nc.dram_tensor("out_0_dram", (128, 8192), _mybir.dt.float32, kind="ExternalOutput").ap()
    program(nc, A, out)
    r = _run(nc, [arrays], core_ids=[0])
    return _np.ascontiguousarray(r.results[0]["out_0_dram"].T).reshape(128, 64, 128)
```
